# Optimizing a Trainium2 kernel written in Bass

```python
import numpy as np
import jax
import jax.numpy as jnp

def _softmax(x, axis=-1):
    return jax.nn.softmax(x, axis=axis)

def _gelu(x):
    return jax.nn.gelu(x, approximate=True)

def _silu(x):
    return jax.nn.silu(x)

def _sigmoid(x):
    return jax.nn.sigmoid(x)

def _layernorm(x, axis=-1, eps=1e-05):
    m = jnp.mean(x, axis=axis, keepdims=True)
    v = jnp.var(x, axis=axis, keepdims=True)
    return (x - m) / jnp.sqrt(v + eps)

def _scatter_add(tgt, idx, src, axis=0):
    return tgt.at[idx].add(src)

def _segment_sum(src, seg, n):
    return jax.ops.segment_sum(src, seg, n)
kernel_name = 'mk_decoder_postln_d1_seqx_r8_2a3434'

def setup_inputs(seed: int=0):
    np.random.seed(seed)
    _w = jnp.asarray

    def _rec_inputs():
        import jax
        import jax.numpy as jnp
        _rk = jax.random.key(seed)
        x = -0.000125 + 0.9999 * jax.random.normal(jax.random.fold_in(_rk, 1), (4, 256, 256), jnp.float32)
        _lenS = 256 - jax.random.randint(jax.random.fold_in(_rk, 7), (4,), 0, max(1, 256 // 4) + 1, jnp.int32)
        _lenS2 = 512 - jax.random.randint(jax.random.fold_in(_rk, 8), (4,), 0, max(1, 512 // 4) + 1, jnp.int32)
        _ctx_2048P = jax.random.normal(jax.random.fold_in(_rk, 11), (4, 16, 256), jnp.float32)
        _ctx_2048c = jax.random.dirichlet(jax.random.fold_in(_rk, 511), 0.3 * jnp.ones((16,), jnp.float32), (4, 512))
        _ctx_2048t = jnp.einsum('bsk,bkd->bsd', _ctx_2048c, _ctx_2048P)
        _ctx_2048t = _ctx_2048t * jax.lax.rsqrt(jnp.mean(jnp.square(_ctx_2048t)) + 1e-12) * 0.953939
        ctx_2048 = -0.000514642 + 1.00011 * (_ctx_2048t + 0.3 * jax.random.normal(jax.random.fold_in(_rk, 611), (4, 512, 256), jnp.float32))
        _validS = jnp.arange(256)[None, :] < _lenS[:, None]
        _validS2 = jnp.arange(512)[None, :] < _lenS2[:, None]
        _causal = jnp.tril(jnp.ones((256, 256), dtype=bool))
        mask_BxS2_bk0 = jnp.logical_not(jnp.broadcast_to(_validS2[:, :], (4, 512)))
        return (x, ctx_2048, mask_BxS2_bk0)
    x, ctx_2048, mask_BxS2_bk0 = _rec_inputs()

    def _L0_attn_setup():
        import jax, jax.numpy as jnp
        import numpy as np
        H = 16
        DK = 128
        DV = 128
        M = 64
        EPS = 1e-05
        CLAMP = 32.0
        ROPE_BASE = 10000.0

        def _rope(x, cos, sin):
            x1, x2 = jnp.split(x, 2, axis=-1)
            return jnp.concatenate([x1 * cos - x2 * sin, x2 * cos + x1 * sin], axis=-1)
        key = jax.random.key(seed)
        ks = jax.random.split(key, 9)
        B, T, D = (1, 256, 256)
        sc = 0.02
        return {'hidden_states': jax.random.normal(ks[0], (B, T, D), jnp.float32), 'Wq': jax.random.normal(ks[1], (H * DK, D), jnp.float32) * sc, 'Wk': jax.random.normal(ks[2], (H * DK, D), jnp.float32) * sc, 'Wv': jax.random.normal(ks[3], (H * DV, D), jnp.float32) * sc, 'Wg': jax.random.normal(ks[4], (H * DV, D), jnp.float32) * sc, 'Wo': jax.random.normal(ks[5], (D, H * DV), jnp.float32) * sc, 'Ws1': jax.random.normal(ks[6], (16, D), jnp.float32) * sc, 'Ws2': jax.random.normal(ks[7], (H * M, 16), jnp.float32) * sc, 'bs2': jnp.zeros((H * M,), jnp.float32), 'g_norm_weight': jnp.ones((DV,), jnp.float32)}
    _L0_attn_all = _L0_attn_setup()
    _L0_attn_in = {k: v for k, v in _L0_attn_all.items() if k in ('Wq', 'Wk', 'Wv', 'Wg', 'Wo', 'Ws1', 'Ws2', 'bs2', 'g_norm_weight')}
    del _L0_attn_all

    def _L0_xattn_setup():
        import jax, jax.numpy as jnp
        import numpy as np
        key = jax.random.key(seed)
        k1, k2, k3 = jax.random.split(key, 3)
        B, S, D, M = (8, 256, 256, 128)
        hidden_states = jax.random.normal(k1, (B, S, D), dtype=jnp.float32)
        memory_tokens = jax.random.normal(k2, (B, M, D), dtype=jnp.float32)
        memory_mask = jax.random.randint(k3, (B, M), 0, 2).astype(jnp.bool_)
        return {'hidden_states': hidden_states, 'memory_tokens': memory_tokens, 'memory_mask': memory_mask}
    _L0_xattn_all = _L0_xattn_setup()
    _L0_xattn_in = {k: v for k, v in _L0_xattn_all.items() if k in ()}
    del _L0_xattn_all

    def _L0_ffn_setup():
        import jax, jax.numpy as jnp
        import numpy as np
        B, S, D, DFF = (4, 512, 256, 1024)
        CAPACITY_FACTOR = 0.5
        K = int(CAPACITY_FACTOR * S)
        key = jax.random.key(seed)
        ks = jax.random.split(key, 5)
        hidden_states = jax.random.normal(ks[0], (B, S, D), dtype=jnp.float32)
        router_weight = jax.random.normal(ks[1], (D,), dtype=jnp.float32) * 0.02
        router_bias = jnp.zeros((1,), dtype=jnp.float32)
        w1 = jax.random.normal(ks[2], (D, DFF), dtype=jnp.float32) * (1.0 / np.sqrt(D))
        b1 = jnp.zeros((DFF,), dtype=jnp.float32)
        w2 = jax.random.normal(ks[3], (DFF, D), dtype=jnp.float32) * (1.0 / np.sqrt(DFF))
        b2 = jnp.zeros((D,), dtype=jnp.float32)
        return {'hidden_states': hidden_states, 'router_weight': router_weight, 'router_bias': router_bias, 'w1': w1, 'b1': b1, 'w2': w2, 'b2': b2}
    _L0_ffn_all = _L0_ffn_setup()
    _L0_ffn_in = {k: v for k, v in _L0_ffn_all.items() if k in ('router_weight', 'router_bias', 'w1', 'b1', 'w2', 'b2')}
    del _L0_ffn_all
    return {'x': x, 'ctx_2048': ctx_2048, 'mask_BxS2_bk0': mask_BxS2_bk0, 'L0_attn_Wq': _L0_attn_in['Wq'], 'L0_attn_Wk': _L0_attn_in['Wk'], 'L0_attn_Wv': _L0_attn_in['Wv'], 'L0_attn_Wg': _L0_attn_in['Wg'], 'L0_attn_Wo': _L0_attn_in['Wo'], 'L0_attn_Ws1': _L0_attn_in['Ws1'], 'L0_attn_Ws2': _L0_attn_in['Ws2'], 'L0_attn_bs2': _L0_attn_in['bs2'], 'L0_attn_g_norm_weight': _L0_attn_in['g_norm_weight'], 'L0_ffn_router_weight': _L0_ffn_in['router_weight'], 'L0_ffn_router_bias': _L0_ffn_in['router_bias'], 'L0_ffn_w1': _L0_ffn_in['w1'], 'L0_ffn_b1': _L0_ffn_in['b1'], 'L0_ffn_w2': _L0_ffn_in['w2'], 'L0_ffn_b2': _L0_ffn_in['b2']}

def reference(x, ctx_2048, mask_BxS2_bk0, L0_attn_Wq, L0_attn_Wk, L0_attn_Wv, L0_attn_Wg, L0_attn_Wo, L0_attn_Ws1, L0_attn_Ws2, L0_attn_bs2, L0_attn_g_norm_weight, L0_ffn_router_weight, L0_ffn_router_bias, L0_ffn_w1, L0_ffn_b1, L0_ffn_w2, L0_ffn_b2):
    import jax
    import jax.numpy as jnp

    def _L0_attn_ref(hidden_states, Wq, Wk, Wv, Wg, Wo, Ws1, Ws2, bs2, g_norm_weight):
        import jax, jax.numpy as jnp
        import numpy as np
        H = 16
        DK = 128
        DV = 128
        M = 64
        EPS = 1e-05
        CLAMP = 32.0
        ROPE_BASE = 10000.0

        def _rope(x, cos, sin):
            x1, x2 = jnp.split(x, 2, axis=-1)
            return jnp.concatenate([x1 * cos - x2 * sin, x2 * cos + x1 * sin], axis=-1)
        B, T, D = hidden_states.shape
        hs = hidden_states
        q = (hs @ Wq.T).reshape(B, T, H, DK)
        k = (hs @ Wk.T).reshape(B, T, H, DK)
        pos = jnp.arange(T, dtype=jnp.float32)
        inv_freq = 1.0 / ROPE_BASE ** (jnp.arange(0, DK, 2, dtype=jnp.float32) / DK)
        ang = pos[:, None] * inv_freq[None, :]
        cos = jnp.cos(ang)[None, :, None, :]
        sin = jnp.sin(ang)[None, :, None, :]
        q = _rope(q, cos, sin).transpose(0, 2, 1, 3)
        k = _rope(k, cos, sin).transpose(0, 2, 1, 3)
        v = (hs @ Wv.T).reshape(B, T, H, DV).transpose(0, 2, 1, 3)
        s = hs @ Ws1.T @ Ws2.T + bs2
        s = jnp.clip(s, -CLAMP, CLAMP).reshape(B, T, H, M).transpose(0, 2, 1, 3)
        z = jax.lax.cumlogsumexp(s, axis=2)
        es = jnp.exp(s)
        enz = jnp.exp(-z)
        scale = DK ** (-0.5)
        mask = jnp.tril(jnp.ones((T, T), dtype=bool))
        A = jnp.einsum('bhtd,bhjd->bhtj', q, k) * scale
        A = jnp.where(mask, A, 0.0)
        ok = enz * jnp.einsum('bhtj,bhjm->bhtm', A, es)
        qv = jax.nn.softmax(ok, axis=-1)
        W2 = jnp.einsum('bhtm,bhjm->bhtj', qv * enz, es)
        W2 = jnp.where(mask, W2, 0.0)
        o = jnp.einsum('bhtj,bhjd->bhtd', W2, v)
        o = o.transpose(0, 2, 1, 3)
        g = (hs @ Wg.T).reshape(B, T, H, DV)
        o_n = o * jax.lax.rsqrt(jnp.mean(o * o, axis=-1, keepdims=True) + EPS) * g_norm_weight
        o_g = o_n * (g * jax.nn.sigmoid(g))
        return o_g.reshape(B, T, H * DV) @ Wo.T

    def _L0_xattn_ref(hidden_states, memory_tokens, memory_mask):
        import jax, jax.numpy as jnp
        import numpy as np
        B, S, D = hidden_states.shape
        scale = 1.0 / jnp.sqrt(jnp.asarray(D, hidden_states.dtype))
        scores = jnp.einsum('bsd,bmd->bsm', hidden_states, memory_tokens) * scale
        neg_inf = jnp.asarray(-1e+30, scores.dtype)
        scores = jnp.where(memory_mask[:, None, :], scores, neg_inf)
        attn = jax.nn.softmax(scores, axis=-1)
        readout = jnp.einsum('bsm,bmd->bsd', attn, memory_tokens)
        valid_b = jnp.any(memory_mask, axis=-1)
        out = jnp.where(valid_b[:, None, None], readout, jnp.zeros_like(readout))
        return out

    def _L0_ffn_ref(hidden_states, router_weight, router_bias, w1, b1, w2, b2):
        import jax, jax.numpy as jnp
        import numpy as np
        B, S, D, DFF = (4, 512, 256, 1024)
        CAPACITY_FACTOR = 0.5
        K = int(CAPACITY_FACTOR * S)
        b, s, d = hidden_states.shape
        scores = jnp.einsum('bsd,d->bs', hidden_states, router_weight) + router_bias[0]
        top_scores, indices = jax.lax.top_k(scores, K)
        weights = jax.nn.sigmoid(top_scores)
        selected = jnp.take_along_axis(hidden_states, indices[:, :, None], axis=1)
        h = jax.nn.gelu(jnp.einsum('bkd,df->bkf', selected, w1) + b1)
        processed = jnp.einsum('bkf,fd->bkd', h, w2) + b2
        weighted = processed * weights[:, :, None]
        flat = hidden_states.reshape(b * s, d)
        flat_idx = (indices + jnp.arange(b)[:, None] * s).reshape(-1)
        out = flat.at[flat_idx].add(weighted.reshape(b * K, d))
        return out.reshape(b, s, d)
    x = _layernorm(x + _L0_attn_ref(x, L0_attn_Wq, L0_attn_Wk, L0_attn_Wv, L0_attn_Wg, L0_attn_Wo, L0_attn_Ws1, L0_attn_Ws2, L0_attn_bs2, L0_attn_g_norm_weight), axis=-1)
    x = _layernorm(x + _L0_xattn_ref(x, ctx_2048, mask_BxS2_bk0), axis=-1)
    x = _layernorm(x + _L0_ffn_ref(x, L0_ffn_router_weight, L0_ffn_router_bias, L0_ffn_w1, L0_ffn_b1, L0_ffn_w2, L0_ffn_b2), axis=-1)
    return x

_drawn_inputs = setup_inputs


def setup_inputs(seed=0):
    import zlib

    import numpy as np

    out = dict(_drawn_inputs(seed))
    spreads = {'L0_attn_bs2': (0.0, 0.8),
     'L0_attn_g_norm_weight': (1.0, 0.57),
     'L0_ffn_b1': (0.0, 0.478),
     'L0_ffn_b2': (0.0, 0.329)}
    factors = {'L0_attn_Wq': 8.0, 'L0_attn_Wk': 8.0, 'L0_attn_Ws1': 8.0, 'L0_attn_Ws2': 8.0}
    for name, (base, spread) in spreads.items():
        noise = np.random.default_rng([zlib.crc32(name.encode()), seed]).standard_normal(out[name].shape)
        drawn = base * np.exp(spread * noise) if base else spread * noise
        out[name] = jnp.asarray(drawn.astype(out[name].dtype))
    for name, factor in factors.items():
        out[name] = (out[name] * factor).astype(out[name].dtype)
    return out
```

```python
import numpy as np
import concourse.bass as bass
from concourse import mybir
from contextlib import ExitStack

F32 = mybir.dt.float32
F32R = mybir.dt.float32r
U8 = mybir.dt.uint8
I32 = mybir.dt.int32
ALU = mybir.AluOpType
ACT = mybir.ActivationFunctionType
AX = mybir.AxisListType.X

B, T, D = 4, 256, 256
H, DK, M, R = 16, 128, 64, 16
S2 = 512
DFF = 1024
P = 128
KT = D // P
TT = T // P
PAIRS = H // 2
UNITS = PAIRS * B
MT = S2 // P
FT = DFF // P
CLAMP = 32.0
EPS = 1e-5
NEG = -1e30

C_COS, C_SIN, C_TRI, C_ID, C_ONES, C_ONECOL, C_HALF, C_END = 0, 256, 512, 640, 768, 896, 897, 905
V_GN, V_B1, V_RW, V_RB, V_B2, V_END = 0, 1, 9, 265, 266, 522
W_QK, W_S, W_END = 1024, KT * 1024, KT * 1024 + 128


def decoder_layer(nc, x_tok, x_feat, w_pairs, wo_pairs, ws1, consts, vectors, ctx_feat, ctx_tok,
                  mask, w1, w2, out):
    ctx = ExitStack()
    with ctx:
        def sb(name, shape, dt=F32):
            return ctx.enter_context(nc.sbuf_tensor(name, shape, dt))

        def sem(name):
            return ctx.enter_context(nc.semaphore(name))

        con = sb("con", [P, C_END])
        vec = sb("vec", [P, V_END])
        cos = con[:, C_COS:C_COS + T]
        sin = con[:, C_SIN:C_SIN + T]
        tri = con[:, C_TRI:C_TRI + P]
        ident = con[:, C_ID:C_ID + P]
        ones = con[:, C_ONES:C_ONES + P]
        acc = sb("acc", [P, B * TT, D])
        xh = sb("xh", [P, KT, B * T], F32R)
        xl = sb("xl", [P, KT, B * T], F32R)
        s1 = sb("s1", [P, B * T], F32R)
        wraw = sb("wraw", [P, W_END])
        wh = sb("wh", [P, KT, 1024], F32R)
        wl = sb("wl", [P, KT, 1024], F32R)
        ws2 = sb("ws2", [P, 2 * M], F32R)
        woraw = sb("woraw", [P, 2, D])
        woh = sb("woh", [P, 2, D], F32R)
        wol = sb("wol", [P, 2, D], F32R)
        gn = sb("gn", [P, 1])
        swq = sb("swq", [P, 2 * T])
        swk = sb("swk", [P, 2 * T])
        qcos = sb("qcos", [P, 2 * T])
        kcos = sb("kcos", [P, 2 * T])
        qsin = sb("qsin", [P, 2 * T])
        ksin = sb("ksin", [P, 2 * T])
        qr = sb("qr", [P, 2 * T])
        kr = sb("kr", [P, 2 * T])
        val = sb("val", [P, 2, TT, 2 * DK])
        th = sb("th", [P, TT, 2 * DK])
        gate = sb("gate", [P, 2, TT, 2 * DK])
        sc = sb("sc", [P, 2 * P])
        es = sb("es", [P, TT, 2 * M])
        esT = sb("esT", [P, 2, T])
        enz = sb("enz", [P, 2 * P])
        at = sb("at", [P, 2, 384])
        wt = sb("wt", [P, 2, 384])
        ok = sb("ok", [P, 2 * P])
        okm = sb("okm", [P, 2 * P])
        ee = sb("ee", [P, 2 * P])
        qe = sb("qe", [P, TT, P])
        qeT = sb("qeT", [P, T])
        mx = sb("mx", [P, 4])
        sume = sb("sume", [P, 4])
        sq = sb("sq", [P, 4, DK])
        ss = sb("ss", [P, 4])
        zs = sb("zs", [P, 4])
        ze = sb("ze", [P, 4])
        rstd = sb("rstd", [P, 4])
        og = sb("og", [P, 4, DK])
        ogh = sb("ogh", [P, 4, P], F32R)
        ogl = sb("ogl", [P, 4, P], F32R)
        ctxf = sb("ctxf", [P, B, KT, S2])
        ctxt = sb("ctxt", [P, B, MT, D])
        mrow = sb("mrow", [1, B, S2 // 4], I32)
        mneg = sb("mneg", [1, B, S2], F32R)
        mval = sb("mval", [1, B])
        valid = sb("valid", [P, B])
        one_r = sb("one_r", [1, P], F32R)
        w1raw = sb("w1raw", [P, KT, DFF])
        w1h, w1l = wh, wl
        w2s = sb("w2s", [P, FT, D])
        halfrb = sb("halfrb", [P, 1])
        bn1 = sb("bn1", [P, TT, 6])
        st1, st2, st3 = (sb(n, [P, 5, TT]) for n in ("st1", "st2", "st3"))
        mv1 = sb("mv1", [P, B, TT])
        ve1 = sb("ve1", [P, B, TT])
        rs1 = sb("rs1", [P, B, TT])
        x1 = sb("x1", [P, TT, D])
        x1T = sb("x1T", [P, TT, KT, P])
        smax = sb("smax", [P, TT])
        nmax = sb("nmax", [P, TT])
        prob = sb("prob", [P, TT, S2])
        psum_ = sb("psum_", [P, TT])
        pinv = sb("pinv", [P, TT])
        pval = sb("pval", [P, TT])
        probT = sb("probT", [P, TT, MT, P])
        x2p = sb("x2p", [P, TT, D])
        bn2 = sb("bn2", [P, TT, 6])
        mv2 = sb("mv2", [P, TT])
        ve2 = sb("ve2", [P, TT])
        rs2 = sb("rs2", [P, TT])
        x2 = sb("x2", [P, TT, D])
        x2h = woh[:, :, :].rearrange("p k (a t) -> p k a t", a=TT)
        x2l = wol[:, :, :].rearrange("p k (a t) -> p k a t", a=TT)
        rprod = sb("rprod", [P, TT, D])
        rz = sb("rz", [P, TT])
        rt = sb("rt", [P, TT])
        rw = sb("rw", [P, TT])
        hT = w1raw[:, :, :].rearrange("p k (f t) -> p (k f) t", t=T)
        yb = sb("yb", [P, TT, D])
        x3 = sb("x3", [P, TT, D])
        bn3 = sb("bn3", [P, TT, 6])
        mv3 = sb("mv3", [P, TT])
        ve3 = sb("ve3", [P, TT])
        rs3 = sb("rs3", [P, TT])
        res = sb("res", [P, TT, D])

        ps = ctx.enter_context(nc.psum_tensor("ps", [P, 8, 512], F32))
        ps_q, ps_k, ps_c = ps[:, 0, :], ps[:, 1, :], ps[:, 1, 0:256]
        ps_vg, ps_o, ps_wo = ps[:, 2:4, :], ps[:, 2, :], ps[:, 3, :]
        ps_aw = ps[:, 4:6, 0:384]
        ps_s, ps_p, ps_qet = ps[:, 4, 0:256], ps[:, 6, 0:256], ps[:, 6, 0:256]
        ps_ogt, ps_est = ps[:, 7, :], ps[:, 7, 0:256]

        ld_con, ld_vec, ld_xf, ld_xt, ld_ws1 = (sem("ld_" + n) for n in ("con", "vec", "xf", "xt", "ws1"))
        ld_w, ld_wo = sem("ld_w"), sem("ld_wo")
        w_hi, w_qk, w_vg, w_s = sem("w_hi"), sem("w_qk"), sem("w_vg"), sem("w_s")
        wv_hi, ws_hi, wo_hi, w_wo = sem("wv_hi"), sem("ws_hi"), sem("wo_hi"), sem("w_wo")
        gn_ok, x_hi, x_ok = sem("gn_ok"), sem("x_hi"), sem("x_ok")
        ws1_hi, ws1_ok, s1_mm, s1_full, s1_ok = (sem(n) for n in ("ws1_hi", "ws1_ok", "s1_mm", "s1_full", "s1_ok"))
        s1_cp = sem("s1_cp")
        pe_q, pe_k, pe_s, pe_vg, pe_est, pe_c, pe_a, pe_p, pe_qet, pe_w2, pe_o, pe_ogt, pe_wo = (
            sem("pe_" + n) for n in ("q", "k", "s", "vg", "est", "c", "a", "p", "qet", "w2", "o", "ogt", "wo"))
        ac_swq, ac_swk, ac_at, ac_ogh, ac_es, ac_exp, ac_val, ac_qet, ac_th, ac_est, ac_wt, ac_sq = (
            sem("ac_" + n) for n in ("swq", "swk", "at", "ogh", "es", "exp", "val", "qet", "th", "est", "wt", "sq"))
        ve_ss, ve_zs, ve_ze, ve_at, ve_og, ve_qcos, ve_kcos, ve_ok, ve_mx, ve_sc, ve_ogl, ve_qsin = (
            sem("ve_" + n) for n in ("ss", "zs", "ze", "at", "og", "qcos", "kcos", "ok", "mx", "sc", "ogl", "qsin"))
        ve_sum, ve_gate, ve_enz, ve_wt, ve_acc = (sem("ve_" + n) for n in ("sum", "gate", "enz", "wt", "acc"))
        po_rstd, po_okm, po_qe, po_ksin, po_qr, po_kr = (
            sem("po_" + n) for n in ("rstd", "okm", "qe", "ksin", "qr", "kr"))
        ld_tail = sem("ld_tail")
        stored = sem("stored")
        w1_hi, w1_ok, mask_ok, mval_ok, pe_valid, valid_ok, one_ok, rb_ok = (
            sem(n) for n in ("w1_hi", "w1_ok", "mask_ok", "mval_ok", "pe_valid", "valid_ok", "one_ok", "rb_ok"))
        t_bn1, t_mv1, t_ve1, t_rs1, t_x1, t_x1T, t_x1Ts = (sem("t_" + n) for n in ("bn1", "mv1", "ve1", "rs1", "x1", "x1T", "x1Ts"))
        t_sc, t_max, t_nmax, t_prob, t_pT, t_pTs0, t_pTs1 = (sem("t_" + n) for n in ("sc", "max", "nmax", "prob", "pT", "pTs0", "pTs1"))
        t_pinv, t_pval, t_r, t_x2p, t_bn2, t_mv2, t_ve2, t_rs2, t_x2 = (
            sem("t_" + n) for n in ("pinv", "pval", "r", "x2p", "bn2", "mv2", "ve2", "rs2", "x2"))
        t_x2T, t_x2h, t_x2l, t_rprod, t_rz, t_rt, t_rw = (sem("t_" + n) for n in ("x2T", "x2h", "x2l", "rprod", "rz", "rt", "rw"))
        t_st1, t_st2, t_st3 = sem("t_st1"), sem("t_st2"), sem("t_st3")
        t_h, t_gelu = sem("t_h"), sem("t_gelu")
        t_y, t_yb, t_x3, t_bn3, t_mv3, t_ve3, t_rs3, t_out = (
            sem("t_" + n) for n in ("y", "yb", "x3", "bn3", "mv3", "ve3", "rs3", "out"))

        ws1_raw = sc[:, 0:256].rearrange("p (k c) -> p k c", k=KT)
        ws1h, ws1l = ogh[:, 0:2, :], ogl[:, 0:2, :]
        xraw = ctxf[:, 0:2, :, :].rearrange("p b k s -> p (b k s)").rearrange("p (k t) -> p k t", k=KT)
        s1_raw = ctxt[:, 0, :, :].rearrange("p m d -> p (m d)")

        def after(eng, semaphore, count):
            if not isinstance(count, int) or count > 0:
                eng.wait_ge(semaphore, count)

        def over_main(eng, step):
            step(0, 0, 0)
            with eng.Fori(0, PAIRS - 1) as i:
                for b in range(1, B):
                    step(4 * i + b, i, b)
                step(4 * i + 4, i + 1, 0)
            for b in range(1, B):
                step(4 * (PAIRS - 1) + b, PAIRS - 1, b)

        def over_tail(eng, enter, both, leave):
            enter(0)
            with eng.Fori(0, B - 1) as b:
                both(b)
            leave(B - 1)

        def is_last(u):
            return isinstance(u, int) and u == UNITS - 1

        def is_first(u):
            return isinstance(u, int) and u == 0

        def has_next_pair(p):
            return not (isinstance(p, int) and p == PAIRS - 1)

        with nc.Block() as block:

            @block.sync
            def _(sp):
                sp.dma_start(xraw, x_feat).then_inc(ld_xf, 16)
                sp.dma_start(wraw[:, :], w_pairs[0]).then_inc(ld_w, 16)
                sp.dma_start(ws1_raw, ws1).then_inc(ld_ws1, 16)
                sp.dma_start(con[:, :], consts).then_inc(ld_con, 16)
                sp.dma_start(vec[:, :], vectors).then_inc(ld_vec, 16)
                sp.dma_start(woraw[:, :, :], wo_pairs[0]).then_inc(ld_wo, 16)
                sp.dma_start(acc[:, :, :], x_tok).then_inc(ld_xt, 16)
                with sp.Fori(1, PAIRS) as i:
                    sp.wait_ge(w_qk, i)
                    sp.wait_ge(w_vg, i)
                    sp.wait_ge(w_s, i)
                    sp.dma_start(wraw[:, :], w_pairs[bass.ds(i, 1)].rearrange("a p c -> (a p) c")).then_inc(ld_w, 16)
                    sp.wait_ge(w_wo, i)
                    sp.dma_start(woraw[:, :, :], wo_pairs[bass.ds(i, 1)].rearrange("a p h d -> (a p) h d")).then_inc(ld_wo, 16)
                sp.wait_ge(x_ok, 1)
                sp.wait_ge(s1_ok, 1)
                sp.dma_start(ctxf[:, :, :, :], ctx_feat).then_inc(ld_tail, 16)
                sp.dma_start(ctxt[:, :, :, :], ctx_tok).then_inc(ld_tail, 16)
                sp.dma_start(mrow[:, :, :], mask).then_inc(ld_tail, 16)
                sp.dma_start(w1raw[:, :, :], w1).then_inc(ld_tail, 16)
                sp.dma_start(w2s[:, :, :], w2).then_inc(ld_tail, 16)
                with sp.Fori(0, B) as b:
                    sp.wait_ge(t_out, b + 1)
                    sp.dma_start(out[:, bass.ds(b, 1), :, :].rearrange("p a t d -> p (a t) d"), res[:, :, :]).then_inc(stored, 16)
                sp.wait_ge(stored, 16 * B)

            @block.tensor
            def _(pe):
                def passes(o, pairs, first=True, last=True):
                    ops = [x for (ah, al, bh, bl) in pairs for x in ((ah, bh), (ah, bl), (al, bh))]
                    for n, (a, b) in enumerate(ops):
                        mm = pe.matmul(o, a, b, start=first and n == 0, stop=last and n == len(ops) - 1)
                    return mm

                def project_qk(n, p, b):
                    after(pe, ve_qcos, n)
                    after(pe, ac_swq, n)
                    if b == 0:
                        pe.wait_ge(w_qk, p + 1)
                    cols = slice(b * T, (b + 1) * T)
                    for m in range(4):
                        if m == 2:
                            after(pe, ve_kcos, n)
                            after(pe, ac_swk, n)
                            after(pe, ve_enz, n)
                        o = (ps_q if m < 2 else ps_k)[:, (m % 2) * T:(m % 2 + 1) * T]
                        f = slice(m * P, (m + 1) * P)
                        mm = passes(o, [(wh[:, k, f], wl[:, k, f], xh[:, k, cols], xl[:, k, cols]) for k in range(KT)])
                        if m == 1:
                            mm.then_inc(pe_q, 1)
                    mm.then_inc(pe_k, 1)

                def project_vg(n, p, b):
                    after(pe, ac_val, n)
                    after(pe, ac_th, n)
                    after(pe, ve_gate, n)
                    after(pe, ve_og, n - 1)
                    after(pe, ac_sq, n - 1)
                    after(pe, ve_acc, n - 2)
                    if b == 0:
                        pe.wait_ge(w_vg, p + 1)
                    for tt in range(TT):
                        t = slice((b * TT + tt) * P, (b * TT + tt + 1) * P)
                        mm = passes(ps_vg[:, tt, :], [(xh[:, k, t], xl[:, k, t], wh[:, k, W_QK - 512:W_QK], wl[:, k, W_QK - 512:W_QK]) for k in range(KT)])
                    mm.then_inc(pe_vg, 1)

                def slots(n, p, b):
                    after(pe, ve_sc, n)
                    if b == 0:
                        pe.wait_ge(w_s, p + 1)
                    for tt in range(TT):
                        t = slice((b * TT + tt) * P, (b * TT + tt + 1) * P)
                        mm = pe.matmul(ps_s[:, tt * P:(tt + 1) * P], s1[:, t], ws2[:, :], start=True, stop=True)
                    mm.then_inc(pe_s, 1)

                def slot_sums(n):
                    pe.wait_ge(ac_es, n + 1)
                    after(pe, ac_ogh, n - 1)
                    after(pe, ve_ogl, n - 1)
                    for tt in range(TT):
                        mm = pe.transpose(ps_est[:, tt * P:(tt + 1) * P], es[:, tt, :], ident)
                    mm.then_inc(pe_est, 1)
                    pe.wait_ge(ve_kcos, n + 1)
                    pe.wait_ge(ac_swk, n + 1)
                    pe.matmul(ps_c[:, 0:P], tri, es[:, 0, :], start=True, stop=True)
                    pe.matmul(ps_c[:, P:2 * P], ones, es[:, 0, :], start=True, stop=False)
                    pe.matmul(ps_c[:, P:2 * P], tri, es[:, 1, :], start=False, stop=True).then_inc(pe_c, 1)

                def scores(u):
                    pe.wait_ge(po_qr, u + 1)
                    pe.wait_ge(po_kr, u + 1)
                    after(pe, ve_wt, 2 * u)
                    for h in range(2):
                        a = h * T
                        pe.matmul(ps_aw[:, h, 0:T], kr[:, a:a + P], qr[:, a:a + T], start=True, stop=True)
                        pe.matmul(ps_aw[:, h, T:T + P], kr[:, a + P:a + T], qr[:, a + P:a + T], start=True, stop=True).then_inc(pe_a, 1)

                def slot_scores(u):
                    pe.wait_ge(ve_at, 2 * u + 2)
                    after(pe, ac_qet, u)
                    for h in range(2):
                        m = slice(h * M, (h + 1) * M)
                        pe.matmul(ps_p[:, h * M:(h + 1) * M], at[:, h, 0:P], es[:, 0, m], start=True, stop=True)
                        pe.matmul(ps_p[:, (2 + h) * M:(3 + h) * M], at[:, h, P:T], es[:, 0, m], start=True, stop=False)
                        mm = pe.matmul(ps_p[:, (2 + h) * M:(3 + h) * M], at[:, h, T:T + P], es[:, 1, m], start=False, stop=True)
                    mm.then_inc(pe_p, 1)

                def turn_probs(u):
                    pe.wait_ge(po_qe, u + 1)
                    for tt in range(TT):
                        mm = pe.transpose(ps_qet[:, tt * P:(tt + 1) * P], qe[:, tt, :], ident)
                    mm.then_inc(pe_qet, 1)

                def token_weights(u, b):
                    pe.wait_ge(ac_qet, u + 1)
                    pe.wait_ge(ac_est, u + 1)
                    if not is_last(u):
                        pe.wait_ge(ve_sc, u + 2)
                    for h in range(2):
                        m = slice(h * M, (h + 1) * M)
                        e = esT[m, b % 2, :]
                        pe.matmul(ps_aw[:, h, 0:T], e[:, 0:P], qeT[m, 0:T], start=True, stop=True)
                        pe.matmul(ps_aw[:, h, T:T + P], e[:, P:T], qeT[m, P:T], start=True, stop=True).then_inc(pe_w2, 1)

                def outputs(u, b):
                    pe.wait_ge(ve_wt, 2 * u + 2)
                    if not is_last(u):
                        pe.wait_ge(ac_val, u + 2)
                        pe.wait_ge(ac_th, u + 2)
                        pe.wait_ge(ve_gate, u + 2)
                    for h in range(2):
                        d = slice(h * DK, (h + 1) * DK)
                        v = val[:, b % 2, :, d]
                        pe.matmul(ps_o[:, h * P:(h + 1) * P], wt[:, h, 0:P], v[:, 0, :], start=True, stop=True)
                        pe.matmul(ps_o[:, (2 + h) * P:(3 + h) * P], wt[:, h, P:T], v[:, 0, :], start=True, stop=False)
                        mm = pe.matmul(ps_o[:, (2 + h) * P:(3 + h) * P], wt[:, h, T:T + P], v[:, 1, :], start=False, stop=True)
                    mm.then_inc(pe_o, 1)

                def turn_outputs(u):
                    pe.wait_ge(ve_og, u + 1)
                    if is_last(u):
                        pe.wait_ge(ac_est, u + 1)
                    else:
                        pe.wait_ge(ac_est, u + 2)
                    for g in range(4):
                        mm = pe.transpose(ps_ogt[:, g * P:(g + 1) * P], og[:, g, :], ident)
                    mm.then_inc(pe_ogt, 1)

                def project_out(u, p, b):
                    pe.wait_ge(ac_ogh, u + 1)
                    pe.wait_ge(ve_ogl, u + 1)
                    if b == 0:
                        pe.wait_ge(w_wo, p + 1)
                    if not is_last(u):
                        if isinstance(u, int) and u == UNITS - 2:
                            pe.wait_ge(ac_val, u + 2)
                            pe.wait_ge(ac_th, u + 2)
                            pe.wait_ge(ve_gate, u + 2)
                        else:
                            pe.wait_ge(ac_val, u + 3)
                            pe.wait_ge(ac_th, u + 3)
                            pe.wait_ge(ve_gate, u + 3)
                    else:
                        pe.wait_ge(ve_acc, u)
                    for tt in range(TT):
                        mm = passes(ps_wo[:, tt * D:(tt + 1) * D], [(ogh[:, 2 * tt + h, :], ogl[:, 2 * tt + h, :], woh[:, h, :], wol[:, h, :]) for h in range(2)])
                    mm.then_inc(pe_wo, 1)

                pe.wait_ge(x_ok, 1)
                pe.wait_ge(ws1_ok, 1)
                for c in range(2):
                    t = slice(c * 512, (c + 1) * 512)
                    passes(ps[:, 6 + c, :], [(ws1h[:, k, :], ws1l[:, k, :], xh[:, k, t], xl[:, k, t]) for k in range(KT)]).then_inc(s1_mm, 1)
                project_qk(0, 0, 0)
                project_vg(0, 0, 0)
                pe.wait_ge(s1_ok, 1)
                slots(0, 0, 0)
                pe.wait_ge(ld_con, 16)
                slot_sums(0)

                def step(u, p, b):
                    nb = (b + 1) % B
                    np_ = p + 1 if b == B - 1 and has_next_pair(p) else p
                    scores(u)
                    if not is_last(u):
                        project_qk(u + 1, np_, nb)
                    slot_scores(u)
                    if not is_first(u):
                        turn_outputs(u - 1)
                    if not is_last(u):
                        slots(u + 1, np_, nb)
                        project_vg(u + 1, np_, nb)
                    turn_probs(u)
                    if not is_last(u):
                        slot_sums(u + 1)
                    token_weights(u, b)
                    if not is_first(u):
                        project_out(u - 1, p - 1 if b == 0 else p, (b - 1) % B)
                    outputs(u, b)

                over_main(pe, step)
                turn_outputs(UNITS - 1)
                project_out(UNITS - 1, PAIRS - 1, B - 1)

                pe.wait_ge(mval_ok, 1)
                pe.wait_ge(ac_wt, 2 * UNITS)
                pe.matmul(ps[:, 4, 0:B], ones[0:1, :], mval[:, :], start=True, stop=True).then_inc(pe_valid, 1)
                pe.wait_ge(mask_ok, 1)
                pe.wait_ge(one_ok, 1)

                def turn_x1(b):
                    pe.wait_ge(t_x1, b + 1)
                    after(pe, t_gelu, 8 * (b - 1))
                    for g in range(4):
                        mm = pe.transpose(ps[:, 0, g * P:(g + 1) * P], x1[:, g // 2, (g % 2) * P:(g % 2 + 1) * P], ident)
                    mm.then_inc(t_x1T, 1)

                def memory_scores(b):
                    pe.wait_ge(t_x1Ts, b + 1)
                    after(pe, t_yb, b - 1)
                    for tt in range(TT):
                        pe.matmul(ps[:, 1 + tt, :], one_r[:, :], mneg[:, bass.ds(b, 1), :].rearrange("p a s -> p (a s)"), start=True, stop=False)
                        for k in range(KT):
                            mm = pe.matmul(ps[:, 1 + tt, :], x1T[:, tt, k, :], ctxf[:, bass.ds(b, 1), k, :].rearrange("p a s -> p (a s)"),
                                           start=False, stop=(k == KT - 1))
                    mm.then_inc(t_sc, 1)

                def turn_probs_tail(b):
                    pe.wait_ge(t_prob, b + 1)
                    for tt in range(TT):
                        for m in range(MT):
                            mm = pe.transpose(ps[:, 3 + tt, m * P:(m + 1) * P], prob[:, tt, m * P:(m + 1) * P], ident)
                    mm.then_inc(t_pT, 1)

                def readout(b):
                    pe.wait_ge(t_pTs0, b + 1)
                    pe.wait_ge(t_pTs1, b + 1)
                    for tt in range(TT):
                        for m in range(MT):
                            mm = pe.matmul(ps[:, 5, tt * D:(tt + 1) * D], probT[:, tt, m, :],
                                           ctxt[:, bass.ds(b, 1), m, :].rearrange("p a d -> p (a d)"), start=(m == 0), stop=(m == MT - 1))
                    mm.then_inc(t_r, 1)

                def turn_x2(b):
                    pe.wait_ge(t_x2, b + 1)
                    for k in range(KT):
                        for tt in range(TT):
                            mm = pe.transpose(ps[:, 6, (k * TT + tt) * P:(k * TT + tt + 1) * P], x2[:, tt, k * P:(k + 1) * P], ident)
                    mm.then_inc(t_x2T, 1)

                def hidden(b, fs):
                    for f in fs:
                        if f == 0:
                            pe.wait_ge(t_x2l, b + 1)
                            after(pe, t_gelu, 8 * b)
                        if f >= 2:
                            pe.wait_ge(t_gelu, 8 * b + (f - 1))
                        c = slice(f * P, (f + 1) * P)
                        passes(ps[:, 7 if f % 2 == 0 else 0, 0:T], [(w1h[:, k, c], w1l[:, k, c], x2h[:, k, :, :].rearrange("p a t -> p (a t)"),
                               x2l[:, k, :, :].rearrange("p a t -> p (a t)")) for k in range(KT)]).then_inc(t_h, 1)

                def down(b, tt, mem):
                    if tt == 0:
                        pe.wait_ge(t_gelu, 8 * b + 8)
                        pe.wait_ge(t_prob, mem)
                    for f in range(FT):
                        mm = pe.matmul(ps[:, 1 + tt, 0:D], hT[:, f, tt * P:(tt + 1) * P], w2s[:, f, :], start=(f == 0), stop=(f == FT - 1))
                    if tt == TT - 1:
                        mm.then_inc(t_y, 1)

                def enter(b):
                    turn_x1(b)
                    memory_scores(b)
                    turn_probs_tail(b)
                    readout(b)
                    turn_x2(b)
                    pe.wait_ge(w1_ok, 1)

                def both(b):
                    turn_x1(b + 1)
                    hidden(b, range(1))
                    pe.wait_ge(t_x1Ts, b + 2)
                    hidden(b, range(1, 2))
                    memory_scores(b + 1)
                    hidden(b, range(2, FT))
                    turn_probs_tail(b + 1)
                    down(b, 0, b + 2)
                    readout(b + 1)
                    down(b, 1, b + 2)
                    turn_x2(b + 1)

                def leave(b):
                    hidden(b, range(FT))
                    down(b, 0, b + 1)
                    down(b, 1, b + 1)

                over_tail(pe, enter, both, leave)

            @block.scalar
            def _(act):
                def copy(o, i):
                    return act.activation(o, i, ACT.Copy)

                def swap(n, src, dst, done, ready, used):
                    act.wait_ge(ready, n + 1)
                    after(act, used, n)
                    copy(dst[0:64, :], src[64:128, :])
                    copy(dst[64:128, :], src[0:64, :]).then_inc(done, 1)

                def exp_slots(n):
                    act.wait_ge(ve_sc, n + 1)
                    after(act, pe_p, n)
                    act.activation(es[:, :, :], sc[:, :].rearrange("p (a m) -> p a m", a=TT), ACT.Exp).then_inc(ac_es, 1)

                def values(n, b):
                    act.wait_ge(pe_vg, n + 1)
                    after(act, pe_o, n - 1)
                    copy(val[:, b % 2, :, :], ps_vg[:, :, 0:256]).then_inc(ac_val, 1)

                def tanh_gate(n):
                    act.wait_ge(pe_vg, n + 1)
                    after(act, ve_gate, n)
                    act.activation(th[:, :, :], ps_vg[:, :, 256:512], ACT.Tanh, scale=0.5).then_inc(ac_th, 1)

                def slots_turned(n, b):
                    act.wait_ge(pe_est, n + 1)
                    after(act, pe_w2, n - 1)
                    copy(esT[:, b % 2, :], ps_est).then_inc(ac_est, 1)

                def off_diagonal(u, dst, ready, used, done):
                    after(act, used, u)
                    for h in range(2):
                        act.wait_ge(ready, 2 * u + h + 1)
                        copy(dst[:, h, P:T], ps_aw[:, h, P:T]).then_inc(done, 1)

                def square(u):
                    act.wait_ge(pe_o, u + 1)
                    after(act, ve_ss, u)
                    act.activation(sq[:, :, :], ps_o.rearrange("p (a d) -> p a d", a=4), ACT.Square).then_inc(ac_sq, 1)

                def outputs_turned(u):
                    act.wait_ge(pe_ogt, u + 1)
                    after(act, pe_wo, u)
                    copy(ogh[:, :, :], ps_ogt.rearrange("p (a d) -> p a d", a=4)).then_inc(ac_ogh, 1)

                def split_qk(p):
                    act.wait_ge(ld_w, 16 * p + 16)
                    after(act, pe_k, 4 * p)
                    copy(wh[:, :, 0:512], wraw[:, 0:W_S].rearrange("p (k c) -> p k c", k=KT)[:, :, 0:512]).then_inc(w_hi, 1)

                def split_vg(p):
                    after(act, pe_vg, 4 * p)
                    copy(wh[:, :, 512:1024], wraw[:, 0:W_S].rearrange("p (k c) -> p k c", k=KT)[:, :, 512:1024]).then_inc(wv_hi, 1)
                    after(act, pe_s, 4 * p)
                    copy(ws2[:, :], wraw[:, W_S:W_END]).then_inc(ws_hi, 1)

                def split_wo(p):
                    act.wait_ge(ld_wo, 16 * p + 16)
                    after(act, pe_wo, 4 * p)
                    act.activation(woh[:, :, :], woraw[:, :, :], ACT.Copy, scale=gn[:, 0:1]).then_inc(wo_hi, 1)

                act.wait_ge(ld_xf, 16)
                for k in range(KT):
                    copy(xh[:, k, :], xraw[:, k, :]).then_inc(x_hi, 1)
                act.wait_ge(ld_ws1, 16)
                copy(ws1h, ws1_raw).then_inc(ws1_hi, 1)
                split_qk(0)
                split_vg(0)
                act.wait_ge(ld_con, 16)
                for c in range(2):
                    act.wait_ge(s1_mm, c + 1)
                    act.activation(s1_raw[:, c * 512:(c + 1) * 512], ps[:, 6 + c, :], ACT.Identity,
                                   bias=con[:, C_ONECOL:C_ONECOL + 1]).then_inc(s1_full, 1)
                act.wait_ge(s1_full, 2)
                copy(s1[:, :], s1_raw).then_inc(s1_cp, 1)
                swap(0, ps_q, swq, ac_swq, pe_q, ve_qsin)
                swap(0, ps_k, swk, ac_swk, ve_kcos, po_ksin)
                values(0, 0)
                tanh_gate(0)
                exp_slots(0)
                slots_turned(0, 0)
                act.wait_ge(gn_ok, 1)
                split_wo(0)

                def step(u, p, b):
                    nb = (b + 1) % B
                    if not is_first(u):
                        square(u - 1)
                    off_diagonal(u, at, pe_a, pe_p, ac_at)
                    if not is_last(u):
                        swap(u + 1, ps_q, swq, ac_swq, pe_q, ve_qsin)
                        swap(u + 1, ps_k, swk, ac_swk, ve_kcos, po_ksin)
                    if not is_first(u):
                        outputs_turned(u - 1)
                    if not is_last(u):
                        exp_slots(u + 1)
                    act.wait_ge(po_okm, u + 1)
                    after(act, po_qe, u)
                    after(act, ve_sum, u)
                    act.activation(ee[:, :], okm[:, :], ACT.Exp, scale=float(DK) ** -0.5).then_inc(ac_exp, 1)
                    if not is_last(u):
                        values(u + 1, nb)
                    act.wait_ge(pe_qet, u + 1)
                    after(act, pe_w2, u)
                    copy(qeT[:, :], ps_qet).then_inc(ac_qet, 1)
                    if not is_last(u):
                        tanh_gate(u + 1)
                        slots_turned(u + 1, nb)
                    if b == 2 and has_next_pair(p):
                        split_qk(p + 1)
                    off_diagonal(u, wt, pe_w2, pe_o, ac_wt)
                    if b == 2 and has_next_pair(p):
                        split_vg(p + 1)
                    if b == 0 and not is_first(u):
                        split_wo(p)
                    if b == 3 and not has_next_pair(p):
                        act.wait_ge(ld_tail, 80)
                        act.wait_ge(pe_vg, UNITS)
                        copy(w1h[:, :, :], w1raw[:, :, :]).then_inc(w1_hi, 1)

                over_main(act, step)
                square(UNITS - 1)
                outputs_turned(UNITS - 1)

                def x1_turned(b):
                    act.wait_ge(t_x1T, b + 1)
                    after(act, t_sc, b)
                    copy(x1T[:, :, :, :], ps[:, 0, :].rearrange("p (a k t) -> p a k t", a=TT, k=KT)).then_inc(t_x1Ts, 1)

                def exp_memory(b):
                    after(act, t_pT, b)
                    after(act, t_pinv, b)
                    act.wait_ge(t_nmax, b + 1)
                    for tt in range(TT):
                        ins = act.activation(prob[:, tt, :], ps[:, 1 + tt, :], ACT.Exp, bias=nmax[:, tt:tt + 1],
                                             scale=float(D) ** -0.5, accum_out=psum_[:, tt:tt + 1])
                    ins.then_inc(t_prob, 1)

                def probs_turned(b):
                    act.wait_ge(t_pT, b + 1)
                    after(act, t_r, b)
                    copy(probT[:, 0, :, :], ps[:, 3, :].rearrange("p (m t) -> p m t", m=MT)).then_inc(t_pTs0, 1)

                def x2_turned(b):
                    act.wait_ge(t_x2T, b + 1)
                    after(act, t_h, 8 * b)
                    copy(x2h[:, :, :, :], ps[:, 6, :].rearrange("p (k a t) -> p k a t", k=KT, a=TT)).then_inc(t_x2h, 1)

                def router_tanh(b):
                    act.wait_ge(t_rz, b + 1)
                    after(act, t_rw, b)
                    act.activation(rt[:, :], rz[:, :], ACT.Tanh, bias=halfrb[:, 0:1], scale=0.5).then_inc(t_rt, 1)

                def gelu(b, fs):
                    for f in fs:
                        act.wait_ge(t_h, 8 * b + f + 1)
                        if f == 0:
                            after(act, t_y, b)
                        act.activation(hT[:, f, :], ps[:, 7 if f % 2 == 0 else 0, 0:T], ACT.Gelu_apprx_tanh,
                                       bias=vec[:, V_B1 + f:V_B1 + f + 1]).then_inc(t_gelu, 1)

                def enter(b):
                    x1_turned(b)
                    exp_memory(b)
                    probs_turned(b)
                    x2_turned(b)
                    act.wait_ge(rb_ok, 1)
                    router_tanh(b)

                def both(b):
                    x1_turned(b + 1)
                    gelu(b, range(2))
                    exp_memory(b + 1)
                    gelu(b, range(2, FT))
                    probs_turned(b + 1)
                    x2_turned(b + 1)
                    router_tanh(b + 1)

                over_tail(act, enter, both, lambda b: gelu(b, range(FT)))

            @block.vector
            def _(ve):
                tri2 = tri.unsqueeze(1).broadcast_to([P, 2, P])
                cos2 = cos.unsqueeze(1).broadcast_to([P, 2, T])
                sin2 = sin.unsqueeze(1).broadcast_to([P, 2, T])

                def heads(a):
                    return a.rearrange("p (h t) -> p h t", h=2)

                def groups(a, n=4):
                    return a.rearrange("p (g m) -> p g m", g=n)

                def diag(a):
                    return a.rearrange("p (c t) -> p c t", c=3)[:, 0:3:2, :]

                def times_cos(n, src, dst, ready, used, done):
                    ve.wait_ge(ready, n + 1)
                    after(ve, used, n)
                    ve.tensor_tensor(heads(dst[:, :]), heads(src), cos2, ALU.mult).then_inc(done, 1)

                def q_times_sin(n):
                    ve.wait_ge(ac_swq, n + 1)
                    after(ve, po_qr, n)
                    ve.tensor_tensor(heads(qsin[:, :]), heads(swq[:, :]), sin2, ALU.mult).then_inc(ve_qsin, 1)

                def causal(u, dst, ready, used, done):
                    after(ve, used, u)
                    for h in range(2):
                        ve.wait_ge(ready, 2 * u + h + 1)
                        ve.tensor_tensor(diag(dst[:, h, :]), diag(ps_aw[:, h, :]), tri2, ALU.mult).then_inc(done, 1)

                def clip(n):
                    ve.wait_ge(pe_s, n + 1)
                    after(ve, ac_es, n)
                    ve.tensor_scalar(sc[:, :], ps_s, CLAMP, -CLAMP, ALU.min, ALU.max).then_inc(ve_sc, 1)

                def gates(n, b):
                    ve.wait_ge(ac_th, n + 1)
                    ve.scalar_tensor_tensor(out=gate[:, b % 2, :, :], in0=th[:, :, :], scalar=1.0,
                                            in1=ps_vg[:, :, 256:512], op0=ALU.add, op1=ALU.mult).then_inc(ve_gate, 1)

                def inverse_sums(n):
                    ve.wait_ge(pe_c, n + 1)
                    after(ve, po_qe, n)
                    ve.reciprocal(enz[:, :], ps_c).then_inc(ve_enz, 1)

                def mean_square(u):
                    ve.wait_ge(ac_sq, u + 1)
                    after(ve, ve_ze, u)
                    ve.tensor_reduce(ss[:, :], sq[:, :, :], AX, ALU.add).then_inc(ve_ss, 1)
                    ve.wait_ge(ve_sum, u + 1)
                    ve.scalar_tensor_tensor(out=zs[:, :], in0=sume[:, :], scalar=EPS, in1=sume[:, :],
                                            op0=ALU.mult, op1=ALU.mult).then_inc(ve_zs, 1)
                    ve.wait_ge(ve_ss, u + 1)
                    ve.wait_ge(ve_zs, u + 1)
                    after(ve, po_rstd, u)
                    ve.scalar_tensor_tensor(out=ze[:, :], in0=ss[:, :], scalar=1.0 / DK, in1=zs[:, :],
                                            op0=ALU.mult, op1=ALU.add).then_inc(ve_ze, 1)

                def gated(u, b):
                    ve.wait_ge(po_rstd, u + 1)
                    ve.wait_ge(ve_gate, u + 1)
                    after(ve, pe_ogt, u)
                    for g in range(4):
                        mm = ve.scalar_tensor_tensor(
                            out=og[:, g, :], in0=ps_o[:, g * P:(g + 1) * P], scalar=rstd[:, g:g + 1],
                            in1=gate[:, b % 2, g // 2, (g % 2) * DK:(g % 2 + 1) * DK], op0=ALU.mult, op1=ALU.mult)
                    mm.then_inc(ve_og, 1)

                def low_outputs(u):
                    ve.wait_ge(ac_ogh, u + 1)
                    after(ve, pe_wo, u)
                    ve.tensor_tensor(ogl[:, :, :], ps_ogt.rearrange("p (a d) -> p a d", a=4), ogh[:, :, :].bitcast(F32), ALU.subtract).then_inc(ve_ogl, 1)

                def accumulate(u, b):
                    ve.wait_ge(pe_wo, u + 1)
                    after(ve, ve_acc, u)
                    a = acc[:, b * TT:(b + 1) * TT, :]
                    ve.tensor_tensor(a, ps_wo.rearrange("p (a d) -> p a d", a=TT), a, ALU.add).then_inc(ve_acc, 1)

                def low_qk(p):
                    ve.wait_ge(w_hi, p + 1)
                    ve.tensor_tensor(wl[:, :, 0:512], wraw[:, 0:W_S].rearrange("p (k c) -> p k c", k=KT)[:, :, 0:512],
                                     wh[:, :, 0:512].bitcast(F32), ALU.subtract).then_inc(w_qk, 1)

                def low_ws2(p):
                    ve.wait_ge(ws_hi, p + 1)
                    ve.tensor_tensor(ws2[64:128, :], wraw[64:128, W_S:W_END], ws2[64:128, :].bitcast(F32), ALU.subtract).then_inc(w_s, 1)

                def low_wo(p):
                    ve.wait_ge(wo_hi, p + 1)
                    ve.scalar_tensor_tensor(out=wol[:, :, :], in0=woraw[:, :, :], scalar=gn[:, 0:1], in1=woh[:, :, :].bitcast(F32),
                                            op0=ALU.mult, op1=ALU.subtract).then_inc(w_wo, 1)

                for k in range(KT):
                    ve.wait_ge(x_hi, k + 1)
                    ins = ve.tensor_tensor(xl[:, k, :], xraw[:, k, :], xh[:, k, :].bitcast(F32), ALU.subtract)
                ins.then_inc(x_ok, 1)
                ve.wait_ge(ws1_hi, 1)
                ve.tensor_tensor(ws1l, ws1_raw, ws1h.bitcast(F32), ALU.subtract).then_inc(ws1_ok, 1)
                low_qk(0)
                low_ws2(0)
                ve.wait_ge(ld_vec, 16)
                ve.tensor_scalar(gn[:, :], vec[:, V_GN:V_GN + 1], 0.5, None, ALU.mult).then_inc(gn_ok, 1)
                ve.wait_ge(s1_cp, 1)
                for q in (32, 96):
                    ins = ve.tensor_tensor(s1[q:q + 32, :], s1_raw[q:q + 32, :], s1[q:q + 32, :].bitcast(F32), ALU.subtract)
                ins.then_inc(s1_ok, 1)
                ve.wait_ge(ld_con, 16)
                times_cos(0, ps_q, qcos, ac_swq, po_qr, ve_qcos)
                times_cos(0, ps_k, kcos, pe_k, po_kr, ve_kcos)
                q_times_sin(0)
                clip(0)
                gates(0, 0)
                inverse_sums(0)
                ve.wait_ge(gn_ok, 1)
                low_wo(0)
                ve.wait_ge(ld_xt, 16)

                def step(u, p, b):
                    nb = (b + 1) % B
                    if not is_first(u):
                        mean_square(u - 1)
                    causal(u, at, ac_at, pe_p, ve_at)
                    if not is_first(u):
                        gated(u - 1, (b - 1) % B)
                    if not is_last(u):
                        times_cos(u + 1, ps_q, qcos, ac_swq, po_qr, ve_qcos)
                        times_cos(u + 1, ps_k, kcos, pe_k, po_kr, ve_kcos)
                    ve.wait_ge(pe_p, u + 1)
                    ve.wait_ge(ve_enz, u + 1)
                    after(ve, po_okm, u)
                    ve.tensor_tensor(ok[:, :], ps_p, enz[:, :], ALU.mult).then_inc(ve_ok, 1)
                    ve.wait_ge(ve_ok, u + 1)
                    ve.tensor_reduce(mx[:, :], groups(ok[:, :]), AX, ALU.max).then_inc(ve_mx, 1)
                    if not is_last(u):
                        clip(u + 1)
                    if not is_first(u):
                        low_outputs(u - 1)
                    if not is_last(u):
                        q_times_sin(u + 1)
                    ve.wait_ge(ac_exp, u + 1)
                    after(ve, ve_zs, u)
                    ve.tensor_reduce(sume[:, :], groups(ee[:, :]), AX, ALU.add).then_inc(ve_sum, 1)
                    if not is_last(u):
                        gates(u + 1, nb)
                        inverse_sums(u + 1)
                    causal(u, wt, ac_wt, pe_o, ve_wt)
                    if b == 2 and has_next_pair(p):
                        low_qk(p + 1)
                        low_ws2(p + 1)
                    if not is_first(u):
                        accumulate(u - 1, (b - 1) % B)
                    if b == 0 and not is_first(u):
                        low_wo(p)
                    if not has_next_pair(p):
                        moments_x1(b - 1)

                def moments(n, eps, src, bn, st, mv, va, s_bn, s_st, s_mv, s_va):
                    for tt in range(TT):
                        ins = ve.bn_stats(bn[:, tt, :], src(tt))
                    ins.then_inc(s_bn, 1)
                    ve.wait_ge(s_bn, n)
                    ve.tensor_tensor(st[:, 0, :], bn[:, :, 1], bn[:, :, 4], ALU.add)
                    ve.tensor_tensor(st[:, 1, :], bn[:, :, 1], bn[:, :, 4], ALU.subtract)
                    ve.tensor_tensor(st[:, 2, :], bn[:, :, 2], bn[:, :, 5], ALU.add).then_inc(s_st, 1)
                    ve.wait_ge(s_st, n)
                    ve.tensor_scalar(mv, st[:, 0, :], 0.5, None, ALU.mult)
                    ve.scalar_tensor_tensor(out=st[:, 3, :], in0=st[:, 1, :], scalar=0.25, in1=st[:, 1, :], op0=ALU.mult, op1=ALU.mult)
                    ve.tensor_scalar(st[:, 4, :], st[:, 2, :], 1.0 / D, eps, ALU.mult, ALU.add).then_inc(s_mv, 1)
                    ve.wait_ge(s_mv, n)
                    ve.tensor_tensor(va, st[:, 3, :], st[:, 4, :], ALU.add).then_inc(s_va, 1)

                def moments_x1(b):
                    ve.wait_ge(ve_acc, UNITS - B + b + 1)
                    moments(b + 1, EPS, lambda tt: acc[:, b * TT + tt, :], bn1, st1, mv1[:, b, :], ve1[:, b, :], t_bn1, t_st1, t_mv1, t_ve1)

                over_main(ve, step)
                mean_square(UNITS - 1)
                gated(UNITS - 1, B - 1)
                low_outputs(UNITS - 1)
                accumulate(UNITS - 1, B - 1)
                moments_x1(B - 1)

                ve.tensor_scalar(halfrb[:, :], vec[:, V_RB:V_RB + 1], 0.5, None, ALU.mult).then_inc(rb_ok, 1)
                ve.wait_ge(ld_tail, 80)
                m8 = mrow[:, :, :].bitcast(U8)
                ve.tensor_scalar(mneg[:, :, :], m8, -NEG, NEG, ALU.mult, ALU.add).then_inc(mask_ok, 1)
                ve.tensor_reduce(mval[:, :], m8, AX, ALU.max).then_inc(mval_ok, 1)
                ve.tensor_copy(one_r[:, :], ones[0:1, :]).then_inc(one_ok, 1)
                ve.wait_ge(pe_valid, 1)
                ve.tensor_copy(valid[:, :], ps[:, 4, 0:B]).then_inc(valid_ok, 1)

                def norm_x1(b):
                    ve.wait_ge(t_rs1, b + 1)
                    ve.wait_ge(t_mv1, b + 1)
                    after(ve, t_x2p, b)
                    after(ve, t_x1T, b)
                    for tt in range(TT):
                        a = acc[:, bass.ds(b * TT + tt, 1), :].rearrange("p a d -> p (a d)")
                        mean = mv1[:, bass.ds(b, 1), tt:tt + 1].rearrange("p a c -> p (a c)")
                        rs = rs1[:, bass.ds(b, 1), tt:tt + 1].rearrange("p a c -> p (a c)")
                        ins = ve.tensor_scalar(x1[:, tt, :], a, mean, rs, ALU.subtract, ALU.mult)
                    ins.then_inc(t_x1, 1)

                def max_memory(b):
                    ve.wait_ge(t_sc, b + 1)
                    for tt in range(TT):
                        ins = ve.tensor_reduce(smax[:, tt:tt + 1], ps[:, 1 + tt, :], AX, ALU.max)
                    ins.then_inc(t_max, 1)
                    ve.wait_ge(t_max, b + 1)
                    after(ve, t_prob, b)
                    ve.tensor_scalar(nmax[:, :], smax[:, :], -float(D) ** -0.5, None, ALU.mult).then_inc(t_nmax, 1)

                def probs_turned(b):
                    ve.wait_ge(t_pT, b + 1)
                    after(ve, t_r, b)
                    ve.tensor_copy(probT[:, 1, :, :], ps[:, 4, :].rearrange("p (m t) -> p m t", m=MT)).then_inc(t_pTs1, 1)
                    ve.wait_ge(t_prob, b + 1)
                    after(ve, t_pval, b)
                    ve.reciprocal(pinv[:, :], psum_[:, :]).then_inc(t_pinv, 1)
                    ve.wait_ge(t_pinv, b + 1)
                    after(ve, t_x2p, b)
                    ve.tensor_scalar(pval[:, :], pinv[:, :], valid[:, bass.ds(b, 1)], None, ALU.mult).then_inc(t_pval, 1)

                def add_memory(b):
                    ve.wait_ge(t_r, b + 1)
                    ve.wait_ge(t_pval, b + 1)
                    ve.wait_ge(t_x1, b + 1)
                    for tt in range(TT):
                        ins = ve.scalar_tensor_tensor(out=x2p[:, tt, :], in0=ps[:, 5, tt * D:(tt + 1) * D], scalar=pval[:, tt:tt + 1],
                                                      in1=x1[:, tt, :], op0=ALU.mult, op1=ALU.add)
                    ins.then_inc(t_x2p, 1)
                    ve.wait_ge(t_x2p, b + 1)
                    after(ve, t_rs2, b)
                    moments(b + 1, EPS, lambda tt: x2p[:, tt, :], bn2, st2, mv2[:, :], ve2[:, :], t_bn2, t_st2, t_mv2, t_ve2)

                def norm_x2(b):
                    ve.wait_ge(t_rs2, b + 1)
                    after(ve, t_x3, b)
                    for tt in range(TT):
                        ins = ve.tensor_scalar(x2[:, tt, :], x2p[:, tt, :], mv2[:, tt:tt + 1], rs2[:, tt:tt + 1], ALU.subtract, ALU.mult)
                    ins.then_inc(t_x2, 1)
                    ve.wait_ge(t_x2, b + 1)
                    ve.tensor_tensor(rprod[:, :, :], x2[:, :, :], vec[:, V_RW:V_RW + D].unsqueeze(1).broadcast_to([P, TT, D]), ALU.mult).then_inc(t_rprod, 1)
                    ve.wait_ge(t_rprod, b + 1)
                    after(ve, t_rt, b)
                    ve.tensor_reduce(rz[:, :], rprod[:, :, :], AX, ALU.add).then_inc(t_rz, 1)

                def low_x2(b):
                    ve.wait_ge(t_x2h, b + 1)
                    after(ve, t_h, 8 * b)
                    ve.tensor_tensor(x2l[:, :, :, :], ps[:, 6, :].rearrange("p (k a t) -> p k a t", k=KT, a=TT), x2h[:, :, :, :].bitcast(F32),
                                     ALU.subtract).then_inc(t_x2l, 1)
                    ve.wait_ge(t_rt, b + 1)
                    after(ve, t_x3, b)
                    ve.tensor_scalar(rw[:, :], rt[:, :], 0.25, 0.25, ALU.mult, ALU.add).then_inc(t_rw, 1)

                def add_ffn(b):
                    ve.wait_ge(t_y, b + 1)
                    b2 = vec[:, V_B2:V_B2 + D].unsqueeze(1).broadcast_to([P, TT, D])
                    ve.tensor_tensor(yb[:, :, :], ps[:, 1:3, 0:D], b2, ALU.add).then_inc(t_yb, 1)
                    ve.wait_ge(t_yb, b + 1)
                    ve.wait_ge(t_rw, b + 1)
                    for tt in range(TT):
                        ins = ve.scalar_tensor_tensor(out=x3[:, tt, :], in0=yb[:, tt, :], scalar=rw[:, tt:tt + 1], in1=x2[:, tt, :],
                                                      op0=ALU.mult, op1=ALU.add)
                    ins.then_inc(t_x3, 1)
                    ve.wait_ge(t_x3, b + 1)
                    after(ve, t_rs3, b)
                    moments(b + 1, EPS / 4, lambda tt: x3[:, tt, :], bn3, st3, mv3[:, :], ve3[:, :], t_bn3, t_st3, t_mv3, t_ve3)

                def norm_out(b):
                    ve.wait_ge(t_rs3, b + 1)
                    after(ve, stored, 16 * b)
                    for tt in range(TT):
                        ins = ve.tensor_scalar(res[:, tt, :], x3[:, tt, :], mv3[:, tt:tt + 1], rs3[:, tt:tt + 1], ALU.subtract, ALU.mult)
                    ins.then_inc(t_out, 1)

                def enter(b):
                    norm_x1(b)
                    max_memory(b)
                    ve.wait_ge(valid_ok, 1)
                    probs_turned(b)
                    add_memory(b)
                    norm_x2(b)
                    low_x2(b)

                def both(b):
                    norm_x1(b + 1)
                    max_memory(b + 1)
                    probs_turned(b + 1)
                    add_memory(b + 1)
                    add_ffn(b)
                    norm_x2(b + 1)
                    low_x2(b + 1)
                    norm_out(b)

                def leave(b):
                    add_ffn(b)
                    norm_out(b)

                over_tail(ve, enter, both, leave)

            @block.gpsimd
            def _(po):
                sin2 = sin.unsqueeze(1).broadcast_to([P, 2, T])

                def rotate(n):
                    po.wait_ge(ac_swk, n + 1)
                    after(po, po_kr, n)
                    po.tensor_tensor(ksin[:, :].rearrange("p (h t) -> p h t", h=2), swk[:, :].rearrange("p (h t) -> p h t", h=2), sin2, ALU.mult).then_inc(po_ksin, 1)
                    po.wait_ge(ve_qcos, n + 1)
                    po.wait_ge(ve_qsin, n + 1)
                    after(po, pe_a, n)
                    po.tensor_tensor(qr[:, :], qcos[:, :], qsin[:, :], ALU.add).then_inc(po_qr, 1)
                    po.wait_ge(ve_kcos, n + 1)
                    po.wait_ge(po_ksin, n + 1)
                    po.tensor_tensor(kr[:, :], kcos[:, :], ksin[:, :], ALU.add).then_inc(po_kr, 1)

                def inverse_root(u):
                    po.wait_ge(ve_ze, u + 1)
                    after(po, ve_og, u)
                    po.tensor_tensor(rstd[:, :], ze[:, :], con[:, C_HALF:C_HALF + 4], ALU.pow).then_inc(po_rstd, 1)

                def low_vg(p):
                    po.wait_ge(wv_hi, p + 1)
                    po.tensor_tensor(wl[:, :, 512:1024], wraw[:, 0:W_S].rearrange("p (k c) -> p k c", k=KT)[:, :, 512:1024],
                                     wh[:, :, 512:1024].bitcast(F32), ALU.subtract).then_inc(w_vg, 1)

                low_vg(0)
                po.wait_ge(ld_con, 16)
                rotate(0)

                def step(u, p, b):
                    if not is_first(u):
                        inverse_root(u - 1)
                    po.wait_ge(ve_mx, u + 1)
                    after(po, ac_exp, u)
                    po.tensor_tensor(okm[:, :].rearrange("p (g m) -> p g m", g=4), ok[:, :].rearrange("p (g m) -> p g m", g=4),
                                     mx[:, :].unsqueeze(2).broadcast_to([P, 4, M]), ALU.subtract).then_inc(po_okm, 1)
                    po.wait_ge(ac_exp, u + 1)
                    after(po, pe_qet, u)
                    po.tensor_tensor(qe[:, :, :], ee[:, :].rearrange("p (a m) -> p a m", a=TT),
                                     enz[:, :].rearrange("p (a m) -> p a m", a=TT), ALU.mult).then_inc(po_qe, 1)
                    if not is_last(u):
                        rotate(u + 1)
                    if b == 2 and has_next_pair(p):
                        low_vg(p + 1)

                    if b == 3 and not has_next_pair(p):
                        po.wait_ge(w1_hi, 1)
                        po.tensor_tensor(w1l[:, :, :], w1raw[:, :, :], w1h[:, :, :].bitcast(F32), ALU.subtract).then_inc(w1_ok, 1)

                over_main(po, step)
                inverse_root(UNITS - 1)

                half = con[:, C_HALF:C_HALF + B * TT]
                po.wait_ge(t_ve1, B)
                po.tensor_tensor(rs1[:, :, :].rearrange("p b t -> p (b t)"), ve1[:, :, :].rearrange("p b t -> p (b t)"), half, ALU.pow).then_inc(t_rs1, B)

                def root2(b):
                    po.wait_ge(t_ve2, b + 1)
                    after(po, t_x2, b)
                    po.tensor_tensor(rs2[:, :], ve2[:, :], half[:, 0:TT], ALU.pow).then_inc(t_rs2, 1)

                def root3(b):
                    po.wait_ge(t_ve3, b + 1)
                    after(po, t_out, b)
                    po.tensor_tensor(rs3[:, :], ve3[:, :], half[:, 0:TT], ALU.pow).then_inc(t_rs3, 1)

                def both(b):
                    root2(b + 1)
                    root3(b)

                over_tail(po, root2, both, root3)



def _constants():
    inv_freq = (np.float32(1.0) / np.float32(10000.0) ** (np.arange(0, DK, 2, dtype=np.float32) / np.float32(DK))).astype(np.float32)
    ang = (inv_freq[:, None] * np.arange(T, dtype=np.float32)[None, :]).astype(np.float32).astype(np.float64)
    con = np.zeros((P, C_END), np.float32)
    con[:, C_COS:C_COS + T] = np.concatenate([np.cos(ang), np.cos(ang)], 0)
    con[:, C_SIN:C_SIN + T] = np.concatenate([-np.sin(ang), np.sin(ang)], 0)
    con[:, C_TRI:C_TRI + P] = np.triu(np.ones((P, P)))
    con[:, C_ID:C_ID + P] = np.eye(P)
    con[:, C_ONES:C_ONES + P] = 1.0
    con[R::32, C_ONECOL] = 1.0
    con[:, C_HALF:C_HALF + 8] = -0.5
    return con


def kernel(x, ctx_2048, mask_BxS2_bk0, L0_attn_Wq, L0_attn_Wk, L0_attn_Wv, L0_attn_Wg, L0_attn_Wo, L0_attn_Ws1,
           L0_attn_Ws2, L0_attn_bs2, L0_attn_g_norm_weight, L0_ffn_router_weight, L0_ffn_router_bias, L0_ffn_w1,
           L0_ffn_b1, L0_ffn_w2, L0_ffn_b2):
    import concourse.bacc as bacc
    from concourse.bass_utils import run_bass_kernel_spmd

    f32 = np.float32
    x, c = np.asarray(x), np.asarray(ctx_2048)

    def by_partition(a, tiles):
        return a.reshape(tiles, P, -1).transpose(1, 0, 2)

    w = [np.asarray(a).reshape(PAIRS, 2 * DK, KT, P).transpose(0, 3, 2, 1) for a in (L0_attn_Wq, L0_attn_Wk, L0_attn_Wv, L0_attn_Wg)]
    w = np.concatenate(w, 3).reshape(PAIRS, P, KT * 1024)
    stack = np.zeros((PAIRS, 4, 32, 2 * M), f32)
    stack[:, :, 0:R] = np.asarray(L0_attn_Ws2).reshape(PAIRS, 1, 2 * M, R).transpose(0, 1, 3, 2)
    stack[:, :, R] = np.asarray(L0_attn_bs2).reshape(PAIRS, 1, 2 * M)
    w_pairs = np.concatenate([w, stack.reshape(PAIRS, P, 2 * M)], 2)
    wo_pairs = np.asarray(L0_attn_Wo).T.reshape(PAIRS, 2, DK, D).transpose(0, 2, 1, 3)
    ws1 = np.zeros((P, KT, 4, 32), f32)
    ws1[:, :, :, 0:R] = np.asarray(L0_attn_Ws1).T.reshape(KT, P, 1, R).transpose(1, 0, 2, 3)
    vectors = np.zeros((P, V_END), f32)
    vectors[:, V_GN] = np.asarray(L0_attn_g_norm_weight)
    vectors[:, V_B1:V_B1 + FT] = np.asarray(L0_ffn_b1).reshape(FT, P).T
    vectors[:, V_RW:V_RW + D] = np.asarray(L0_ffn_router_weight)[None, :]
    vectors[:, V_RB] = np.asarray(L0_ffn_router_bias)[0]
    vectors[:, V_B2:V_B2 + D] = np.asarray(L0_ffn_b2)[None, :]
    arrays = {
        "x_tok": by_partition(x.reshape(B * T, D), B * TT),
        "x_feat": by_partition(x.reshape(B * T, D).T, KT),
        "w_pairs": w_pairs,
        "wo_pairs": wo_pairs,
        "ws1": ws1.reshape(P, KT, P),
        "consts": _constants(),
        "vectors": vectors,
        "ctx_feat": c.transpose(2, 0, 1).reshape(KT, P, B, S2).transpose(1, 2, 0, 3),
        "ctx_tok": c.reshape(B, MT, P, D).transpose(2, 0, 1, 3),
        "mask": np.ascontiguousarray(mask_BxS2_bk0).view(np.int32).reshape(1, B, S2 // 4),
        "w1": by_partition(np.asarray(L0_ffn_w1), KT),
        "w2": by_partition(np.asarray(L0_ffn_w2), FT),
    }
    arrays = {n: np.ascontiguousarray(a) for n, a in arrays.items()}
    nc = bacc.Bacc("TRN2", target_bir_lowering=False, num_devices=1)
    aps = [nc.dram_tensor(n, a.shape, mybir.dt.from_np(a.dtype), kind="ExternalInput").ap() for n, a in arrays.items()]
    out = nc.dram_tensor("out", (P, B, TT, D), F32, kind="ExternalOutput").ap()
    decoder_layer(nc, *aps, out)
    r = run_bass_kernel_spmd(nc, [arrays], core_ids=[0])
    return r.results[0]["out"].reshape(P, B * TT, D).transpose(1, 0, 2).reshape(B, T, D)
```

```python
import numpy as np
import concourse.bass as bass
from concourse import mybir
from contextlib import ExitStack

F32 = mybir.dt.float32
F32R = mybir.dt.float32r
U8 = mybir.dt.uint8
I32 = mybir.dt.int32
ALU = mybir.AluOpType
ACT = mybir.ActivationFunctionType
AX = mybir.AxisListType.X

B, T, D = 4, 256, 256
H, DK, M, R = 16, 128, 64, 16
S2 = 512
DFF = 1024
P = 128
KT = D // P
TT = T // P
PAIRS = H // 2
UNITS = PAIRS * B
MT = S2 // P
FT = DFF // P
CLAMP = 32.0
EPS = 1e-5
NEG = -1e30

C_COS, C_SIN, C_TRI, C_ID, C_ONES, C_ONECOL, C_HALF, C_END = 0, 256, 512, 640, 768, 896, 897, 905
V_GN, V_B1, V_RW, V_RB, V_B2, V_END = 0, 1, 9, 265, 266, 522
W_QK, W_S, W_END = 1024, KT * 1024, KT * 1024 + 128


def decoder_layer(nc, x_tok, x_feat, w_pairs, wo_pairs, ws1, consts, vectors, ctx_feat, ctx_tok,
                  mask, w1, w2, out):
    ctx = ExitStack()
    with ctx:
        def sb(name, shape, dt=F32):
            return ctx.enter_context(nc.sbuf_tensor(name, shape, dt))

        def sem(name):
            return ctx.enter_context(nc.semaphore(name))

        con = sb("con", [P, C_END])
        vec = sb("vec", [P, V_END])
        cos = con[:, C_COS:C_COS + T]
        sin = con[:, C_SIN:C_SIN + T]
        tri = con[:, C_TRI:C_TRI + P]
        ident = con[:, C_ID:C_ID + P]
        ones = con[:, C_ONES:C_ONES + P]
        acc = sb("acc", [P, B * TT, D])
        xh = sb("xh", [P, KT, B * T], F32R)
        xl = sb("xl", [P, KT, B * T], F32R)
        s1 = sb("s1", [P, B * T], F32R)
        wraw = sb("wraw", [P, W_END])
        wh = sb("wh", [P, KT, 1024], F32R)
        wl = sb("wl", [P, KT, 1024], F32R)
        ws2 = sb("ws2", [P, 2 * M], F32R)
        woraw = sb("woraw", [P, 2, D])
        woh = sb("woh", [P, 2, D], F32R)
        wol = sb("wol", [P, 2, D], F32R)
        gn = sb("gn", [P, 1])
        swq = sb("swq", [P, 2 * T])
        swk = sb("swk", [P, 2 * T])
        qcos = sb("qcos", [P, 2 * T])
        kcos = sb("kcos", [P, 2 * T])
        qsin = sb("qsin", [P, 2 * T])
        ksin = sb("ksin", [P, 2 * T])
        qr = sb("qr", [P, 2 * T])
        kr = sb("kr", [P, 2 * T])
        val = sb("val", [P, 2, TT, 2 * DK])
        th = sb("th", [P, TT, 2 * DK])
        gate = sb("gate", [P, 2, TT, 2 * DK])
        sc = sb("sc", [P, 2 * P])
        es = sb("es", [P, TT, 2 * M])
        esT = sb("esT", [P, 2, T])
        enz = sb("enz", [P, 2 * P])
        at = sb("at", [P, 2, 384])
        wt = sb("wt", [P, 2, 384])
        ok = sb("ok", [P, 2 * P])
        okm = sb("okm", [P, 2 * P])
        ee = sb("ee", [P, 2 * P])
        qe = sb("qe", [P, TT, P])
        qeT = sb("qeT", [P, T])
        mx = sb("mx", [P, 4])
        sume = sb("sume", [P, 4])
        sq = sb("sq", [P, 4, DK])
        ss = sb("ss", [P, 4])
        zs = sb("zs", [P, 4])
        ze = sb("ze", [P, 4])
        rstd = sb("rstd", [P, 4])
        og = sb("og", [P, 4, DK])
        ogh = sb("ogh", [P, 4, P], F32R)
        ogl = sb("ogl", [P, 4, P], F32R)
        ctxf = sb("ctxf", [P, B, KT, S2])
        ctxt = sb("ctxt", [P, B, MT, D])
        mrow = sb("mrow", [1, B, S2 // 4], I32)
        mneg = sb("mneg", [1, B, S2], F32R)
        mval = sb("mval", [1, B])
        valid = sb("valid", [P, B])
        one_r = sb("one_r", [1, P], F32R)
        w1raw = sb("w1raw", [P, KT, DFF])
        w1h, w1l = wh, wl
        w2s = sb("w2s", [P, FT, D])
        halfrb = sb("halfrb", [P, 1])
        bn1, bn2, bn3 = (sb(n, [P, TT, 6]) for n in ("bn1", "bn2", "bn3"))
        st1, st2, st3 = (sb(n, [P, 5, TT]) for n in ("st1", "st2", "st3"))
        mean1, var1, root1 = (sb(n, [P, B, TT]) for n in ("mean1", "var1", "root1"))
        mean2, var2, root2 = (sb(n, [P, B, TT]) for n in ("mean2", "var2", "root2"))
        mean3, var3, root3 = (sb(n, [P, B, TT]) for n in ("mean3", "var3", "root3"))
        x1T = sb("x1T", [P, TT, KT, P])
        smax = sb("smax", [P, B, TT])
        nmax = sb("nmax", [P, B, TT])
        prob = sb("prob", [P, TT, S2])
        psums = sb("psums", [P, B, TT])
        pinv = sb("pinv", [P, B, TT])
        pval = sb("pval", [P, B, TT])
        probT = sb("probT", [P, TT, MT, P])
        x2h = woh[:, :, :].rearrange("p k (a t) -> p k a t", a=TT)
        x2l = wol[:, :, :].rearrange("p k (a t) -> p k a t", a=TT)
        rprod = sb("rprod", [P, TT, D])
        rz, rt, rw = (sb(n, [P, B, TT]) for n in ("rz", "rt", "rw"))
        hT = w1raw[:, :, :].rearrange("p k (f t) -> p (k f) t", t=T)
        yb = sb("yb", [P, TT, D])
        res = sb("res", [P, B, TT, D])

        ps = ctx.enter_context(nc.psum_tensor("ps", [P, 8, 512], F32))
        ps_q, ps_k, ps_c = ps[:, 0, :], ps[:, 1, :], ps[:, 1, 0:256]
        ps_vg, ps_o, ps_wo = ps[:, 2:4, :], ps[:, 2, :], ps[:, 3, :]
        ps_aw = ps[:, 4:6, 0:384]
        ps_s, ps_p, ps_qet = ps[:, 4, 0:256], ps[:, 6, 0:256], ps[:, 6, 0:256]
        ps_ogt, ps_est = ps[:, 7, :], ps[:, 7, 0:256]

        ld_con, ld_vec, ld_xf, ld_xt, ld_ws1 = (sem("ld_" + n) for n in ("con", "vec", "xf", "xt", "ws1"))
        ld_w, ld_wo = sem("ld_w"), sem("ld_wo")
        w_hi, w_qk, w_vg, w_s = sem("w_hi"), sem("w_qk"), sem("w_vg"), sem("w_s")
        wv_hi, ws_hi, wo_hi, w_wo = sem("wv_hi"), sem("ws_hi"), sem("wo_hi"), sem("w_wo")
        gn_ok, x_hi, x_ok = sem("gn_ok"), sem("x_hi"), sem("x_ok")
        ws1_hi, ws1_ok, s1_mm, s1_full, s1_ok = (sem(n) for n in ("ws1_hi", "ws1_ok", "s1_mm", "s1_full", "s1_ok"))
        s1_cp = sem("s1_cp")
        pe_q, pe_k, pe_s, pe_vg, pe_est, pe_c, pe_a, pe_p, pe_qet, pe_w2, pe_o, pe_ogt, pe_wo = (
            sem("pe_" + n) for n in ("q", "k", "s", "vg", "est", "c", "a", "p", "qet", "w2", "o", "ogt", "wo"))
        ac_swq, ac_swk, ac_at, ac_ogh, ac_es, ac_exp, ac_val, ac_qet, ac_th, ac_est, ac_wt, ac_sq = (
            sem("ac_" + n) for n in ("swq", "swk", "at", "ogh", "es", "exp", "val", "qet", "th", "est", "wt", "sq"))
        ve_ss, ve_zs, ve_ze, ve_at, ve_og, ve_qcos, ve_kcos, ve_ok, ve_mx, ve_sc, ve_ogl, ve_qsin = (
            sem("ve_" + n) for n in ("ss", "zs", "ze", "at", "og", "qcos", "kcos", "ok", "mx", "sc", "ogl", "qsin"))
        ve_sum, ve_gate, ve_enz, ve_wt, ve_acc = (sem("ve_" + n) for n in ("sum", "gate", "enz", "wt", "acc"))
        po_rstd, po_okm, po_qe, po_ksin, po_qr, po_kr = (
            sem("po_" + n) for n in ("rstd", "okm", "qe", "ksin", "qr", "kr"))
        ld_tail = sem("ld_tail")
        stored = sem("stored")
        w1_hi, w1_ok, mask_ok, mval_ok, pe_valid, valid_ok, one_ok, rb_ok = (
            sem(n) for n in ("w1_hi", "w1_ok", "mask_ok", "mval_ok", "pe_valid", "valid_ok", "one_ok", "rb_ok"))
        t_bn1, t_st1, t_mean1, t_var1, t_root1, t_x1, t_x1T, t_x1Ts = (
            sem("t_" + n) for n in ("bn1", "st1", "mean1", "var1", "root1", "x1", "x1T", "x1Ts"))
        t_sc, t_max, t_nmax, t_prob = (sem("t_" + n) for n in ("sc", "max", "nmax", "prob"))
        t_pT, t_pTs = sem("t_pT"), (sem("t_pTs0"), sem("t_pTs1"))
        t_pinv, t_pval, t_r, t_x2p, t_bn2, t_st2, t_mean2, t_var2, t_root2, t_x2 = (
            sem("t_" + n) for n in ("pinv", "pval", "r", "x2p", "bn2", "st2", "mean2", "var2", "root2", "x2"))
        t_x2T, t_x2h, t_x2l, t_rprod, t_rz, t_rt, t_rw = (sem("t_" + n) for n in ("x2T", "x2h", "x2l", "rprod", "rz", "rt", "rw"))
        t_h, t_gelu = sem("t_h"), sem("t_gelu")
        t_y, t_yb, t_x3, t_bn3, t_st3, t_mean3, t_var3, t_root3, t_out = (
            sem("t_" + n) for n in ("y", "yb", "x3", "bn3", "st3", "mean3", "var3", "root3", "out"))

        ws1_raw = sc[:, 0:256].rearrange("p (k c) -> p k c", k=KT)
        ws1h, ws1l = ogh[:, 0:2, :], ogl[:, 0:2, :]
        xraw = ctxf[:, 0:2, :, :].rearrange("p b k s -> p (b k s)").rearrange("p (k t) -> p k t", k=KT)
        s1_raw = ctxt[:, 0, :, :].rearrange("p m d -> p (m d)")

        def after(eng, semaphore, count):
            if not isinstance(count, int) or count > 0:
                eng.wait_ge(semaphore, count)

        def over_main(eng, step):
            step(0, 0, 0)
            with eng.Fori(0, PAIRS - 1) as i:
                for b in range(1, B):
                    step(4 * i + b, i, b)
                step(4 * i + 4, i + 1, 0)
            for b in range(1, B):
                step(4 * (PAIRS - 1) + b, PAIRS - 1, b)

        SCORE_BANK, H_BANK, Y_BANK = (1, 0), (7, 6, 2), (5, 5, 1, 5)

        def is_last(u):
            return isinstance(u, int) and u == UNITS - 1

        def is_first(u):
            return isinstance(u, int) and u == 0

        def has_next_pair(p):
            return not (isinstance(p, int) and p == PAIRS - 1)

        with nc.Block() as block:

            @block.sync
            def _(sp):
                sp.dma_start(xraw, x_feat).then_inc(ld_xf, 16)
                sp.dma_start(wraw[:, :], w_pairs[0]).then_inc(ld_w, 16)
                sp.dma_start(ws1_raw, ws1).then_inc(ld_ws1, 16)
                sp.dma_start(con[:, :], consts).then_inc(ld_con, 16)
                sp.dma_start(vec[:, :], vectors).then_inc(ld_vec, 16)
                sp.dma_start(woraw[:, :, :], wo_pairs[0]).then_inc(ld_wo, 16)
                sp.dma_start(acc[:, :, :], x_tok).then_inc(ld_xt, 16)
                sp.wait_ge(x_ok, 1)
                sp.wait_ge(s1_ok, 1)
                sp.dma_start(ctxf[:, :, :, :], ctx_feat).then_inc(ld_tail, 16)
                sp.dma_start(ctxt[:, :, :, :], ctx_tok).then_inc(ld_tail, 16)
                sp.dma_start(mrow[:, :, :], mask).then_inc(ld_tail, 16)
                sp.dma_start(w1raw[:, :, :], w1).then_inc(ld_tail, 16)
                sp.dma_start(w2s[:, :, :], w2).then_inc(ld_tail, 16)
                with sp.Fori(1, PAIRS) as i:
                    sp.wait_ge(w_qk, i)
                    sp.wait_ge(w_vg, i)
                    sp.wait_ge(w_s, i)
                    sp.dma_start(wraw[:, :], w_pairs[bass.ds(i, 1)].rearrange("a p c -> (a p) c")).then_inc(ld_w, 16)
                    sp.wait_ge(w_wo, i)
                    sp.dma_start(woraw[:, :, :], wo_pairs[bass.ds(i, 1)].rearrange("a p h d -> (a p) h d")).then_inc(ld_wo, 16)
                for b in range(B):
                    sp.wait_ge(t_out, b + 1)
                    sp.dma_start(out[:, b, :, :], res[:, b, :, :]).then_inc(stored, 16)
                sp.wait_ge(stored, 16 * B)

            @block.tensor
            def _(pe):
                def passes(o, pairs, first=True, last=True):
                    ops = [x for (ah, al, bh, bl) in pairs for x in ((ah, bh), (ah, bl), (al, bh))]
                    for n, (a, b) in enumerate(ops):
                        mm = pe.matmul(o, a, b, start=first and n == 0, stop=last and n == len(ops) - 1)
                    return mm

                def project_qk(n, p, b):
                    after(pe, ve_qcos, n)
                    after(pe, ac_swq, n)
                    if b == 0:
                        pe.wait_ge(w_qk, p + 1)
                    cols = slice(b * T, (b + 1) * T)
                    for m in range(4):
                        if m == 2:
                            after(pe, ve_kcos, n)
                            after(pe, ac_swk, n)
                            after(pe, ve_enz, n)
                        o = (ps_q if m < 2 else ps_k)[:, (m % 2) * T:(m % 2 + 1) * T]
                        f = slice(m * P, (m + 1) * P)
                        mm = passes(o, [(wh[:, k, f], wl[:, k, f], xh[:, k, cols], xl[:, k, cols]) for k in range(KT)])
                        if m == 1:
                            mm.then_inc(pe_q, 1)
                    mm.then_inc(pe_k, 1)

                def project_vg(n, p, b):
                    after(pe, ac_val, n)
                    after(pe, ac_th, n)
                    after(pe, ve_gate, n)
                    after(pe, ve_og, n - 1)
                    after(pe, ac_sq, n - 1)
                    after(pe, ve_acc, n - 2)
                    if b == 0:
                        pe.wait_ge(w_vg, p + 1)
                    for tt in range(TT):
                        t = slice((b * TT + tt) * P, (b * TT + tt + 1) * P)
                        mm = passes(ps_vg[:, tt, :], [(xh[:, k, t], xl[:, k, t], wh[:, k, W_QK - 512:W_QK], wl[:, k, W_QK - 512:W_QK]) for k in range(KT)])
                    mm.then_inc(pe_vg, 1)

                def slots(n, p, b):
                    after(pe, ve_sc, n)
                    if b == 0:
                        pe.wait_ge(w_s, p + 1)
                    for tt in range(TT):
                        t = slice((b * TT + tt) * P, (b * TT + tt + 1) * P)
                        mm = pe.matmul(ps_s[:, tt * P:(tt + 1) * P], s1[:, t], ws2[:, :], start=True, stop=True)
                    mm.then_inc(pe_s, 1)

                def slot_sums(n):
                    pe.wait_ge(ac_es, n + 1)
                    after(pe, ac_ogh, n - 1)
                    after(pe, ve_ogl, n - 1)
                    for tt in range(TT):
                        mm = pe.transpose(ps_est[:, tt * P:(tt + 1) * P], es[:, tt, :], ident)
                    mm.then_inc(pe_est, 1)
                    pe.wait_ge(ve_kcos, n + 1)
                    pe.wait_ge(ac_swk, n + 1)
                    pe.matmul(ps_c[:, 0:P], tri, es[:, 0, :], start=True, stop=True)
                    pe.matmul(ps_c[:, P:2 * P], ones, es[:, 0, :], start=True, stop=False)
                    pe.matmul(ps_c[:, P:2 * P], tri, es[:, 1, :], start=False, stop=True).then_inc(pe_c, 1)

                def scores(u):
                    pe.wait_ge(po_qr, u + 1)
                    pe.wait_ge(po_kr, u + 1)
                    after(pe, ve_wt, 2 * u)
                    for h in range(2):
                        a = h * T
                        pe.matmul(ps_aw[:, h, 0:T], kr[:, a:a + P], qr[:, a:a + T], start=True, stop=True)
                        pe.matmul(ps_aw[:, h, T:T + P], kr[:, a + P:a + T], qr[:, a + P:a + T], start=True, stop=True).then_inc(pe_a, 1)

                def slot_scores(u):
                    pe.wait_ge(ve_at, 2 * u + 2)
                    after(pe, ac_qet, u)
                    for h in range(2):
                        m = slice(h * M, (h + 1) * M)
                        pe.matmul(ps_p[:, h * M:(h + 1) * M], at[:, h, 0:P], es[:, 0, m], start=True, stop=True)
                        pe.matmul(ps_p[:, (2 + h) * M:(3 + h) * M], at[:, h, P:T], es[:, 0, m], start=True, stop=False)
                        mm = pe.matmul(ps_p[:, (2 + h) * M:(3 + h) * M], at[:, h, T:T + P], es[:, 1, m], start=False, stop=True)
                    mm.then_inc(pe_p, 1)

                def turn_probs(u):
                    pe.wait_ge(po_qe, u + 1)
                    for tt in range(TT):
                        mm = pe.transpose(ps_qet[:, tt * P:(tt + 1) * P], qe[:, tt, :], ident)
                    mm.then_inc(pe_qet, 1)

                def token_weights(u, b):
                    pe.wait_ge(ac_qet, u + 1)
                    pe.wait_ge(ac_est, u + 1)
                    if not is_last(u):
                        pe.wait_ge(ve_sc, u + 2)
                    for h in range(2):
                        m = slice(h * M, (h + 1) * M)
                        e = esT[m, b % 2, :]
                        pe.matmul(ps_aw[:, h, 0:T], e[:, 0:P], qeT[m, 0:T], start=True, stop=True)
                        pe.matmul(ps_aw[:, h, T:T + P], e[:, P:T], qeT[m, P:T], start=True, stop=True).then_inc(pe_w2, 1)

                def outputs(u, b):
                    pe.wait_ge(ve_wt, 2 * u + 2)
                    if not is_last(u):
                        pe.wait_ge(ac_val, u + 2)
                        pe.wait_ge(ac_th, u + 2)
                        pe.wait_ge(ve_gate, u + 2)
                    for h in range(2):
                        d = slice(h * DK, (h + 1) * DK)
                        v = val[:, b % 2, :, d]
                        pe.matmul(ps_o[:, h * P:(h + 1) * P], wt[:, h, 0:P], v[:, 0, :], start=True, stop=True)
                        pe.matmul(ps_o[:, (2 + h) * P:(3 + h) * P], wt[:, h, P:T], v[:, 0, :], start=True, stop=False)
                        mm = pe.matmul(ps_o[:, (2 + h) * P:(3 + h) * P], wt[:, h, T:T + P], v[:, 1, :], start=False, stop=True)
                    mm.then_inc(pe_o, 1)

                def turn_outputs(u):
                    pe.wait_ge(ve_og, u + 1)
                    if is_last(u):
                        pe.wait_ge(ac_est, u + 1)
                    else:
                        pe.wait_ge(ac_est, u + 2)
                    for g in range(4):
                        mm = pe.transpose(ps_ogt[:, g * P:(g + 1) * P], og[:, g, :], ident)
                    mm.then_inc(pe_ogt, 1)

                def project_out(u, p, b):
                    pe.wait_ge(ac_ogh, u + 1)
                    pe.wait_ge(ve_ogl, u + 1)
                    if b == 0:
                        pe.wait_ge(w_wo, p + 1)
                    if not is_last(u):
                        if isinstance(u, int) and u == UNITS - 2:
                            pe.wait_ge(ac_val, u + 2)
                            pe.wait_ge(ac_th, u + 2)
                            pe.wait_ge(ve_gate, u + 2)
                        else:
                            pe.wait_ge(ac_val, u + 3)
                            pe.wait_ge(ac_th, u + 3)
                            pe.wait_ge(ve_gate, u + 3)
                    else:
                        pe.wait_ge(ve_acc, u)
                    for tt in range(TT):
                        mm = passes(ps_wo[:, tt * D:(tt + 1) * D], [(ogh[:, 2 * tt + h, :], ogl[:, 2 * tt + h, :], woh[:, h, :], wol[:, h, :]) for h in range(2)])
                    mm.then_inc(pe_wo, 1)

                pe.wait_ge(x_ok, 1)
                pe.wait_ge(ws1_ok, 1)
                for c in range(2):
                    t = slice(c * 512, (c + 1) * 512)
                    passes(ps[:, 6 + c, :], [(ws1h[:, k, :], ws1l[:, k, :], xh[:, k, t], xl[:, k, t]) for k in range(KT)]).then_inc(s1_mm, 1)
                project_qk(0, 0, 0)
                project_vg(0, 0, 0)
                pe.wait_ge(s1_ok, 1)
                slots(0, 0, 0)
                pe.wait_ge(ld_con, 16)
                slot_sums(0)

                def any_token():
                    pe.wait_ge(mval_ok, 1)
                    pe.wait_ge(ve_enz, UNITS)
                    pe.matmul(ps[:, 1, 0:B], ones[0:1, :], mval[:, :], start=True, stop=True).then_inc(pe_valid, 1)

                def turn_x1(b):
                    pe.wait_ge(t_x1, b + 1)
                    if b == 0:
                        pe.wait_ge(ve_qcos, UNITS)
                    else:
                        pe.wait_ge(t_prob, TT * b)
                    for tt in range(TT):
                        for k in range(KT):
                            mm = pe.transpose(ps[:, 0, (tt * KT + k) * P:(tt * KT + k + 1) * P], acc[:, b * TT + tt, k * P:(k + 1) * P], ident)
                    mm.then_inc(t_x1T, 1)

                def memory_scores(b, tt):
                    pe.wait_ge(t_x1Ts, b + 1)
                    if b == 0 and tt == 0:
                        pe.wait_ge(valid_ok, 1)
                        pe.wait_ge(mask_ok, 1)
                        pe.wait_ge(one_ok, 1)
                    if b > 0:
                        pe.wait_ge(t_prob, TT * b)
                    if b == 3:
                        pe.wait_ge(t_prob, TT * b)
                    o = ps[:, SCORE_BANK[tt], :]
                    pe.matmul(o, one_r[:, :], mneg[:, b, :], start=True, stop=False)
                    for k in range(KT):
                        mm = pe.matmul(o, x1T[:, tt, k, :], ctxf[:, b, k, :], start=False, stop=(k == KT - 1))
                    mm.then_inc(t_sc, 1)

                def turn_memory(b):
                    pe.wait_ge(t_prob, TT * b + TT)
                    if b == 0:
                        pe.wait_ge(ve_acc, UNITS - 1)
                        pe.wait_ge(ve_wt, 2 * UNITS)
                    elif b == 1:
                        pe.wait_ge(ve_acc, UNITS)
                    for tt in range(TT):
                        for m in range(MT):
                            mm = pe.transpose(ps[:, 3 + tt, m * P:(m + 1) * P], prob[:, tt, m * P:(m + 1) * P], ident)
                    mm.then_inc(t_pT, 1)

                def readout(b):
                    for tt in range(TT):
                        pe.wait_ge(t_pTs[tt], b + 1)
                        if tt == 0 and b in (1, 2):
                            pe.wait_ge(t_yb, b)
                        for m in range(MT):
                            mm = pe.matmul(ps[:, 5, tt * D:(tt + 1) * D], probT[:, tt, m, :], ctxt[:, b, m, :], start=(m == 0), stop=(m == MT - 1))
                    mm.then_inc(t_r, 1)

                def turn_x2(b):
                    pe.wait_ge(t_x2, b + 1)
                    for k in range(KT):
                        for tt in range(TT):
                            mm = pe.transpose(ps[:, 6, (k * TT + tt) * P:(k * TT + tt + 1) * P], acc[:, b * TT + tt, k * P:(k + 1) * P], ident)
                    mm.then_inc(t_x2T, 1)

                def hidden(b):
                    pe.wait_ge(t_x2l, b + 1)
                    if b == 0:
                        pe.wait_ge(w1_ok, 1)
                        pe.wait_ge(ve_og, UNITS)
                        pe.wait_ge(ve_ogl, UNITS)
                    for f in range(FT):
                        after(pe, t_gelu, FT * b + f - 2 if f > 2 else FT * b)
                        c = slice(f * P, (f + 1) * P)
                        passes(ps[:, H_BANK[f % 3], 0:T], [(w1h[:, k, c], w1l[:, k, c], x2h[:, k, :, :].rearrange("p a t -> p (a t)"),
                               x2l[:, k, :, :].rearrange("p a t -> p (a t)")) for k in range(KT)]).then_inc(t_h, 1)

                def down(b):
                    pe.wait_ge(t_gelu, FT * b + FT)
                    if Y_BANK[b] == 5:
                        pe.wait_ge(t_x2p, b + 1)
                    else:
                        pe.wait_ge(t_prob, TT * B)
                    for tt in range(TT):
                        for f in range(FT):
                            mm = pe.matmul(ps[:, Y_BANK[b], tt * D:(tt + 1) * D], hT[:, f, tt * P:(tt + 1) * P], w2s[:, f, :], start=(f == 0), stop=(f == FT - 1))
                    mm.then_inc(t_y, 1)

                def step(u, p, b):
                    nb = (b + 1) % B
                    np_ = p + 1 if b == B - 1 and has_next_pair(p) else p
                    scores(u)
                    if is_last(u):
                        any_token()
                        turn_x1(0)
                    else:
                        project_qk(u + 1, np_, nb)
                    slot_scores(u)
                    if not is_first(u):
                        turn_outputs(u - 1)
                    if is_last(u):
                        memory_scores(0, 0)
                    else:
                        slots(u + 1, np_, nb)
                        project_vg(u + 1, np_, nb)
                    turn_probs(u)
                    if is_last(u):
                        memory_scores(0, 1)
                    else:
                        slot_sums(u + 1)
                    token_weights(u, b)
                    if not is_first(u):
                        project_out(u - 1, p - 1 if b == 0 else p, (b - 1) % B)
                    outputs(u, b)

                over_main(pe, step)
                turn_memory(0)
                turn_x1(1)
                readout(0)
                turn_outputs(UNITS - 1)
                memory_scores(1, 0)
                memory_scores(1, 1)
                project_out(UNITS - 1, PAIRS - 1, B - 1)
                turn_x2(0)
                for b in range(2):
                    hidden(b)
                    down(b)
                    turn_memory(b + 1)
                    turn_x1(b + 2)
                    readout(b + 1)
                    memory_scores(b + 2, 0)
                    turn_x2(b + 1)
                    memory_scores(b + 2, 1)
                hidden(2)
                turn_memory(3)
                readout(3)
                down(2)
                turn_x2(3)
                hidden(3)
                down(3)

            @block.scalar
            def _(act):
                def copy(o, i):
                    return act.activation(o, i, ACT.Copy)

                def swap(n, src, dst, done, ready, used):
                    act.wait_ge(ready, n + 1)
                    after(act, used, n)
                    copy(dst[0:64, :], src[64:128, :])
                    copy(dst[64:128, :], src[0:64, :]).then_inc(done, 1)

                def exp_slots(n):
                    act.wait_ge(ve_sc, n + 1)
                    after(act, pe_p, n)
                    act.activation(es[:, :, :], sc[:, :].rearrange("p (a m) -> p a m", a=TT), ACT.Exp).then_inc(ac_es, 1)

                def values(n, b):
                    act.wait_ge(pe_vg, n + 1)
                    after(act, pe_o, n - 1)
                    copy(val[:, b % 2, :, :], ps_vg[:, :, 0:256]).then_inc(ac_val, 1)

                def tanh_gate(n):
                    act.wait_ge(pe_vg, n + 1)
                    after(act, ve_gate, n)
                    act.activation(th[:, :, :], ps_vg[:, :, 256:512], ACT.Tanh, scale=0.5).then_inc(ac_th, 1)

                def slots_turned(n, b):
                    act.wait_ge(pe_est, n + 1)
                    after(act, pe_w2, n - 1)
                    copy(esT[:, b % 2, :], ps_est).then_inc(ac_est, 1)

                def off_diagonal(u, dst, ready, used, done):
                    after(act, used, u)
                    for h in range(2):
                        act.wait_ge(ready, 2 * u + h + 1)
                        copy(dst[:, h, P:T], ps_aw[:, h, P:T]).then_inc(done, 1)

                def square(u):
                    act.wait_ge(pe_o, u + 1)
                    after(act, ve_ss, u)
                    act.activation(sq[:, :, :], ps_o.rearrange("p (a d) -> p a d", a=4), ACT.Square).then_inc(ac_sq, 1)

                def outputs_turned(u):
                    act.wait_ge(pe_ogt, u + 1)
                    after(act, pe_wo, u)
                    copy(ogh[:, :, :], ps_ogt.rearrange("p (a d) -> p a d", a=4)).then_inc(ac_ogh, 1)

                def split_qk(p):
                    act.wait_ge(ld_w, 16 * p + 16)
                    after(act, pe_k, 4 * p)
                    copy(wh[:, :, 0:512], wraw[:, 0:W_S].rearrange("p (k c) -> p k c", k=KT)[:, :, 0:512]).then_inc(w_hi, 1)

                def split_vg(p):
                    after(act, pe_vg, 4 * p)
                    copy(wh[:, :, 512:1024], wraw[:, 0:W_S].rearrange("p (k c) -> p k c", k=KT)[:, :, 512:1024]).then_inc(wv_hi, 1)
                    after(act, pe_s, 4 * p)
                    copy(ws2[:, :], wraw[:, W_S:W_END]).then_inc(ws_hi, 1)

                def split_wo(p):
                    act.wait_ge(ld_wo, 16 * p + 16)
                    after(act, pe_wo, 4 * p)
                    act.activation(woh[:, :, :], woraw[:, :, :], ACT.Copy, scale=gn[:, 0:1]).then_inc(wo_hi, 1)

                act.wait_ge(ld_xf, 16)
                for k in range(KT):
                    copy(xh[:, k, :], xraw[:, k, :]).then_inc(x_hi, 1)
                act.wait_ge(ld_ws1, 16)
                copy(ws1h, ws1_raw).then_inc(ws1_hi, 1)
                split_qk(0)
                split_vg(0)
                act.wait_ge(ld_con, 16)
                for c in range(2):
                    act.wait_ge(s1_mm, c + 1)
                    act.activation(s1_raw[:, c * 512:(c + 1) * 512], ps[:, 6 + c, :], ACT.Identity,
                                   bias=con[:, C_ONECOL:C_ONECOL + 1]).then_inc(s1_full, 1)
                act.wait_ge(s1_full, 2)
                copy(s1[:, :], s1_raw).then_inc(s1_cp, 1)
                swap(0, ps_q, swq, ac_swq, pe_q, ve_qsin)
                swap(0, ps_k, swk, ac_swk, ve_kcos, po_ksin)
                values(0, 0)
                tanh_gate(0)
                exp_slots(0)
                slots_turned(0, 0)
                act.wait_ge(gn_ok, 1)
                split_wo(0)

                def exp_memory(b, tt):
                    act.wait_ge(t_nmax, TT * b + tt + 1)
                    after(act, t_pT, b)
                    act.activation(prob[:, tt, :], ps[:, SCORE_BANK[tt], :], ACT.Exp, bias=nmax[:, b, tt:tt + 1],
                                   scale=float(D) ** -0.5, accum_out=psums[:, b, tt:tt + 1]).then_inc(t_prob, 1)

                def memory_turned(b):
                    act.wait_ge(t_pT, b + 1)
                    after(act, t_r, b)
                    copy(probT[:, 0, :, :], ps[:, 3, :].rearrange("p (m t) -> p m t", m=MT)).then_inc(t_pTs[0], 1)

                def x2_turned(b):
                    act.wait_ge(t_x2T, b + 1)
                    after(act, t_h, FT * b)
                    copy(x2h, ps[:, 6, :].rearrange("p (k a t) -> p k a t", k=KT, a=TT)).then_inc(t_x2h, 1)

                def gelu(b):
                    act.wait_ge(t_rz, b + 1)
                    act.activation(rt[:, b, :], rz[:, b, :], ACT.Tanh, bias=halfrb[:, 0:1], scale=0.5).then_inc(t_rt, 1)
                    for f in range(FT):
                        act.wait_ge(t_h, FT * b + f + 1)
                        if f == 0:
                            after(act, t_y, b)
                        act.activation(hT[:, f, :], ps[:, H_BANK[f % 3], 0:T], ACT.Gelu_apprx_tanh,
                                       bias=vec[:, V_B1 + f:V_B1 + f + 1]).then_inc(t_gelu, 1)

                def step(u, p, b):
                    nb = (b + 1) % B
                    if not is_first(u):
                        square(u - 1)
                    off_diagonal(u, at, pe_a, pe_p, ac_at)
                    if not is_last(u):
                        swap(u + 1, ps_q, swq, ac_swq, pe_q, ve_qsin)
                        swap(u + 1, ps_k, swk, ac_swk, ve_kcos, po_ksin)
                    if not is_first(u):
                        outputs_turned(u - 1)
                    if not is_last(u):
                        exp_slots(u + 1)
                    act.wait_ge(po_okm, u + 1)
                    after(act, po_qe, u)
                    after(act, ve_sum, u)
                    act.activation(ee[:, :], okm[:, :], ACT.Exp, scale=float(DK) ** -0.5).then_inc(ac_exp, 1)
                    if not is_last(u):
                        values(u + 1, nb)
                    act.wait_ge(pe_qet, u + 1)
                    after(act, pe_w2, 2 * u)
                    copy(qeT[:, :], ps_qet).then_inc(ac_qet, 1)
                    if is_last(u):
                        exp_memory(0, 0)
                    else:
                        tanh_gate(u + 1)
                        slots_turned(u + 1, nb)
                    if b == 2 and has_next_pair(p):
                        split_qk(p + 1)
                    off_diagonal(u, wt, pe_w2, pe_o, ac_wt)
                    if is_last(u):
                        exp_memory(0, 1)
                    if b == 2 and has_next_pair(p):
                        split_vg(p + 1)
                    if b == 0 and not is_first(u):
                        split_wo(p)
                    if b == 2 and not has_next_pair(p):
                        act.wait_ge(ld_tail, 80)
                        act.wait_ge(pe_vg, UNITS)
                        copy(w1h[:, :, :], w1raw[:, :, :]).then_inc(w1_hi, 1)

                over_main(act, step)
                square(UNITS - 1)
                memory_turned(0)
                outputs_turned(UNITS - 1)
                exp_memory(1, 0)
                exp_memory(1, 1)
                act.wait_ge(rb_ok, 1)
                x2_turned(0)
                gelu(0)
                memory_turned(1)
                x2_turned(1)
                gelu(1)
                exp_memory(2, 0)
                exp_memory(2, 1)
                memory_turned(2)
                x2_turned(2)
                exp_memory(3, 0)
                exp_memory(3, 1)
                gelu(2)
                memory_turned(3)
                x2_turned(3)
                gelu(3)

            @block.vector
            def _(ve):
                tri2 = tri.unsqueeze(1).broadcast_to([P, 2, P])
                cos2 = cos.unsqueeze(1).broadcast_to([P, 2, T])
                sin2 = sin.unsqueeze(1).broadcast_to([P, 2, T])

                def heads(a):
                    return a.rearrange("p (h t) -> p h t", h=2)

                def groups(a, n=4):
                    return a.rearrange("p (g m) -> p g m", g=n)

                def diag(a):
                    return a.rearrange("p (c t) -> p c t", c=3)[:, 0:3:2, :]

                def times_cos(n, src, dst, ready, used, done):
                    ve.wait_ge(ready, n + 1)
                    after(ve, used, n)
                    ve.tensor_tensor(heads(dst[:, :]), heads(src), cos2, ALU.mult).then_inc(done, 1)

                def q_times_sin(n):
                    ve.wait_ge(ac_swq, n + 1)
                    after(ve, po_qr, n)
                    ve.tensor_tensor(heads(qsin[:, :]), heads(swq[:, :]), sin2, ALU.mult).then_inc(ve_qsin, 1)

                def causal(u, dst, ready, used, done):
                    after(ve, used, u)
                    for h in range(2):
                        ve.wait_ge(ready, 2 * u + h + 1)
                        ve.tensor_tensor(diag(dst[:, h, :]), diag(ps_aw[:, h, :]), tri2, ALU.mult).then_inc(done, 1)

                def clip(n):
                    ve.wait_ge(pe_s, n + 1)
                    after(ve, ac_es, n)
                    ve.tensor_scalar(sc[:, :], ps_s, CLAMP, -CLAMP, ALU.min, ALU.max).then_inc(ve_sc, 1)

                def gates(n, b):
                    ve.wait_ge(ac_th, n + 1)
                    ve.scalar_tensor_tensor(out=gate[:, b % 2, :, :], in0=th[:, :, :], scalar=1.0,
                                            in1=ps_vg[:, :, 256:512], op0=ALU.add, op1=ALU.mult).then_inc(ve_gate, 1)

                def inverse_sums(n):
                    ve.wait_ge(pe_c, n + 1)
                    after(ve, po_qe, n)
                    ve.reciprocal(enz[:, :], ps_c).then_inc(ve_enz, 1)

                def mean_square(u):
                    ve.wait_ge(ac_sq, u + 1)
                    after(ve, ve_ze, u)
                    ve.tensor_reduce(ss[:, :], sq[:, :, :], AX, ALU.add).then_inc(ve_ss, 1)
                    ve.wait_ge(ve_sum, u + 1)
                    ve.scalar_tensor_tensor(out=zs[:, :], in0=sume[:, :], scalar=EPS, in1=sume[:, :],
                                            op0=ALU.mult, op1=ALU.mult).then_inc(ve_zs, 1)
                    ve.wait_ge(ve_ss, u + 1)
                    ve.wait_ge(ve_zs, u + 1)
                    after(ve, po_rstd, u)
                    ve.scalar_tensor_tensor(out=ze[:, :], in0=ss[:, :], scalar=1.0 / DK, in1=zs[:, :],
                                            op0=ALU.mult, op1=ALU.add).then_inc(ve_ze, 1)

                def gated(u, b):
                    ve.wait_ge(po_rstd, u + 1)
                    ve.wait_ge(ve_gate, u + 1)
                    after(ve, pe_ogt, u)
                    for g in range(4):
                        mm = ve.scalar_tensor_tensor(
                            out=og[:, g, :], in0=ps_o[:, g * P:(g + 1) * P], scalar=rstd[:, g:g + 1],
                            in1=gate[:, b % 2, g // 2, (g % 2) * DK:(g % 2 + 1) * DK], op0=ALU.mult, op1=ALU.mult)
                    mm.then_inc(ve_og, 1)

                def low_outputs(u):
                    ve.wait_ge(ac_ogh, u + 1)
                    after(ve, pe_wo, u)
                    ve.tensor_tensor(ogl[:, :, :], ps_ogt.rearrange("p (a d) -> p a d", a=4), ogh[:, :, :].bitcast(F32), ALU.subtract).then_inc(ve_ogl, 1)

                def accumulate(u, b):
                    ve.wait_ge(pe_wo, u + 1)
                    after(ve, ve_acc, u)
                    a = acc[:, b * TT:(b + 1) * TT, :]
                    ve.tensor_tensor(a, ps_wo.rearrange("p (a d) -> p a d", a=TT), a, ALU.add).then_inc(ve_acc, 1)

                def low_qk(p):
                    ve.wait_ge(w_hi, p + 1)
                    ve.tensor_tensor(wl[:, :, 0:512], wraw[:, 0:W_S].rearrange("p (k c) -> p k c", k=KT)[:, :, 0:512],
                                     wh[:, :, 0:512].bitcast(F32), ALU.subtract).then_inc(w_qk, 1)

                def low_ws2(p):
                    ve.wait_ge(ws_hi, p + 1)
                    ve.tensor_tensor(ws2[64:128, :], wraw[64:128, W_S:W_END], ws2[64:128, :].bitcast(F32), ALU.subtract).then_inc(w_s, 1)

                def low_wo(p):
                    ve.wait_ge(wo_hi, p + 1)
                    ve.scalar_tensor_tensor(out=wol[:, :, :], in0=woraw[:, :, :], scalar=gn[:, 0:1], in1=woh[:, :, :].bitcast(F32),
                                            op0=ALU.mult, op1=ALU.subtract).then_inc(w_wo, 1)

                for k in range(KT):
                    ve.wait_ge(x_hi, k + 1)
                    ins = ve.tensor_tensor(xl[:, k, :], xraw[:, k, :], xh[:, k, :].bitcast(F32), ALU.subtract)
                ins.then_inc(x_ok, 1)
                ve.wait_ge(ws1_hi, 1)
                ve.tensor_tensor(ws1l, ws1_raw, ws1h.bitcast(F32), ALU.subtract).then_inc(ws1_ok, 1)
                low_qk(0)
                low_ws2(0)
                ve.wait_ge(ld_vec, 16)
                ve.tensor_scalar(gn[:, :], vec[:, V_GN:V_GN + 1], 0.5, None, ALU.mult).then_inc(gn_ok, 1)
                ve.wait_ge(s1_cp, 1)
                for q in (32, 96):
                    ins = ve.tensor_tensor(s1[q:q + 32, :], s1_raw[q:q + 32, :], s1[q:q + 32, :].bitcast(F32), ALU.subtract)
                ins.then_inc(s1_ok, 1)
                ve.wait_ge(ld_con, 16)
                times_cos(0, ps_q, qcos, ac_swq, po_qr, ve_qcos)
                times_cos(0, ps_k, kcos, pe_k, po_kr, ve_kcos)
                q_times_sin(0)
                clip(0)
                gates(0, 0)
                inverse_sums(0)
                ve.wait_ge(gn_ok, 1)
                low_wo(0)
                ve.wait_ge(ld_xt, 16)

                def moments(b, eps, bn, st, mean, var, s_bn, s_st, s_mean, s_var):
                    for tt in range(TT):
                        ins = ve.bn_stats(bn[:, tt, :], acc[:, b * TT + tt, :])
                    ins.then_inc(s_bn, 1)
                    ve.wait_ge(s_bn, b + 1)
                    ve.tensor_tensor(st[:, 0, :], bn[:, :, 1], bn[:, :, 4], ALU.add)
                    ve.tensor_tensor(st[:, 1, :], bn[:, :, 1], bn[:, :, 4], ALU.subtract)
                    ve.tensor_tensor(st[:, 2, :], bn[:, :, 2], bn[:, :, 5], ALU.add).then_inc(s_st, 1)
                    ve.wait_ge(s_st, b + 1)
                    ve.tensor_scalar(mean[:, b, :], st[:, 0, :], 0.5, None, ALU.mult)
                    ve.scalar_tensor_tensor(out=st[:, 3, :], in0=st[:, 1, :], scalar=0.25, in1=st[:, 1, :], op0=ALU.mult, op1=ALU.mult)
                    ve.tensor_scalar(st[:, 4, :], st[:, 2, :], 1.0 / D, eps, ALU.mult, ALU.add).then_inc(s_mean, 1)
                    ve.wait_ge(s_mean, b + 1)
                    ve.tensor_tensor(var[:, b, :], st[:, 3, :], st[:, 4, :], ALU.add).then_inc(s_var, 1)

                def normalise(b, dst, mean, root, s_root, s_out):
                    ve.wait_ge(s_root, b + 1)
                    for tt in range(TT):
                        ins = ve.tensor_scalar(dst(tt), acc[:, b * TT + tt, :], mean[:, b, tt:tt + 1], root[:, b, tt:tt + 1], ALU.subtract, ALU.mult)
                    ins.then_inc(s_out, 1)

                def in_place(b):
                    return lambda tt: acc[:, b * TT + tt, :]

                def moments_x1(b):
                    ve.wait_ge(ve_acc, UNITS - B + b + 1)
                    moments(b, EPS, bn1, st1, mean1, var1, t_bn1, t_st1, t_mean1, t_var1)

                def norm_x1(b):
                    normalise(b, in_place(b), mean1, root1, t_root1, t_x1)

                def small_inputs():
                    ve.tensor_scalar(halfrb[:, :], vec[:, V_RB:V_RB + 1], 0.5, None, ALU.mult).then_inc(rb_ok, 1)
                    ve.wait_ge(ld_tail, 80)
                    m8 = mrow[:, :, :].bitcast(U8)
                    ve.tensor_scalar(mneg[:, :, :], m8, -NEG, NEG, ALU.mult, ALU.add).then_inc(mask_ok, 1)
                    ve.tensor_reduce(mval[:, :], m8, AX, ALU.max).then_inc(mval_ok, 1)
                    ve.tensor_copy(one_r[:, :], ones[0:1, :]).then_inc(one_ok, 1)

                def x1_turned(b):
                    ve.wait_ge(t_x1T, b + 1)
                    after(ve, t_sc, TT * b)
                    ve.tensor_copy(x1T[:, :, :, :], ps[:, 0, :].rearrange("p (a k t) -> p a k t", a=TT, k=KT)).then_inc(t_x1Ts, 1)

                def max_memory(b, tt):
                    ve.wait_ge(t_sc, TT * b + tt + 1)
                    ve.tensor_reduce(smax[:, b, tt:tt + 1], ps[:, SCORE_BANK[tt], :], AX, ALU.max).then_inc(t_max, 1)
                    ve.wait_ge(t_max, TT * b + tt + 1)
                    ve.tensor_scalar(nmax[:, b, tt:tt + 1], smax[:, b, tt:tt + 1], -float(D) ** -0.5, None, ALU.mult).then_inc(t_nmax, 1)

                def memory_turned(b):
                    ve.wait_ge(t_pT, b + 1)
                    after(ve, t_r, b)
                    ve.tensor_copy(probT[:, 1, :, :], ps[:, 4, :].rearrange("p (m t) -> p m t", m=MT)).then_inc(t_pTs[1], 1)
                    ve.wait_ge(t_prob, TT * b + TT)
                    ve.reciprocal(pinv[:, b, :], psums[:, b, :]).then_inc(t_pinv, 1)
                    ve.wait_ge(t_pinv, b + 1)
                    ve.tensor_scalar(pval[:, b, :], pinv[:, b, :], valid[:, b:b + 1], None, ALU.mult).then_inc(t_pval, 1)

                def add_memory(b):
                    ve.wait_ge(t_r, b + 1)
                    ve.wait_ge(t_pval, b + 1)
                    for tt in range(TT):
                        ins = ve.scalar_tensor_tensor(out=acc[:, b * TT + tt, :], in0=ps[:, 5, tt * D:(tt + 1) * D], scalar=pval[:, b, tt:tt + 1],
                                                      in1=acc[:, b * TT + tt, :], op0=ALU.mult, op1=ALU.add)
                    ins.then_inc(t_x2p, 1)
                    ve.wait_ge(t_x2p, b + 1)
                    moments(b, EPS, bn2, st2, mean2, var2, t_bn2, t_st2, t_mean2, t_var2)

                def norm_x2(b):
                    normalise(b, in_place(b), mean2, root2, t_root2, t_x2)

                def router(b):
                    ve.wait_ge(t_x2, b + 1)
                    ve.tensor_tensor(rprod[:, :, :], acc[:, b * TT:(b + 1) * TT, :], vec[:, V_RW:V_RW + D].unsqueeze(1).broadcast_to([P, TT, D]), ALU.mult).then_inc(t_rprod, 1)
                    ve.wait_ge(t_rprod, b + 1)
                    ve.tensor_reduce(rz[:, b, :], rprod[:, :, :], AX, ALU.add).then_inc(t_rz, 1)

                def low_x2(b):
                    ve.wait_ge(t_x2h, b + 1)
                    after(ve, t_h, FT * b)
                    ve.tensor_tensor(x2l, ps[:, 6, :].rearrange("p (k a t) -> p k a t", k=KT, a=TT), x2h.bitcast(F32),
                                     ALU.subtract).then_inc(t_x2l, 1)

                def add_ffn(b):
                    ve.wait_ge(t_rt, b + 1)
                    ve.tensor_scalar(rw[:, b, :], rt[:, b, :], 0.25, 0.25, ALU.mult, ALU.add).then_inc(t_rw, 1)
                    ve.wait_ge(t_y, b + 1)
                    b2 = vec[:, V_B2:V_B2 + D].unsqueeze(1).broadcast_to([P, TT, D])
                    ve.tensor_tensor(yb[:, :, :], ps[:, Y_BANK[b], :].rearrange("p (a d) -> p a d", a=TT), b2, ALU.add).then_inc(t_yb, 1)
                    ve.wait_ge(t_yb, b + 1)
                    ve.wait_ge(t_rw, b + 1)
                    for tt in range(TT):
                        ins = ve.scalar_tensor_tensor(out=acc[:, b * TT + tt, :], in0=yb[:, tt, :], scalar=rw[:, b, tt:tt + 1], in1=acc[:, b * TT + tt, :],
                                                      op0=ALU.mult, op1=ALU.add)
                    ins.then_inc(t_x3, 1)
                    ve.wait_ge(t_x3, b + 1)
                    moments(b, EPS / 4, bn3, st3, mean3, var3, t_bn3, t_st3, t_mean3, t_var3)

                def norm_out(b):
                    normalise(b, lambda tt: res[:, b, tt, :], mean3, root3, t_root3, t_out)

                def step(u, p, b):
                    nb = (b + 1) % B
                    if not is_first(u):
                        mean_square(u - 1)
                    causal(u, at, ac_at, pe_p, ve_at)
                    if is_last(u):
                        ve.wait_ge(pe_valid, 1)
                        ve.tensor_copy(valid[:, :], ps[:, 1, 0:B]).then_inc(valid_ok, 1)
                        x1_turned(0)
                    if not is_first(u):
                        gated(u - 1, (b - 1) % B)
                    if not is_last(u):
                        times_cos(u + 1, ps_q, qcos, ac_swq, po_qr, ve_qcos)
                        times_cos(u + 1, ps_k, kcos, pe_k, po_kr, ve_kcos)
                    ve.wait_ge(pe_p, u + 1)
                    ve.wait_ge(ve_enz, u + 1)
                    after(ve, po_okm, u)
                    ve.tensor_tensor(ok[:, :], ps_p, enz[:, :], ALU.mult).then_inc(ve_ok, 1)
                    ve.wait_ge(ve_ok, u + 1)
                    ve.tensor_reduce(mx[:, :], groups(ok[:, :]), AX, ALU.max).then_inc(ve_mx, 1)
                    if not is_last(u):
                        clip(u + 1)
                    if not is_first(u):
                        low_outputs(u - 1)
                    if not is_last(u):
                        q_times_sin(u + 1)
                    ve.wait_ge(ac_exp, u + 1)
                    after(ve, ve_zs, u)
                    ve.tensor_reduce(sume[:, :], groups(ee[:, :]), AX, ALU.add).then_inc(ve_sum, 1)
                    if is_last(u):
                        max_memory(0, 0)
                    else:
                        gates(u + 1, nb)
                    causal(u, wt, ac_wt, pe_o, ve_wt)
                    if not is_last(u):
                        inverse_sums(u + 1)
                    else:
                        max_memory(0, 1)
                    if b == 2 and has_next_pair(p):
                        low_qk(p + 1)
                        low_ws2(p + 1)
                    if not is_first(u):
                        accumulate(u - 1, (b - 1) % B)
                    if b == 0 and not is_first(u):
                        low_wo(p)
                    if not has_next_pair(p):
                        moments_x1(b - 1)
                        if b == 1:
                            small_inputs()
                        if b == 2:
                            norm_x1(0)

                over_main(ve, step)
                mean_square(UNITS - 1)
                ve.wait_ge(valid_ok, 1)
                norm_x1(1)
                gated(UNITS - 1, B - 1)
                memory_turned(0)
                x1_turned(1)
                add_memory(0)
                low_outputs(UNITS - 1)
                max_memory(1, 0)
                norm_x2(0)
                max_memory(1, 1)
                low_x2(0)
                router(0)
                accumulate(UNITS - 1, B - 1)
                moments_x1(3)
                norm_x1(2)
                norm_x1(3)
                for b in range(2):
                    add_ffn(b)
                    memory_turned(b + 1)
                    x1_turned(b + 2)
                    norm_out(b)
                    add_memory(b + 1)
                    max_memory(b + 2, 0)
                    norm_x2(b + 1)
                    low_x2(b + 1)
                    max_memory(b + 2, 1)
                    router(b + 1)
                memory_turned(3)
                add_memory(3)
                norm_x2(3)
                low_x2(3)
                router(3)
                add_ffn(2)
                norm_out(2)
                add_ffn(3)
                norm_out(3)

            @block.gpsimd
            def _(po):
                sin2 = sin.unsqueeze(1).broadcast_to([P, 2, T])

                def rotate(n):
                    po.wait_ge(ac_swk, n + 1)
                    after(po, po_kr, n)
                    po.tensor_tensor(ksin[:, :].rearrange("p (h t) -> p h t", h=2), swk[:, :].rearrange("p (h t) -> p h t", h=2), sin2, ALU.mult).then_inc(po_ksin, 1)
                    po.wait_ge(ve_qcos, n + 1)
                    po.wait_ge(ve_qsin, n + 1)
                    after(po, pe_a, n)
                    po.tensor_tensor(qr[:, :], qcos[:, :], qsin[:, :], ALU.add).then_inc(po_qr, 1)
                    po.wait_ge(ve_kcos, n + 1)
                    po.wait_ge(po_ksin, n + 1)
                    po.tensor_tensor(kr[:, :], kcos[:, :], ksin[:, :], ALU.add).then_inc(po_kr, 1)

                def inverse_root(u):
                    po.wait_ge(ve_ze, u + 1)
                    after(po, ve_og, u)
                    po.tensor_tensor(rstd[:, :], ze[:, :], con[:, C_HALF:C_HALF + 4], ALU.pow).then_inc(po_rstd, 1)

                def low_vg(p):
                    po.wait_ge(wv_hi, p + 1)
                    po.tensor_tensor(wl[:, :, 512:1024], wraw[:, 0:W_S].rearrange("p (k c) -> p k c", k=KT)[:, :, 512:1024],
                                     wh[:, :, 512:1024].bitcast(F32), ALU.subtract).then_inc(w_vg, 1)

                low_vg(0)
                po.wait_ge(ld_con, 16)
                rotate(0)

                def step(u, p, b):
                    if not is_first(u):
                        inverse_root(u - 1)
                    po.wait_ge(ve_mx, u + 1)
                    after(po, ac_exp, u)
                    po.tensor_tensor(okm[:, :].rearrange("p (g m) -> p g m", g=4), ok[:, :].rearrange("p (g m) -> p g m", g=4),
                                     mx[:, :].unsqueeze(2).broadcast_to([P, 4, M]), ALU.subtract).then_inc(po_okm, 1)
                    po.wait_ge(ac_exp, u + 1)
                    after(po, pe_qet, u)
                    po.tensor_tensor(qe[:, :, :], ee[:, :].rearrange("p (a m) -> p a m", a=TT),
                                     enz[:, :].rearrange("p (a m) -> p a m", a=TT), ALU.mult).then_inc(po_qe, 1)
                    if not is_last(u):
                        rotate(u + 1)
                    if b == 2 and has_next_pair(p):
                        low_vg(p + 1)

                    if not has_next_pair(p):
                        root(b - 1, var1, root1, t_var1, t_root1)
                    if b == 2 and not has_next_pair(p):
                        po.wait_ge(w1_hi, 1)
                        po.tensor_tensor(w1l[:, :, :], w1raw[:, :, :], w1h[:, :, :].bitcast(F32), ALU.subtract).then_inc(w1_ok, 1)

                def root(b, var, out_root, ready, done):
                    po.wait_ge(ready, b + 1)
                    po.tensor_tensor(out_root[:, b, :], var[:, b, :], con[:, C_HALF:C_HALF + TT], ALU.pow).then_inc(done, 1)

                over_main(po, step)
                inverse_root(UNITS - 1)
                root(0, var2, root2, t_var2, t_root2)
                root(3, var1, root1, t_var1, t_root1)
                for b in range(2):
                    root(b, var3, root3, t_var3, t_root3)
                    root(b + 1, var2, root2, t_var2, t_root2)
                root(3, var2, root2, t_var2, t_root2)
                root(2, var3, root3, t_var3, t_root3)
                root(3, var3, root3, t_var3, t_root3)


def _constants():
    inv_freq = (np.float32(1.0) / np.float32(10000.0) ** (np.arange(0, DK, 2, dtype=np.float32) / np.float32(DK))).astype(np.float32)
    ang = (inv_freq[:, None] * np.arange(T, dtype=np.float32)[None, :]).astype(np.float32).astype(np.float64)
    con = np.zeros((P, C_END), np.float32)
    con[:, C_COS:C_COS + T] = np.concatenate([np.cos(ang), np.cos(ang)], 0)
    con[:, C_SIN:C_SIN + T] = np.concatenate([-np.sin(ang), np.sin(ang)], 0)
    con[:, C_TRI:C_TRI + P] = np.triu(np.ones((P, P)))
    con[:, C_ID:C_ID + P] = np.eye(P)
    con[:, C_ONES:C_ONES + P] = 1.0
    con[R::32, C_ONECOL] = 1.0
    con[:, C_HALF:C_HALF + 8] = -0.5
    return con


def kernel(x, ctx_2048, mask_BxS2_bk0, L0_attn_Wq, L0_attn_Wk, L0_attn_Wv, L0_attn_Wg, L0_attn_Wo, L0_attn_Ws1,
           L0_attn_Ws2, L0_attn_bs2, L0_attn_g_norm_weight, L0_ffn_router_weight, L0_ffn_router_bias, L0_ffn_w1,
           L0_ffn_b1, L0_ffn_w2, L0_ffn_b2):
    import concourse.bacc as bacc
    from concourse.bass_utils import run_bass_kernel_spmd

    f32 = np.float32
    x, c = np.asarray(x), np.asarray(ctx_2048)

    def by_partition(a, tiles):
        return a.reshape(tiles, P, -1).transpose(1, 0, 2)

    w = [np.asarray(a).reshape(PAIRS, 2 * DK, KT, P).transpose(0, 3, 2, 1) for a in (L0_attn_Wq, L0_attn_Wk, L0_attn_Wv, L0_attn_Wg)]
    w = np.concatenate(w, 3).reshape(PAIRS, P, KT * 1024)
    stack = np.zeros((PAIRS, 4, 32, 2 * M), f32)
    stack[:, :, 0:R] = np.asarray(L0_attn_Ws2).reshape(PAIRS, 1, 2 * M, R).transpose(0, 1, 3, 2)
    stack[:, :, R] = np.asarray(L0_attn_bs2).reshape(PAIRS, 1, 2 * M)
    w_pairs = np.concatenate([w, stack.reshape(PAIRS, P, 2 * M)], 2)
    wo_pairs = np.asarray(L0_attn_Wo).T.reshape(PAIRS, 2, DK, D).transpose(0, 2, 1, 3)
    ws1 = np.zeros((P, KT, 4, 32), f32)
    ws1[:, :, :, 0:R] = np.asarray(L0_attn_Ws1).T.reshape(KT, P, 1, R).transpose(1, 0, 2, 3)
    vectors = np.zeros((P, V_END), f32)
    vectors[:, V_GN] = np.asarray(L0_attn_g_norm_weight)
    vectors[:, V_B1:V_B1 + FT] = np.asarray(L0_ffn_b1).reshape(FT, P).T
    vectors[:, V_RW:V_RW + D] = np.asarray(L0_ffn_router_weight)[None, :]
    vectors[:, V_RB] = np.asarray(L0_ffn_router_bias)[0]
    vectors[:, V_B2:V_B2 + D] = np.asarray(L0_ffn_b2)[None, :]
    arrays = {
        "x_tok": by_partition(x.reshape(B * T, D), B * TT),
        "x_feat": by_partition(x.reshape(B * T, D).T, KT),
        "w_pairs": w_pairs,
        "wo_pairs": wo_pairs,
        "ws1": ws1.reshape(P, KT, P),
        "consts": _constants(),
        "vectors": vectors,
        "ctx_feat": c.transpose(2, 0, 1).reshape(KT, P, B, S2).transpose(1, 2, 0, 3),
        "ctx_tok": c.reshape(B, MT, P, D).transpose(2, 0, 1, 3),
        "mask": np.ascontiguousarray(mask_BxS2_bk0).view(np.int32).reshape(1, B, S2 // 4),
        "w1": by_partition(np.asarray(L0_ffn_w1), KT),
        "w2": by_partition(np.asarray(L0_ffn_w2), FT),
    }
    arrays = {n: np.ascontiguousarray(a) for n, a in arrays.items()}
    nc = bacc.Bacc("TRN2", target_bir_lowering=False, num_devices=1)
    aps = [nc.dram_tensor(n, a.shape, mybir.dt.from_np(a.dtype), kind="ExternalInput").ap() for n, a in arrays.items()]
    out = nc.dram_tensor("out", (P, B, TT, D), F32, kind="ExternalOutput").ap()
    decoder_layer(nc, *aps, out)
    r = run_bass_kernel_spmd(nc, [arrays], core_ids=[0])
    return r.results[0]["out"].reshape(P, B * TT, D).transpose(1, 0, 2).reshape(B, T, D)
```

```python
import numpy as np
import concourse.bass as bass
from concourse import mybir
from contextlib import ExitStack

F32 = mybir.dt.float32
F32R = mybir.dt.float32r
U8 = mybir.dt.uint8
I32 = mybir.dt.int32
ALU = mybir.AluOpType
ACT = mybir.ActivationFunctionType
AX = mybir.AxisListType.X

B, T, D = 4, 256, 256
H, DK, M, R = 16, 128, 64, 16
S2 = 512
DFF = 1024
P = 128
KT = D // P
TT = T // P
PAIRS = H // 2
UNITS = PAIRS * B
MT = S2 // P
FT = DFF // P
CLAMP = 32.0
EPS = 1e-5
NEG = -1e30

C_COS, C_SIN, C_TRI, C_ID, C_ONECOL, C_HALF, C_END = 0, 256, 512, 896, 1024, 1025, 1033
V_GN, V_B1, V_RW, V_RB, V_B2, V_END = 0, 1, 9, 265, 266, 522
W_TILE = 8 * DK
W_Q, W_K, W_VG = slice(0, 2 * DK), slice(2 * DK, 4 * DK), slice(4 * DK, 8 * DK)
W_S, W_END = KT * W_TILE, KT * W_TILE + 2 * M


def decoder_layer(nc, x_tok, x_feat, w_pairs, wo_pairs, ws1, consts, vectors, ctx_feat, ctx_tok,
                  mask, w1, w2, out):
    ctx = ExitStack()
    with ctx:
        def sb(name, shape, dt=F32):
            return ctx.enter_context(nc.sbuf_tensor(name, shape, dt))

        def sem(name):
            return ctx.enter_context(nc.semaphore(name))

        con = sb("con", [P, C_END])
        vec = sb("vec", [P, V_END])
        cos = con[:, C_COS:C_COS + T]
        sin = con[:, C_SIN:C_SIN + T]
        tri = con[:, C_TRI:C_TRI + P]
        mask3 = con[:, C_TRI:C_TRI + 3 * P]
        ident = con[:, C_ID:C_ID + P]
        ones = con[:, C_TRI + P:C_TRI + 2 * P]
        acc = sb("acc", [P, B * TT, D])
        xh = sb("xh", [P, KT, B * T], F32R)
        xl = sb("xl", [P, KT, B * T], F32R)
        s1 = sb("s1", [P, B * T], F32R)
        wraw = sb("wraw", [P, W_END])
        wh = sb("wh", [P, KT, W_TILE], F32R)
        wl = sb("wl", [P, KT, W_TILE], F32R)
        ws2 = sb("ws2", [P, 2 * M], F32R)
        woraw = sb("woraw", [P, 2, D])
        wos = sb("wos", [P, 2, D])
        woh = sb("woh", [P, 2, D], F32R)
        wol = sb("wol", [P, 2, D], F32R)
        gn = sb("gn", [P, 1])
        rot = sb("rot", [P, 8 * 2 * T])
        swq, swk, qcos, kcos, qsin, ksin, qr, kr = (rot[:, n * 2 * T:(n + 1) * 2 * T] for n in range(8))
        val = sb("val", [P, 2, TT, 2 * DK])
        th = sb("th", [P, TT, 2 * DK])
        gate = sb("gate", [P, 2, TT, 2 * DK])
        sc = sb("sc", [P, 2 * T])
        es = sb("es", [P, 2, 2 * T])
        esh = sb("esh", [P, T], F32R)
        esl = sb("esl", [P, T], F32R)
        tri_r = sb("tri_r", [P, 2 * P], F32R)
        enz = sb("enz", [P, 2 * P])
        at = sb("at", [P, 2, 384])
        wt = sb("wt", [P, 2, 384])
        ok = sb("ok", [P, 2 * P])
        okm = sb("okm", [P, 2 * P])
        ee = sb("ee", [P, 2 * P])
        qe = sb("qe", [P, TT, P])
        qeT = sb("qeT", [P, T])
        mx = sb("mx", [P, 4])
        sume = sb("sume", [P, 4])
        sq = sb("sq", [P, 4, DK])
        ss = sb("ss", [P, 4])
        zs = sb("zs", [P, 4])
        ze = sb("ze", [P, 4])
        rstd = sb("rstd", [P, 4])
        og = sb("og", [P, 4, DK])
        ogh = sb("ogh", [P, 4, P], F32R)
        ogl = sb("ogl", [P, 4, P], F32R)
        ctxf = sb("ctxf", [P, B, KT, S2])
        ctxt = sb("ctxt", [P, B, MT, D])
        mrow = sb("mrow", [1, B, S2 // 4], I32)
        mneg = sb("mneg", [1, B, S2], F32R)
        mval = sb("mval", [1, B])
        valid = sb("valid", [P, B])
        one_r = sb("one_r", [1, P], F32R)
        w1raw = sb("w1raw", [P, KT, DFF])
        w1h, w1l = wh, wl
        halfrb = sb("halfrb", [P, 1])
        bn1, bn2, bn3 = (sb(n, [P, TT, 6]) for n in ("bn1", "bn2", "bn3"))
        st1, st2, st3 = (sb(n, [P, 5, TT]) for n in ("st1", "st2", "st3"))
        mean1, var1, root1 = (sb(n, [P, B, TT]) for n in ("mean1", "var1", "root1"))
        mean2, var2, root2 = (sb(n, [P, B, TT]) for n in ("mean2", "var2", "root2"))
        mean3, var3, root3 = (sb(n, [P, B, TT]) for n in ("mean3", "var3", "root3"))
        x1T = sb("x1T", [P, TT, KT, P])
        smax = sb("smax", [P, B, TT])
        nmax = sb("nmax", [P, B, TT])
        prob = sb("prob", [P, TT, S2])
        psums = sb("psums", [P, B, TT])
        pinv = sb("pinv", [P, B, TT])
        pval = sb("pval", [P, B, TT])
        probT = sb("probT", [P, TT, MT, P])
        rprod = sb("rprod", [P, TT, D])
        rz, rt, rw = (sb(n, [P, B, TT]) for n in ("rz", "rt", "rw"))
        hT = w1raw[:, :, :].rearrange("p k (f t) -> p (k f) t", t=T)
        hTh, hTl = (a[:, :, :].rearrange("p k (f t) -> p (k f) t", t=T) for a in (xh, xl))
        x2h, x2l = (s1[:, n * KT * T:(n + 1) * KT * T].rearrange("p (k t) -> p k t", t=T) for n in range(2))
        w2s = rot[:, 0:FT * D].rearrange("p (f d) -> p f d", d=D)
        w2h, w2l = sb("w2h", [P, FT, D], F32R), sb("w2l", [P, FT, D], F32R)

        ps = ctx.enter_context(nc.psum_tensor("ps", [P, 8, 512], F32))
        ps_q, ps_k, ps_c = ps[:, 0, :], ps[:, 1, :], ps[:, 1, 0:256]
        ps_vg, ps_o = ps[:, 2:4, :], ps[:, 2, :]
        ps_aw = ps[:, 4:6, 0:384]
        ps_s, ps_p, ps_qet = ps[:, 4, :], ps[:, 6, 0:256], ps[:, 6, 0:256]
        ps_ogt = ps[:, 7, :]

        ld_con, ld_vec, ld_xf, ld_xt, ld_ws1 = (sem("ld_" + n) for n in ("con", "vec", "xf", "xt", "ws1"))
        ld_w, ld_wo = sem("ld_w"), sem("ld_wo")
        ld_wq0, ld_wv0 = sem("ld_wq0"), sem("ld_wv0")
        ld_xr, ld_mask = sem("ld_xr"), sem("ld_mask")
        wq_hi, wk_hi, wv_hi, ws_hi, wo_scaled, wo_hi = (
            sem(n) for n in ("wq_hi", "wk_hi", "wv_hi", "ws_hi", "wo_scaled", "wo_hi"))
        w_q, w_k, w_vg, w_s, w_wo = (sem("w_" + n) for n in ("q", "k", "vg", "s", "wo"))
        gn_ok, x0_hi, x_hi, x_ok = sem("gn_ok"), sem("x0_hi"), sem("x_hi"), sem("x_ok")
        ws1_hi, ws1_ok, s1_mm, s1_full, s1_ok = (sem(n) for n in ("ws1_hi", "ws1_ok", "s1_mm", "s1_full", "s1_ok"))
        s1_cp, s1_last = sem("s1_cp"), sem("s1_last")
        pe_q, pe_k, pe_s, pe_vg, pe_c, pe_a, pe_p, pe_qet, pe_w2, pe_o, pe_ogt, pe_wo = (
            sem("pe_" + n) for n in ("q", "k", "s", "vg", "c", "a", "p", "qet", "w2", "o", "ogt", "wo"))
        ac_swq, ac_swk, ac_at, ac_ogh, ac_es, ac_exp, ac_val, ac_qet, ac_th, ac_sq = (
            sem("ac_" + n) for n in ("swq", "swk", "at", "ogh", "es", "exp", "val", "qet", "th", "sq"))
        ve_ss, ve_zs, ve_ze, ve_at, ve_og, ve_qcos, ve_kcos, ve_ok, ve_mx, ve_sc, ve_ogl, ve_qsin = (
            sem("ve_" + n) for n in ("ss", "zs", "ze", "at", "og", "qcos", "kcos", "ok", "mx", "sc", "ogl", "qsin"))
        ac_esh, ve_esl = sem("ac_esh"), sem("ve_esl")
        ve_sum, ve_gate, ve_enz, ve_wt, ve_acc = (sem("ve_" + n) for n in ("sum", "gate", "enz", "wt", "acc"))
        po_rstd, po_okm, po_qe, po_ksin, po_qr, po_kr = (
            sem("po_" + n) for n in ("rstd", "okm", "qe", "ksin", "qr", "kr"))
        ld_tail, ld_w2 = sem("ld_tail"), sem("ld_w2")
        stored = sem("stored")
        w1_hi, w1_ok, mask_ok, mval_ok, pe_valid, valid_ok = (
            sem(n) for n in ("w1_hi", "w1_ok", "mask_ok", "mval_ok", "pe_valid", "valid_ok"))
        t_bn1, t_st1, t_mean1, t_var1, t_root1, t_x1, t_x1T, t_x1Ts = (
            sem("t_" + n) for n in ("bn1", "st1", "mean1", "var1", "root1", "x1", "x1T", "x1Ts"))
        t_sc, t_max, t_nmax, t_prob = (sem("t_" + n) for n in ("sc", "max", "nmax", "prob"))
        t_pT, t_pTs = sem("t_pT"), (sem("t_pTs0"), sem("t_pTs1"))
        t_pinv, t_pval, t_r, t_x2p, t_bn2, t_st2, t_mean2, t_var2, t_root2, t_x2 = (
            sem("t_" + n) for n in ("pinv", "pval", "r", "x2p", "bn2", "st2", "mean2", "var2", "root2", "x2"))
        t_x2T, t_x2h, t_x2l, t_rprod, t_rz, t_rt, t_rw = (sem("t_" + n) for n in ("x2T", "x2h", "x2l", "rprod", "rz", "rt", "rw"))
        t_h, t_gelu = sem("t_h"), sem("t_gelu")
        t_hh = sem("t_hh")
        t_hl = [sem(f"t_hl{j}") for j in range(FT // 2)]
        w2_hi, w2_ok = sem("w2_hi"), sem("w2_ok")
        t_y, t_yb, t_x3, t_bn3, t_st3, t_mean3, t_var3, t_root3, t_out = (
            sem("t_" + n) for n in ("y", "yb", "x3", "bn3", "st3", "mean3", "var3", "root3", "out"))

        ws1_raw = sc[:, 0:256].rearrange("p (k c) -> p k c", k=KT)
        ws1h, ws1l = ogh[:, 0:2, :], ogl[:, 0:2, :]
        raw_tiles = wraw[:, 0:W_S].rearrange("p (k c) -> p k c", k=KT)
        xraw = ctxf[:, 0:2, :, :].rearrange("p b k s -> p (b k s)").rearrange("p (k t) -> p k t", k=KT)
        s1_raw = ctxt[:, 0, :, :].rearrange("p m d -> p (m d)")

        S1_CHUNKS = ((6, slice(0, T)), (6, slice(T, 2 * T)), (7, slice(2 * T, 4 * T)))

        def after(eng, semaphore, count):
            if not isinstance(count, int) or count > 0:
                eng.wait_ge(semaphore, count)

        def over_main(eng, step):
            step(0, 0, 0)
            with eng.Fori(0, PAIRS - 1) as i:
                for b in range(1, B):
                    step(4 * i + b, i, b)
                step(4 * i + 4, i + 1, 0)
            for b in range(1, B):
                step(4 * (PAIRS - 1) + b, PAIRS - 1, b)

        SCORE_BANK, TURN_BANK, H_BANK = (1, 0), (1, 4), (3, 7, 2, 6)
        OUT_PARTS = [(b, slice(0, TT)) for b in range(B - 1)] + [(B - 1, slice(tt, tt + 1)) for tt in range(TT)]

        def is_last(u):
            return isinstance(u, int) and u == UNITS - 1

        def is_first(u):
            return isinstance(u, int) and u == 0

        def y_bank(u):
            return 4 if is_last(u) else 3 if isinstance(u, int) and u == UNITS - 2 else 0

        def has_next_pair(p):
            return not (isinstance(p, int) and p == PAIRS - 1)

        with nc.Block() as block:

            @block.sync
            def _(sp):
                by_tile = w_pairs[0][:, 0:W_S].rearrange("p (k c) -> p k c", k=KT)
                sp.dma_start(xraw[:, :, 0:T], x_feat[:, :, 0:T]).then_inc(ld_xf, 16)
                sp.dma_start(raw_tiles[:, :, W_Q], by_tile[:, :, W_Q]).then_inc(ld_wq0, 16)
                sp.dma_start(raw_tiles[:, :, W_K], by_tile[:, :, W_K]).then_inc(ld_w, 16)
                sp.dma_start(ws1_raw, ws1).then_inc(ld_ws1, 16)
                sp.dma_start(raw_tiles[:, :, W_VG], by_tile[:, :, W_VG]).then_inc(ld_wv0, 16)
                sp.dma_start(wraw[:, W_S:W_END], w_pairs[0][:, W_S:W_END]).then_inc(ld_wv0, 16)
                sp.dma_start(mrow[:, :, :], mask).then_inc(ld_mask, 16)
                sp.dma_start(con[:, :], consts).then_inc(ld_con, 16)
                sp.dma_start(xraw[:, :, T:B * T], x_feat[:, :, T:B * T]).then_inc(ld_xr, 16)
                sp.dma_start(vec[:, :], vectors).then_inc(ld_vec, 16)
                sp.dma_start(woraw[:, :, :], wo_pairs[0]).then_inc(ld_wo, 16)
                sp.dma_start(acc[:, :, :], x_tok).then_inc(ld_xt, 16)
                sp.wait_ge(x_ok, 2)
                sp.wait_ge(s1_ok, 4)
                sp.wait_ge(s1_last, 2)
                sp.dma_start(ctxf[:, :, :, :], ctx_feat).then_inc(ld_tail, 16)
                sp.dma_start(ctxt[:, :, :, :], ctx_tok).then_inc(ld_tail, 16)
                sp.dma_start(w1raw[:, :, :], w1).then_inc(ld_tail, 16)
                with sp.Fori(1, PAIRS) as i:
                    sp.wait_ge(w_q, i)
                    sp.wait_ge(w_k, i)
                    sp.wait_ge(w_vg, i)
                    sp.wait_ge(w_s, i)
                    sp.dma_start(wraw[:, :], w_pairs[bass.ds(i, 1)].rearrange("a p c -> (a p) c")).then_inc(ld_w, 16)
                    sp.wait_ge(w_wo, i)
                    sp.dma_start(woraw[:, :, :], wo_pairs[bass.ds(i, 1)].rearrange("a p h d -> (a p) h d")).then_inc(ld_wo, 16)
                sp.wait_ge(pe_a, 2 * UNITS)
                sp.dma_start(w2s, w2).then_inc(ld_w2, 16)
                for n, (b, tiles) in enumerate(OUT_PARTS):
                    sp.wait_ge(t_out, n + 1)
                    sp.dma_start(out[:, b, tiles, :], acc[:, b * TT:(b + 1) * TT, :][:, tiles, :]).then_inc(stored, 16)
                sp.wait_ge(stored, 16 * len(OUT_PARTS))

            @block.tensor
            def _(pe):
                def passes(o, pairs, first=True, last=True):
                    ops = [x for (ah, al, bh, bl) in pairs for x in ((ah, bh), (ah, bl), (al, bh))]
                    for n, (a, b) in enumerate(ops):
                        mm = pe.matmul(o, a, b, start=first and n == 0, stop=last and n == len(ops) - 1)
                    return mm

                def project_qk(n, p, b):
                    after(pe, ve_qcos, n)
                    after(pe, ac_swq, n)
                    after(pe, ve_acc, n - 2)
                    if b == 0:
                        pe.wait_ge(w_q, p + 1)
                    cols = slice(b * T, (b + 1) * T)
                    for m in range(4):
                        if m == 2:
                            if b == 0:
                                pe.wait_ge(w_k, p + 1)
                            after(pe, ve_kcos, n)
                            after(pe, ac_swk, n)
                            after(pe, ve_enz, n)
                        o = (ps_q if m < 2 else ps_k)[:, (m % 2) * T:(m % 2 + 1) * T]
                        f = slice(m * P, (m + 1) * P)
                        mm = passes(o, [(wh[:, k, f], wl[:, k, f], xh[:, k, cols], xl[:, k, cols]) for k in range(KT)])
                        if m == 1:
                            mm.then_inc(pe_q, 1)
                    mm.then_inc(pe_k, 1)

                def project_vg(n, p, b):
                    after(pe, ac_val, TT * n)
                    after(pe, ac_th, TT * n)
                    after(pe, ve_gate, n)
                    after(pe, ve_og, n - 1)
                    after(pe, ac_sq, n - 1)
                    if b == 0:
                        pe.wait_ge(w_vg, p + 1)
                    for tt in range(TT):
                        t = slice((b * TT + tt) * P, (b * TT + tt + 1) * P)
                        passes(ps_vg[:, tt, :], [(xh[:, k, t], xl[:, k, t], wh[:, k, W_VG], wl[:, k, W_VG]) for k in range(KT)]).then_inc(pe_vg, 1)

                def slots(n, p, b):
                    after(pe, ve_sc, n)
                    if b == 0:
                        pe.wait_ge(w_s, p + 1)
                    for tt in range(TT):
                        t = slice((b * TT + tt) * P, (b * TT + tt + 1) * P)
                        pe.matmul(ps_s[:, tt * P:(tt + 1) * P], s1[:, t], ws2[:, :], start=True, stop=True)
                    mm = pe.matmul(ps_s[:, T:2 * T], ws2[:, :], s1[:, b * T:(b + 1) * T], start=True, stop=True)
                    mm.then_inc(pe_s, 1)

                def slot_sums_high(n):
                    pe.wait_ge(ve_kcos, n + 1)
                    pe.wait_ge(ac_swk, n + 1)
                    pe.wait_ge(ac_esh, n + 1)
                    pe.matmul(ps_c, tri_r[:, 0:P], esh[:, :], start=True, stop=False)
                    pe.matmul(ps_c[:, P:2 * P], tri_r[:, P:2 * P], esh[:, 0:P], start=False, stop=False)

                def slot_sums_low(n):
                    pe.wait_ge(ve_esl, n + 1)
                    c1 = ps_c[:, P:2 * P]
                    pe.matmul(c1, tri_r[:, P:2 * P], esl[:, 0:P], start=False, stop=False)
                    pe.matmul(ps_c, tri_r[:, 0:P], esl[:, :], start=False, stop=True).then_inc(pe_c, 1)

                def scores(u):
                    after(pe, ve_wt, 2 * u)
                    pe.wait_ge(po_qr, u + 1)
                    pe.wait_ge(po_kr, u + 1)
                    for h in range(2):
                        a = h * T
                        pe.matmul(ps_aw[:, h, 0:T], kr[:, a:a + P], qr[:, a:a + T], start=True, stop=True)
                        pe.matmul(ps_aw[:, h, T:T + P], kr[:, a + P:a + T], qr[:, a + P:a + T], start=True, stop=True).then_inc(pe_a, 1)

                def slot_scores(u, b):
                    after(pe, ac_qet, u)
                    pe.wait_ge(ve_at, 2 * u + 2)
                    for h in range(2):
                        m = slice(h * M, (h + 1) * M)
                        pe.matmul(ps_p[:, h * M:(h + 1) * M], at[:, h, 0:P], es[:, b % 2, m], start=True, stop=True)
                        pe.matmul(ps_p[:, (2 + h) * M:(3 + h) * M], at[:, h, P:T], es[:, b % 2, m], start=True, stop=False)
                        mm = pe.matmul(ps_p[:, (2 + h) * M:(3 + h) * M], at[:, h, T:T + P], es[:, b % 2, P + h * M:P + (h + 1) * M], start=False, stop=True)
                    mm.then_inc(pe_p, 1)

                def turn_probs(u):
                    pe.wait_ge(po_qe, u + 1)
                    for tt in range(TT):
                        mm = pe.transpose(ps_qet[:, tt * P:(tt + 1) * P], qe[:, tt, :], ident)
                    mm.then_inc(pe_qet, 1)

                def token_weights(u, b):
                    if not is_last(u):
                        pe.wait_ge(ve_sc, u + 2)
                    pe.wait_ge(ac_qet, u + 1)
                    for h in range(2):
                        m = slice(h * M, (h + 1) * M)
                        e = es[m, b % 2, T:2 * T]
                        pe.matmul(ps_aw[:, h, 0:T], e[:, 0:P], qeT[m, 0:T], start=True, stop=True)
                        pe.matmul(ps_aw[:, h, T:T + P], e[:, P:T], qeT[m, P:T], start=True, stop=True).then_inc(pe_w2, 1)

                def outputs(u, b):
                    if not is_last(u):
                        pe.wait_ge(ac_val, TT * (u + 2))
                        pe.wait_ge(ac_th, TT * (u + 2))
                        pe.wait_ge(ve_gate, u + 2)
                    for h in range(2):
                        pe.wait_ge(ve_wt, 2 * u + h + 1)
                        d = slice(h * DK, (h + 1) * DK)
                        v = val[:, b % 2, :, d]
                        pe.matmul(ps_o[:, h * P:(h + 1) * P], wt[:, h, 0:P], v[:, 0, :], start=True, stop=True)
                        pe.matmul(ps_o[:, (2 + h) * P:(3 + h) * P], wt[:, h, P:T], v[:, 0, :], start=True, stop=False)
                        mm = pe.matmul(ps_o[:, (2 + h) * P:(3 + h) * P], wt[:, h, T:T + P], v[:, 1, :], start=False, stop=True)
                    mm.then_inc(pe_o, 1)

                def turn_outputs(u):
                    pe.wait_ge(ve_og, u + 1)
                    after(pe, ac_ogh, u)
                    after(pe, ve_ogl, u)
                    for g in range(4):
                        mm = pe.transpose(ps_ogt[:, g * P:(g + 1) * P], og[:, g, :], ident)
                    mm.then_inc(pe_ogt, 1)

                def project_out(u, p, b, tiles=range(TT)):
                    if tiles[0] == 0:
                        if b == 0:
                            pe.wait_ge(w_wo, p + 1)
                        if is_last(u):
                            pe.wait_ge(ve_wt, 2 * UNITS)
                        elif y_bank(u) == 3:
                            pe.wait_ge(ac_val, TT * UNITS)
                            pe.wait_ge(ac_th, TT * UNITS)
                            pe.wait_ge(ve_gate, UNITS)
                        else:
                            pe.wait_ge(ve_qcos, u + 3)
                            pe.wait_ge(ac_swq, u + 3)
                        pe.wait_ge(ac_ogh, u + 1)
                        pe.wait_ge(ve_ogl, u + 1)
                    for tt in tiles:
                        mm = passes(ps[:, y_bank(u), tt * D:(tt + 1) * D], [(ogh[:, 2 * tt + h, :], ogl[:, 2 * tt + h, :], woh[:, h, :], wol[:, h, :]) for h in range(2)])
                    if tiles[-1] == TT - 1:
                        mm.then_inc(pe_wo, 1)

                def slot_inner(c):
                    bank, t = S1_CHUNKS[c]
                    passes(ps[:, bank, 0:t.stop - t.start], [(ws1h[:, k, :], ws1l[:, k, :], xh[:, k, t], xl[:, k, t]) for k in range(KT)]).then_inc(s1_mm, 1)

                pe.wait_ge(x_ok, 1)
                project_qk(0, 0, 0)
                pe.wait_ge(ws1_ok, 1)
                slot_inner(0)
                pe.wait_ge(ld_con, 16)
                pe.wait_ge(mval_ok, 1)
                pe.matmul(ps[:, 7, 0:B], ones[0:1, :], mval[:, :], start=True, stop=True).then_inc(pe_valid, 1)
                project_vg(0, 0, 0)
                pe.wait_ge(s1_ok, 2)
                slots(0, 0, 0)
                pe.wait_ge(x_ok, 2)
                pe.wait_ge(s1_full, 1)
                slot_inner(1)
                pe.wait_ge(valid_ok, 1)
                slot_inner(2)
                slot_sums_high(0)
                slot_sums_low(0)

                def turn_x1(b):
                    pe.wait_ge(t_x1, b + 1)
                    if b == 0:
                        pe.wait_ge(ve_qcos, UNITS)
                        pe.wait_ge(ac_swq, UNITS)
                        pe.wait_ge(ve_acc, UNITS - 2)
                    else:
                        pe.wait_ge(t_prob, TT * b)
                    for tt in range(TT):
                        for k in range(KT):
                            mm = pe.transpose(ps[:, 0, (tt * KT + k) * P:(tt * KT + k + 1) * P], acc[:, b * TT + tt, k * P:(k + 1) * P], ident)
                    mm.then_inc(t_x1T, 1)

                def memory_scores(b, tt):
                    pe.wait_ge(t_x1Ts, b + 1)
                    if b == 0 and tt == 0:
                        pe.wait_ge(ve_enz, UNITS)
                        pe.wait_ge(mask_ok, 1)
                    if b > 0:
                        pe.wait_ge(t_prob, TT * b)
                        pe.wait_ge(t_pTs[0], b)
                    o = ps[:, SCORE_BANK[tt], :]
                    pe.matmul(o, one_r[:, :], mneg[:, b, :], start=True, stop=False)
                    for k in range(KT):
                        mm = pe.matmul(o, x1T[:, tt, k, :], ctxf[:, b, k, :], start=False, stop=(k == KT - 1))
                    mm.then_inc(t_sc, 1)

                def turn_memory(b, tiles=range(TT)):
                    for tt in tiles:
                        if b == 0 and tt == 1:
                            pe.wait_ge(ve_wt, 2 * UNITS)
                        if b == 1 and tt == 1:
                            pe.wait_ge(ve_acc, UNITS)
                        if b > 1 and tt == 1:
                            pe.wait_ge(t_x3, b - 1)
                        pe.wait_ge(t_prob, TT * b + tt + 1)
                        for m in range(MT):
                            mm = pe.transpose(ps[:, TURN_BANK[tt], m * P:(m + 1) * P], prob[:, tt, m * P:(m + 1) * P], ident)
                        mm.then_inc(t_pT, 1)

                def readout(b):
                    for tt in range(TT):
                        pe.wait_ge(t_pTs[tt], b + 1)
                        if tt == 0:
                            after(pe, t_x2p, b)
                        for m in range(MT):
                            mm = pe.matmul(ps[:, 5, tt * D:(tt + 1) * D], probT[:, tt, m, :], ctxt[:, b, m, :], start=(m == 0), stop=(m == MT - 1))
                    mm.then_inc(t_r, 1)

                def turn_x2(b):
                    pe.wait_ge(t_x2, b + 1)
                    for k in range(KT):
                        for tt in range(TT):
                            mm = pe.transpose(ps[:, 6, (k * TT + tt) * P:(k * TT + tt + 1) * P], acc[:, b * TT + tt, k * P:(k + 1) * P], ident)
                    mm.then_inc(t_x2T, 1)

                def hidden(b, tiles=range(FT)):
                    pe.wait_ge(t_x2l, b + 1)
                    if b == 0 and tiles[0] == 0:
                        pe.wait_ge(ve_acc, UNITS - 1)
                        pe.wait_ge(w1_ok, 2)
                        pe.wait_ge(ve_og, UNITS)
                        pe.wait_ge(ve_ogl, UNITS)
                    for f in tiles:
                        c = slice(f * P, (f + 1) * P)
                        mm = passes(ps[:, H_BANK[f // 2], (f % 2) * T:(f % 2 + 1) * T],
                               [(w1h[:, k, c], w1l[:, k, c], x2h[:, k, :], x2l[:, k, :]) for k in range(KT)])
                        if f % 2 == 1:
                            mm.then_inc(t_h, 1)

                def down(b, tt, tiles=range(FT)):
                    bank = 5 if b == B - 1 and tt == 0 else 4
                    if bank == 5:
                        pe.wait_ge(t_x2p, B)
                    elif b == B - 1:
                        pe.wait_ge(t_x3, B - 1)
                    if b == 0 and tt == 0:
                        pe.wait_ge(w2_ok, 2)
                    t = slice(tt * P, (tt + 1) * P)
                    for f in tiles:
                        pe.wait_ge(t_hl[f // 2], b + 1)
                        mm = passes(ps[:, bank, tt * D:(tt + 1) * D], [(hTh[:, f, t], hTl[:, f, t], w2h[:, f, :], w2l[:, f, :])],
                                    first=(f == 0), last=(f == FT - 1))
                    if tiles[-1] == FT - 1 and (tt == TT - 1 or b == B - 1):
                        mm.then_inc(t_y, 1)

                def step(u, p, b):
                    nb = (b + 1) % B
                    np_ = p + 1 if b == B - 1 and has_next_pair(p) else p
                    scores(u)
                    if is_last(u):
                        memory_scores(0, 0)
                    else:
                        project_qk(u + 1, np_, nb)
                    if is_first(u):
                        pe.wait_ge(s1_full, 2)
                    slot_scores(u, b)
                    if not is_first(u):
                        turn_outputs(u - 1)
                    if is_last(u):
                        memory_scores(0, 1)
                    else:
                        if is_first(u):
                            pe.wait_ge(s1_ok, 4)
                        slots(u + 1, np_, nb)
                        project_vg(u + 1, np_, nb)
                    if is_last(u):
                        project_out(u - 1, p, b - 1, [0])
                        turn_probs(u)
                        project_out(u - 1, p, b - 1, [1])
                        token_weights(u, b)
                    else:
                        turn_probs(u)
                        if not is_first(u):
                            project_out(u - 1, p - 1 if b == 0 else p, (b - 1) % B, [0])
                        slot_sums_high(u + 1)
                        token_weights(u, b)
                        slot_sums_low(u + 1)
                        if not is_first(u):
                            project_out(u - 1, p - 1 if b == 0 else p, (b - 1) % B, [1])
                    if is_first(u):
                        pe.wait_ge(s1_last, 2)
                    outputs(u, b)
                    if b == 2 and not has_next_pair(p):
                        turn_x1(0)

                over_main(pe, step)
                turn_memory(0)
                turn_x1(1)
                readout(0)
                turn_outputs(UNITS - 1)
                memory_scores(1, 0)
                memory_scores(1, 1)
                turn_x2(0)
                project_out(UNITS - 1, PAIRS - 1, B - 1)
                for b in range(B - 1):
                    hidden(b, range(FT - 2))
                    turn_memory(b + 1, [0])
                    hidden(b, range(FT - 2, FT))
                    turn_memory(b + 1, [1])
                    if b + 2 < B:
                        turn_x1(b + 2)
                    readout(b + 1)
                    down(b, 0)
                    if b + 2 < B:
                        down(b, 1)
                        turn_x2(b + 1)
                        memory_scores(b + 2, 0)
                        memory_scores(b + 2, 1)
                    else:
                        down(b, 1, range(FT // 2))
                        turn_x2(b + 1)
                        down(b, 1, range(FT // 2, FT))
                hidden(B - 1)
                for f in (range(FT // 2), range(FT // 2, FT)):
                    down(B - 1, 0, f)
                    down(B - 1, 1, f)

            @block.scalar
            def _(act):
                def copy(o, i):
                    return act.activation(o, i, ACT.Copy)

                def swap(n, src, dst, done, ready, used):
                    act.wait_ge(ready, n + 1)
                    after(act, used, n)
                    copy(dst[0:64, :], src[64:128, :])
                    copy(dst[64:128, :], src[0:64, :]).then_inc(done, 1)

                def exp_slots(n, b):
                    act.wait_ge(ve_sc, n + 1)
                    after(act, pe_w2, 2 * (n - 1))
                    act.activation(es[:, b % 2, :], sc[:, :], ACT.Exp).then_inc(ac_es, 1)
                    after(act, pe_c, n)
                    act.wait_ge(ac_es, n + 1)
                    copy(esh[:, :], es[:, b % 2, 0:T]).then_inc(ac_esh, 1)

                def values(n, b, tt):
                    if tt == 0:
                        after(act, pe_o, n - 1)
                    act.wait_ge(pe_vg, TT * n + tt + 1)
                    copy(val[:, b % 2, tt, :], ps_vg[:, tt, 0:256]).then_inc(ac_val, 1)

                def gate_tanh(n, tt):
                    if tt == 0:
                        after(act, ve_gate, n)
                    act.activation(th[:, tt, :], ps_vg[:, tt, 256:512], ACT.Tanh, scale=0.5).then_inc(ac_th, 1)

                def off_diagonal(u):
                    after(act, pe_p, u)
                    for h in range(2):
                        act.wait_ge(pe_a, 2 * u + h + 1)
                        copy(at[:, h, P:T], ps_aw[:, h, P:T]).then_inc(ac_at, 1)

                def square(u):
                    act.wait_ge(pe_o, u + 1)
                    after(act, ve_ss, u)
                    act.activation(sq[:, :, :], ps_o.rearrange("p (a d) -> p a d", a=4), ACT.Square).then_inc(ac_sq, 1)

                def outputs_turned(u):
                    act.wait_ge(pe_ogt, u + 1)
                    after(act, pe_wo, u)
                    copy(ogh[:, :, :], ps_ogt.rearrange("p (a d) -> p a d", a=4)).then_inc(ac_ogh, 1)

                def split_q(p):
                    act.wait_ge(ld_w, 16 * p + 16)
                    after(act, pe_q, 4 * p)
                    copy(wh[:, :, W_Q], raw_tiles[:, :, W_Q]).then_inc(wq_hi, 1)

                def split_k(p):
                    act.wait_ge(ld_w, 16 * p + 16)
                    after(act, pe_k, 4 * p)
                    copy(wh[:, :, W_K], raw_tiles[:, :, W_K]).then_inc(wk_hi, 1)

                def split_vg(p):
                    after(act, pe_vg, TT * B * p)
                    copy(wh[:, :, W_VG], raw_tiles[:, :, W_VG]).then_inc(wv_hi, 1)
                    after(act, pe_s, 4 * p)
                    copy(ws2[:, :], wraw[:, W_S:W_END]).then_inc(ws_hi, 1)

                def split_wo(p):
                    act.wait_ge(ld_wo, 16 * p + 16)
                    after(act, pe_wo, 4 * p)
                    act.activation(wos[:, :, :], woraw[:, :, :], ACT.Copy, scale=gn[:, 0:1]).then_inc(wo_scaled, 1)
                    act.wait_ge(wo_scaled, p + 1)
                    copy(woh[:, :, :], wos[:, :, :]).then_inc(wo_hi, 1)

                def inner_full(c):
                    bank, t = S1_CHUNKS[c]
                    act.wait_ge(s1_mm, c + 1)
                    act.activation(s1_raw[:, t], ps[:, bank, 0:t.stop - t.start], ACT.Identity,
                                   bias=con[:, C_ONECOL:C_ONECOL + 1]).then_inc(s1_full, 1)

                act.wait_ge(ld_wq0, 16)
                copy(wh[:, :, W_Q], raw_tiles[:, :, W_Q]).then_inc(wq_hi, 1)
                split_k(0)
                act.wait_ge(ld_ws1, 16)
                copy(ws1h, ws1_raw).then_inc(ws1_hi, 1)
                act.wait_ge(ld_wv0, 32)
                split_vg(0)
                swap(0, ps_q, swq, ac_swq, pe_q, ve_qsin)
                act.wait_ge(ld_xr, 16)
                copy(xh[:, :, T:B * T], xraw[:, :, T:B * T]).then_inc(x_hi, 1)
                act.wait_ge(ld_con, 16)
                inner_full(0)
                act.wait_ge(s1_full, 1)
                copy(s1[:, 0:T], s1_raw[:, 0:T]).then_inc(s1_cp, 1)
                swap(0, ps_k, swk, ac_swk, ve_kcos, po_ksin)
                values(0, 0, 0)
                gate_tanh(0, 0)
                exp_slots(0, 0)
                values(0, 0, 1)
                gate_tanh(0, 1)
                inner_full(1)
                inner_full(2)

                def exp_memory(b, tt):
                    act.wait_ge(t_nmax, TT * b + tt + 1)
                    if b > 0:
                        act.wait_ge(t_pT, TT * (b - 1) + tt + 1)
                    act.activation(prob[:, tt, :], ps[:, SCORE_BANK[tt], :], ACT.Exp, bias=nmax[:, b, tt:tt + 1],
                                   scale=float(D) ** -0.5, accum_out=psums[:, b, tt:tt + 1]).then_inc(t_prob, 1)

                def memory_turned(b):
                    act.wait_ge(t_pT, TT * b + 2)
                    after(act, t_r, b)
                    copy(probT[:, 1, :, :], ps[:, TURN_BANK[1], :].rearrange("p (m t) -> p m t", m=MT)).then_inc(t_pTs[1], 1)

                def x2_turned(b):
                    act.wait_ge(t_x2T, b + 1)
                    if b == 0:
                        act.wait_ge(pe_s, UNITS)
                    after(act, t_h, FT // 2 * b)
                    copy(x2h, ps[:, 6, :].rearrange("p (k t) -> p k t", k=KT)).then_inc(t_x2h, 1)

                def gelu(b):
                    for f in range(FT):
                        if b == B - 1 and f % 2 == 0 and f > 0:
                            high_h(b, f // 2 - 1)
                        act.wait_ge(t_h, (FT * b + f) // 2 + 1)
                        if f == 0:
                            for j in range(FT // 2):
                                after(act, t_hl[j], b)
                        act.activation(hT[:, f, :], ps[:, H_BANK[f // 2], (f % 2) * T:(f % 2 + 1) * T], ACT.Gelu_apprx_tanh,
                                       bias=vec[:, V_B1 + f:V_B1 + f + 1]).then_inc(t_gelu, 1)

                def high_h(b, j):
                    act.wait_ge(t_gelu, FT * b + 2 * j + 2)
                    if j == 0:
                        after(act, t_y, b)
                        act.wait_ge(pe_vg, TT * UNITS)
                    copy(hTh[:, 2 * j:2 * j + 2, :], hT[:, 2 * j:2 * j + 2, :]).then_inc(t_hh, 1)

                def router(b):
                    act.wait_ge(t_rz, b + 1)
                    act.activation(rt[:, b, :], rz[:, b, :], ACT.Tanh, bias=halfrb[:, 0:1], scale=0.5).then_inc(t_rt, 1)

                def step(u, p, b):
                    nb = (b + 1) % B
                    if not is_first(u):
                        square(u - 1)
                    off_diagonal(u)
                    if is_first(u):
                        act.wait_ge(s1_full, 3)
                        copy(s1[:, T:B * T], s1_raw[:, T:B * T]).then_inc(s1_cp, 1)
                    if not is_last(u):
                        swap(u + 1, ps_q, swq, ac_swq, pe_q, ve_qsin)
                        if b == 2 and has_next_pair(p):
                            split_q(p + 1)
                            split_k(p + 1)
                        swap(u + 1, ps_k, swk, ac_swk, ve_kcos, po_ksin)
                    if not is_first(u):
                        outputs_turned(u - 1)
                    act.wait_ge(po_okm, u + 1)
                    after(act, po_qe, u)
                    after(act, ve_sum, u)
                    act.activation(ee[:, :], okm[:, :], ACT.Exp, scale=float(DK) ** -0.5).then_inc(ac_exp, 1)
                    if not is_last(u):
                        exp_slots(u + 1, nb)
                        values(u + 1, nb, 0)
                    act.wait_ge(pe_qet, u + 1)
                    after(act, pe_w2, 2 * u)
                    copy(qeT[:, :], ps_qet).then_inc(ac_qet, 1)
                    if is_last(u):
                        exp_memory(0, 0)
                        exp_memory(0, 1)
                    else:
                        gate_tanh(u + 1, 0)
                        values(u + 1, nb, 1)
                        gate_tanh(u + 1, 1)
                    if b == 2 and has_next_pair(p):
                        split_vg(p + 1)
                    if b == 0:
                        if is_first(u):
                            act.wait_ge(gn_ok, 1)
                        split_wo(p)
                    if b == 2 and not has_next_pair(p):
                        act.wait_ge(ld_tail, 48)
                        act.wait_ge(pe_k, UNITS)
                        copy(w1h[:, :, 0:512], w1raw[:, :, 0:512]).then_inc(w1_hi, 1)
                        act.wait_ge(pe_vg, TT * UNITS)
                        copy(w1h[:, :, 512:1024], w1raw[:, :, 512:1024]).then_inc(w1_hi, 1)

                over_main(act, step)
                square(UNITS - 1)
                memory_turned(0)
                act.wait_ge(ld_w2, 16)
                for half in range(2):
                    f = slice(half * FT // 2, (half + 1) * FT // 2)
                    copy(w2h[:, f, :], w2s[:, f, :]).then_inc(w2_hi, 1)
                outputs_turned(UNITS - 1)
                x2_turned(0)
                exp_memory(1, 0)
                exp_memory(1, 1)
                for b in range(B - 1):
                    gelu(b)
                    memory_turned(b + 1)
                    for j in range(FT // 2):
                        high_h(b, j)
                    router(b)
                    x2_turned(b + 1)
                    if b + 2 < B:
                        exp_memory(b + 2, 0)
                        exp_memory(b + 2, 1)
                router(B - 1)
                gelu(B - 1)
                high_h(B - 1, FT // 2 - 1)

            @block.vector
            def _(ve):
                tri2 = tri.unsqueeze(1).broadcast_to([P, 2, P])
                cos2 = cos.unsqueeze(1).broadcast_to([P, 2, T])
                sin2 = sin.unsqueeze(1).broadcast_to([P, 2, T])

                def heads(a):
                    return a.rearrange("p (h t) -> p h t", h=2)

                def groups(a, n=4):
                    return a.rearrange("p (g m) -> p g m", g=n)

                def diag(a):
                    return a.rearrange("p (c t) -> p c t", c=3)[:, 0:3:2, :]

                def times_cos(n, src, dst, ready, used, done):
                    ve.wait_ge(ready, n + 1)
                    after(ve, used, n)
                    ve.tensor_tensor(heads(dst[:, :]), heads(src), cos2, ALU.mult).then_inc(done, 1)

                def q_times_sin(n):
                    ve.wait_ge(ac_swq, n + 1)
                    after(ve, po_qr, n)
                    ve.tensor_tensor(heads(qsin[:, :]), heads(swq[:, :]), sin2, ALU.mult).then_inc(ve_qsin, 1)

                def causal_scores(u):
                    after(ve, pe_p, u)
                    for h in range(2):
                        ve.wait_ge(ac_at, 2 * u + h + 1)
                        ve.tensor_tensor(diag(at[:, h, :]), diag(ps_aw[:, h, :]), tri2, ALU.mult).then_inc(ve_at, 1)

                def causal_weights(u):
                    after(ve, pe_o, u)
                    for h in range(2):
                        ve.wait_ge(pe_w2, 2 * u + h + 1)
                        ve.tensor_tensor(wt[:, h, :], ps_aw[:, h, 0:3 * P], mask3, ALU.mult).then_inc(ve_wt, 1)

                def clip(n):
                    ve.wait_ge(pe_s, n + 1)
                    after(ve, ac_es, n)
                    ve.tensor_scalar(sc[:, :], ps_s, CLAMP, -CLAMP, ALU.min, ALU.max).then_inc(ve_sc, 1)

                def low_es(n, b):
                    ve.wait_ge(ac_esh, n + 1)
                    after(ve, pe_c, n)
                    ve.tensor_tensor(esl[:, :], es[:, b % 2, 0:T], esh[:, :].bitcast(F32), ALU.subtract).then_inc(ve_esl, 1)

                def gates(n, b):
                    for tt in range(TT):
                        ve.wait_ge(ac_th, TT * n + tt + 1)
                        ins = ve.scalar_tensor_tensor(out=gate[:, b % 2, tt, :], in0=th[:, tt, :], scalar=1.0,
                                                      in1=ps_vg[:, tt, 256:512], op0=ALU.add, op1=ALU.mult)
                    ins.then_inc(ve_gate, 1)

                def inverse_sums(n):
                    ve.wait_ge(pe_c, n + 1)
                    after(ve, po_qe, n)
                    ve.reciprocal(enz[:, :], ps_c).then_inc(ve_enz, 1)

                def mean_square(u):
                    ve.wait_ge(ac_sq, u + 1)
                    after(ve, ve_ze, u)
                    ve.tensor_reduce(ss[:, :], sq[:, :, :], AX, ALU.add).then_inc(ve_ss, 1)
                    ve.wait_ge(ve_sum, u + 1)
                    ve.scalar_tensor_tensor(out=zs[:, :], in0=sume[:, :], scalar=EPS, in1=sume[:, :],
                                            op0=ALU.mult, op1=ALU.mult).then_inc(ve_zs, 1)
                    ve.wait_ge(ve_ss, u + 1)
                    ve.wait_ge(ve_zs, u + 1)
                    after(ve, po_rstd, u)
                    ve.scalar_tensor_tensor(out=ze[:, :], in0=ss[:, :], scalar=1.0 / DK, in1=zs[:, :],
                                            op0=ALU.mult, op1=ALU.add).then_inc(ve_ze, 1)

                def gated(u, b):
                    ve.wait_ge(po_rstd, u + 1)
                    ve.wait_ge(ve_gate, u + 1)
                    after(ve, pe_ogt, u)
                    for g in range(4):
                        ins = ve.scalar_tensor_tensor(
                            out=og[:, g, :], in0=ps_o[:, g * P:(g + 1) * P], scalar=rstd[:, g:g + 1],
                            in1=gate[:, b % 2, g // 2, (g % 2) * DK:(g % 2 + 1) * DK], op0=ALU.mult, op1=ALU.mult)
                    ins.then_inc(ve_og, 1)

                def low_outputs(u):
                    ve.wait_ge(ac_ogh, u + 1)
                    after(ve, pe_wo, u)
                    ve.tensor_tensor(ogl[:, :, :], ps_ogt.rearrange("p (a d) -> p a d", a=4), ogh[:, :, :].bitcast(F32), ALU.subtract).then_inc(ve_ogl, 1)

                def accumulate(u, b):
                    ve.wait_ge(pe_wo, u + 1)
                    after(ve, ve_acc, u)
                    a = acc[:, b * TT:(b + 1) * TT, :]
                    ve.tensor_tensor(a, ps[:, y_bank(u), :].rearrange("p (a d) -> p a d", a=TT), a, ALU.add).then_inc(ve_acc, 1)

                def low_part(c):
                    return ve.tensor_tensor(wl[:, :, c], raw_tiles[:, :, c], wh[:, :, c].bitcast(F32), ALU.subtract)

                def low_k(p):
                    ve.wait_ge(wk_hi, p + 1)
                    low_part(W_K).then_inc(w_k, 1)

                def low_ws2(p):
                    ve.wait_ge(ws_hi, p + 1)
                    ve.tensor_tensor(ws2[64:128, :], wraw[64:128, W_S:W_END], ws2[64:128, :].bitcast(F32), ALU.subtract).then_inc(w_s, 1)

                def low_inner(t, n, done):
                    ve.wait_ge(s1_cp, n)
                    for q in (32, 96):
                        ve.tensor_tensor(s1[q:q + 32, t], s1_raw[q:q + 32, t], s1[q:q + 32, t].bitcast(F32), ALU.subtract).then_inc(done, 1)

                def low_x(t):
                    ve.tensor_tensor(xl[:, :, t], xraw[:, :, t], xh[:, :, t].bitcast(F32), ALU.subtract).then_inc(x_ok, 1)

                ve.wait_ge(ld_xf, 16)
                ve.tensor_copy(xh[:, :, 0:T], xraw[:, :, 0:T]).then_inc(x0_hi, 1)
                ve.wait_ge(x0_hi, 1)
                low_x(slice(0, T))
                ve.wait_ge(wq_hi, 1)
                low_part(W_Q).then_inc(w_q, 1)
                low_k(0)
                ve.wait_ge(ws1_hi, 1)
                ve.tensor_tensor(ws1l, ws1_raw, ws1h.bitcast(F32), ALU.subtract).then_inc(ws1_ok, 1)
                low_ws2(0)
                ve.wait_ge(ld_mask, 16)
                ve.tensor_reduce(mval[:, :], mrow[:, :, :], AX, ALU.max).then_inc(mval_ok, 1)
                ve.wait_ge(ld_con, 16)
                ve.tensor_copy(tri_r[:, :], con[:, C_TRI:C_TRI + 2 * P])
                times_cos(0, ps_q, qcos, ac_swq, po_qr, ve_qcos)
                times_cos(0, ps_k, kcos, pe_k, po_kr, ve_kcos)
                ve.wait_ge(x_hi, 1)
                low_x(slice(T, B * T))
                low_inner(slice(0, T), 1, s1_ok)
                q_times_sin(0)
                ve.wait_ge(pe_valid, 1)
                ve.tensor_scalar(valid[:, :], ps[:, 7, 0:B], 1.0, None, ALU.min).then_inc(valid_ok, 1)
                clip(0)
                low_es(0, 0)
                gates(0, 0)
                inverse_sums(0)
                ve.wait_ge(ld_vec, 16)
                ve.tensor_scalar(halfrb[:, :], vec[:, V_RB:V_RB + 1], 0.5, None, ALU.mult)
                ve.tensor_scalar(gn[:, :], vec[:, V_GN:V_GN + 1], 0.5, None, ALU.mult).then_inc(gn_ok, 1)
                ve.wait_ge(ld_xt, 16)
                ve.wait_ge(gn_ok, 1)

                def moments(b, eps, bn, st, mean, var, s_bn, s_st, s_mean, s_var, n=None, tiles=slice(0, TT)):
                    n = b if n is None else n
                    for tt in range(tiles.start, tiles.stop):
                        ins = ve.bn_stats(bn[:, tt, :], acc[:, b * TT + tt, :])
                    ins.then_inc(s_bn, 1)
                    ve.wait_ge(s_bn, n + 1)
                    ve.tensor_tensor(st[:, 0, tiles], bn[:, tiles, 1], bn[:, tiles, 4], ALU.add)
                    ve.tensor_tensor(st[:, 1, tiles], bn[:, tiles, 1], bn[:, tiles, 4], ALU.subtract)
                    ve.tensor_tensor(st[:, 2, tiles], bn[:, tiles, 2], bn[:, tiles, 5], ALU.add).then_inc(s_st, 1)
                    ve.wait_ge(s_st, n + 1)
                    ve.tensor_scalar(mean[:, b, tiles], st[:, 0, tiles], 0.5, None, ALU.mult)
                    ve.scalar_tensor_tensor(out=st[:, 3, tiles], in0=st[:, 1, tiles], scalar=0.25, in1=st[:, 1, tiles], op0=ALU.mult, op1=ALU.mult)
                    ve.tensor_scalar(st[:, 4, tiles], st[:, 2, tiles], 1.0 / D, eps, ALU.mult, ALU.add).then_inc(s_mean, 1)
                    ve.wait_ge(s_mean, n + 1)
                    ve.tensor_tensor(var[:, b, tiles], st[:, 3, tiles], st[:, 4, tiles], ALU.add).then_inc(s_var, 1)

                def normalise(b, dst, mean, root, s_root, s_out, n=None, tiles=slice(0, TT)):
                    ve.wait_ge(s_root, (b if n is None else n) + 1)
                    for tt in range(tiles.start, tiles.stop):
                        ins = ve.tensor_scalar(dst(tt), acc[:, b * TT + tt, :], mean[:, b, tt:tt + 1], root[:, b, tt:tt + 1], ALU.subtract, ALU.mult)
                    ins.then_inc(s_out, 1)

                def in_place(b):
                    return lambda tt: acc[:, b * TT + tt, :]

                def moments_x1(b):
                    ve.wait_ge(ve_acc, UNITS - B + b + 1)
                    moments(b, EPS, bn1, st1, mean1, var1, t_bn1, t_st1, t_mean1, t_var1)

                def norm_x1(b):
                    normalise(b, in_place(b), mean1, root1, t_root1, t_x1)

                def x1_turned(b):
                    ve.wait_ge(t_x1T, b + 1)
                    after(ve, t_sc, TT * b)
                    ve.tensor_copy(x1T[:, :, :, :], ps[:, 0, :].rearrange("p (a k t) -> p a k t", a=TT, k=KT)).then_inc(t_x1Ts, 1)

                def max_memory(b, tt):
                    ve.wait_ge(t_sc, TT * b + tt + 1)
                    ve.tensor_reduce(smax[:, b, tt:tt + 1], ps[:, SCORE_BANK[tt], :], AX, ALU.max).then_inc(t_max, 1)
                    ve.wait_ge(t_max, TT * b + tt + 1)
                    ve.tensor_scalar(nmax[:, b, tt:tt + 1], smax[:, b, tt:tt + 1], -float(D) ** -0.5, None, ALU.mult).then_inc(t_nmax, 1)

                def memory_turned(b):
                    ve.wait_ge(t_pT, TT * b + 1)
                    after(ve, t_r, b)
                    ve.tensor_copy(probT[:, 0, :, :], ps[:, TURN_BANK[0], :].rearrange("p (m t) -> p m t", m=MT)).then_inc(t_pTs[0], 1)
                    ve.wait_ge(t_prob, TT * b + TT)
                    ve.reciprocal(pinv[:, b, :], psums[:, b, :]).then_inc(t_pinv, 1)
                    ve.wait_ge(t_pinv, b + 1)
                    ve.tensor_scalar(pval[:, b, :], pinv[:, b, :], valid[:, b:b + 1], None, ALU.mult).then_inc(t_pval, 1)

                def add_memory(b):
                    ve.wait_ge(t_r, b + 1)
                    ve.wait_ge(t_pval, b + 1)
                    for tt in range(TT):
                        ins = ve.scalar_tensor_tensor(out=acc[:, b * TT + tt, :], in0=ps[:, 5, tt * D:(tt + 1) * D], scalar=pval[:, b, tt:tt + 1],
                                                      in1=acc[:, b * TT + tt, :], op0=ALU.mult, op1=ALU.add)
                    ins.then_inc(t_x2p, 1)
                    ve.wait_ge(t_x2p, b + 1)
                    moments(b, EPS, bn2, st2, mean2, var2, t_bn2, t_st2, t_mean2, t_var2)

                def norm_x2(b):
                    normalise(b, in_place(b), mean2, root2, t_root2, t_x2)

                def router(b):
                    ve.wait_ge(t_x2, b + 1)
                    ve.tensor_tensor(rprod[:, :, :], acc[:, b * TT:(b + 1) * TT, :], vec[:, V_RW:V_RW + D].unsqueeze(1).broadcast_to([P, TT, D]), ALU.mult).then_inc(t_rprod, 1)
                    ve.wait_ge(t_rprod, b + 1)
                    ve.tensor_reduce(rz[:, b, :], rprod[:, :, :], AX, ALU.add).then_inc(t_rz, 1)

                def low_x2(b):
                    ve.wait_ge(t_x2h, b + 1)
                    ve.tensor_tensor(x2l, ps[:, 6, :].rearrange("p (k t) -> p k t", k=KT), x2h.bitcast(F32),
                                     ALU.subtract).then_inc(t_x2l, 1)

                def low_h(b, j):
                    ve.wait_ge(t_hh, FT // 2 * b + j + 1)
                    if j == 0:
                        after(ve, t_y, b)
                    ve.tensor_tensor(hTl[:, 2 * j:2 * j + 2, :], hT[:, 2 * j:2 * j + 2, :], hTh[:, 2 * j:2 * j + 2, :].bitcast(F32),
                                     ALU.subtract).then_inc(t_hl[j], 1)

                def router_weight(b):
                    ve.wait_ge(t_rt, b + 1)
                    ve.tensor_scalar(rw[:, b, :], rt[:, b, :], 0.25, 0.25, ALU.mult, ALU.add).then_inc(t_rw, 1)
                    ve.wait_ge(t_rw, b + 1)
                    ve.wait_ge(t_x2l, b + 1)
                    for tt in range(TT):
                        a = acc[:, b * TT + tt, :]
                        ins = ve.scalar_tensor_tensor(out=a, in0=vec[:, V_B2:V_B2 + D], scalar=rw[:, b, tt:tt + 1], in1=a, op0=ALU.mult, op1=ALU.add)
                    ins.then_inc(t_yb, 1)

                def add_ffn(n):
                    b, tiles = OUT_PARTS[n]
                    ve.wait_ge(t_y, n + 1)
                    ve.wait_ge(t_yb, b + 1)
                    for tt in range(tiles.start, tiles.stop):
                        bank, a = 5 if b == B - 1 and tt == 0 else 4, acc[:, b * TT + tt, :]
                        ins = ve.scalar_tensor_tensor(out=a, in0=ps[:, bank, tt * D:(tt + 1) * D], scalar=rw[:, b, tt:tt + 1], in1=a, op0=ALU.mult, op1=ALU.add)
                    ins.then_inc(t_x3, 1)

                def moments_x3(n):
                    b, tiles = OUT_PARTS[n]
                    ve.wait_ge(t_x3, n + 1)
                    moments(b, EPS / 4, bn3, st3, mean3, var3, t_bn3, t_st3, t_mean3, t_var3, n, tiles)

                def norm_out(n):
                    b, tiles = OUT_PARTS[n]
                    normalise(b, in_place(b), mean3, root3, t_root3, t_out, n, tiles)

                def step(u, p, b):
                    nb = (b + 1) % B
                    if not is_first(u):
                        mean_square(u - 1)
                    causal_scores(u)
                    if is_first(u):
                        low_inner(slice(2 * T, B * T), 2, s1_last)
                    else:
                        gated(u - 1, (b - 1) % B)
                    if not is_last(u):
                        times_cos(u + 1, ps_q, qcos, ac_swq, po_qr, ve_qcos)
                        times_cos(u + 1, ps_k, kcos, pe_k, po_kr, ve_kcos)
                    ve.wait_ge(pe_p, u + 1)
                    ve.wait_ge(ve_enz, u + 1)
                    after(ve, po_okm, u)
                    ve.tensor_tensor(ok[:, :], ps_p, enz[:, :], ALU.mult).then_inc(ve_ok, 1)
                    ve.wait_ge(ve_ok, u + 1)
                    ve.tensor_reduce(mx[:, :], groups(ok[:, :]), AX, ALU.max).then_inc(ve_mx, 1)
                    if not is_last(u):
                        clip(u + 1)
                    if not is_first(u):
                        low_outputs(u - 1)
                    if not is_last(u):
                        q_times_sin(u + 1)
                    if is_first(u):
                        ve.tensor_scalar(mneg[:, :, :], mrow[:, :, :].bitcast(U8), -NEG, NEG, ALU.mult, ALU.add)
                        ve.tensor_copy(one_r[:, :], ones[0:1, :]).then_inc(mask_ok, 1)
                    if not is_last(u):
                        low_es(u + 1, nb)
                    if b >= 2 and not has_next_pair(p):
                        moments_x1(b - 2)
                    ve.wait_ge(ac_exp, u + 1)
                    after(ve, ve_zs, u)
                    ve.tensor_reduce(sume[:, :], groups(ee[:, :]), AX, ALU.add).then_inc(ve_sum, 1)
                    if b == 2 and has_next_pair(p):
                        low_k(p + 1)
                    if is_last(u):
                        max_memory(0, 0)
                    else:
                        gates(u + 1, nb)
                    causal_weights(u)
                    if is_last(u):
                        max_memory(0, 1)
                    if b >= 2 and not has_next_pair(p):
                        norm_x1(b - 2)
                    if b == 2 and not has_next_pair(p):
                        accumulate(u - 1, b - 1)
                    if not is_last(u):
                        inverse_sums(u + 1)
                    if b == 2 and has_next_pair(p):
                        low_ws2(p + 1)
                    if not is_first(u) and not (b == 2 and not has_next_pair(p)):
                        accumulate(u - 1, (b - 1) % B)
                    if b == 2 and not has_next_pair(p):
                        x1_turned(0)

                over_main(ve, step)
                memory_turned(0)
                mean_square(UNITS - 1)
                x1_turned(1)
                gated(UNITS - 1, B - 1)
                add_memory(0)
                low_outputs(UNITS - 1)
                norm_x2(0)
                max_memory(1, 0)
                low_x2(0)
                max_memory(1, 1)
                moments_x1(2)
                norm_x1(2)
                accumulate(UNITS - 1, B - 1)
                router(0)
                for b in range(B - 1):
                    memory_turned(b + 1)
                    if b + 2 < B:
                        x1_turned(b + 2)
                    for j in range(FT // 2 - 1):
                        low_h(b, j)
                    add_memory(b + 1)
                    norm_x2(b + 1)
                    router_weight(b)
                    low_x2(b + 1)
                    add_ffn(b)
                    if b + 2 < B:
                        max_memory(b + 2, 0)
                        moments_x3(b)
                        max_memory(b + 2, 1)
                        norm_out(b)
                    if b == 0:
                        moments_x1(B - 1)
                    router(b + 1)
                    if b == 0:
                        norm_x1(B - 1)
                    if b + 2 == B:
                        moments_x3(b)
                low_h(B - 1, 0)
                low_h(B - 1, 1)
                norm_out(B - 2)
                low_h(B - 1, 2)
                router_weight(B - 1)
                low_h(B - 1, 3)
                for n in range(B - 1, len(OUT_PARTS)):
                    add_ffn(n)
                    moments_x3(n)
                    norm_out(n)

            @block.gpsimd
            def _(po):
                sin2 = sin.unsqueeze(1).broadcast_to([P, 2, T])

                def rotate(n):
                    po.wait_ge(ac_swk, n + 1)
                    after(po, po_kr, n)
                    po.tensor_tensor(ksin[:, :].rearrange("p (h t) -> p h t", h=2), swk[:, :].rearrange("p (h t) -> p h t", h=2), sin2, ALU.mult).then_inc(po_ksin, 1)
                    po.wait_ge(ve_qcos, n + 1)
                    po.wait_ge(ve_qsin, n + 1)
                    after(po, pe_a, n)
                    po.tensor_tensor(qr[:, :], qcos[:, :], qsin[:, :], ALU.add).then_inc(po_qr, 1)
                    po.wait_ge(ve_kcos, n + 1)
                    po.wait_ge(po_ksin, n + 1)
                    po.tensor_tensor(kr[:, :], kcos[:, :], ksin[:, :], ALU.add).then_inc(po_kr, 1)

                def inverse_root(u):
                    po.wait_ge(ve_ze, u + 1)
                    after(po, ve_og, u)
                    po.tensor_tensor(rstd[:, :], ze[:, :], con[:, C_HALF:C_HALF + 4], ALU.pow).then_inc(po_rstd, 1)

                def low_vg(p):
                    po.wait_ge(wv_hi, p + 1)
                    po.tensor_tensor(wl[:, :, W_VG], raw_tiles[:, :, W_VG],
                                     wh[:, :, W_VG].bitcast(F32), ALU.subtract).then_inc(w_vg, 1)

                def low_q(p):
                    po.wait_ge(wq_hi, p + 1)
                    after(po, pe_q, 4 * p)
                    po.tensor_tensor(wl[:, :, W_Q], raw_tiles[:, :, W_Q], wh[:, :, W_Q].bitcast(F32), ALU.subtract).then_inc(w_q, 1)

                def low_wo(p):
                    po.wait_ge(wo_hi, p + 1)
                    po.tensor_tensor(wol[:, :, :], wos[:, :, :], woh[:, :, :].bitcast(F32), ALU.subtract).then_inc(w_wo, 1)

                low_vg(0)
                po.wait_ge(ld_con, 16)
                rotate(0)

                def step(u, p, b):
                    if is_first(u):
                        po.wait_ge(s1_cp, 2)
                        for i, q in enumerate((32, 96)):
                            t = slice(T, 2 * T)
                            po.tensor_tensor(s1[q:q + 32, t], s1_raw[q:q + 32, t], s1[q:q + 32, t].bitcast(F32), ALU.subtract).then_inc(s1_ok, 1)
                            po.wait_ge(s1_ok, 3 + i)
                    else:
                        inverse_root(u - 1)
                    if b == 1:
                        low_wo(p)
                    if b == 2 and has_next_pair(p):
                        low_q(p + 1)
                    po.wait_ge(ve_mx, u + 1)
                    after(po, ac_exp, u)
                    po.tensor_tensor(okm[:, :].rearrange("p (g m) -> p g m", g=4), ok[:, :].rearrange("p (g m) -> p g m", g=4),
                                     mx[:, :].unsqueeze(2).broadcast_to([P, 4, M]), ALU.subtract).then_inc(po_okm, 1)
                    po.wait_ge(ac_exp, u + 1)
                    after(po, pe_qet, u)
                    po.tensor_tensor(qe[:, :, :], ee[:, :].rearrange("p (a m) -> p a m", a=TT),
                                     enz[:, :].rearrange("p (a m) -> p a m", a=TT), ALU.mult).then_inc(po_qe, 1)
                    if not is_last(u):
                        rotate(u + 1)
                    if b >= 2 and not has_next_pair(p):
                        root(b - 2, var1, root1, t_var1, t_root1)
                    if b == 2 and has_next_pair(p):
                        low_vg(p + 1)
                    if b >= 2 and not has_next_pair(p):
                        low_w1(b - 2)

                def low_w1(half):
                    c = slice(half * 512, (half + 1) * 512)
                    po.wait_ge(w1_hi, half + 1)
                    po.tensor_tensor(w1l[:, :, c], w1raw[:, :, c], w1h[:, :, c].bitcast(F32), ALU.subtract).then_inc(w1_ok, 1)

                def root(b, var, out_root, ready, done, n=None, tiles=slice(0, TT)):
                    po.wait_ge(ready, (b if n is None else n) + 1)
                    po.tensor_tensor(out_root[:, b, tiles], var[:, b, tiles], con[:, C_HALF:C_HALF + TT][:, tiles], ALU.pow).then_inc(done, 1)

                def low_w2(half):
                    f = slice(half * FT // 2, (half + 1) * FT // 2)
                    po.wait_ge(w2_hi, half + 1)
                    po.tensor_tensor(w2l[:, f, :], w2s[:, f, :], w2h[:, f, :].bitcast(F32), ALU.subtract).then_inc(w2_ok, 1)

                def low_h(b, j):
                    po.wait_ge(t_hh, FT // 2 * b + j + 1)
                    after(po, t_y, b)
                    po.tensor_tensor(hTl[:, 2 * j:2 * j + 2, :], hT[:, 2 * j:2 * j + 2, :], hTh[:, 2 * j:2 * j + 2, :].bitcast(F32),
                                     ALU.subtract).then_inc(t_hl[j], 1)

                over_main(po, step)
                inverse_root(UNITS - 1)
                low_w2(0)
                root(0, var2, root2, t_var2, t_root2)
                low_w2(1)
                root(2, var1, root1, t_var1, t_root1)
                for b in range(B - 1):
                    low_h(b, FT // 2 - 1)
                    root(b + 1, var2, root2, t_var2, t_root2)
                    root(b, var3, root3, t_var3, t_root3)
                    if b == 0:
                        root(3, var1, root1, t_var1, t_root1)
                for n in range(B - 1, len(OUT_PARTS)):
                    b, tiles = OUT_PARTS[n]
                    root(b, var3, root3, t_var3, t_root3, n, tiles)


def _constants():
    inv_freq = (np.float32(1.0) / np.float32(10000.0) ** (np.arange(0, DK, 2, dtype=np.float32) / np.float32(DK))).astype(np.float32)
    ang = (inv_freq[:, None] * np.arange(T, dtype=np.float32)[None, :]).astype(np.float32).astype(np.float64)
    con = np.zeros((P, C_END), np.float32)
    con[:, C_COS:C_COS + T] = np.concatenate([np.cos(ang), np.cos(ang)], 0)
    con[:, C_SIN:C_SIN + T] = np.concatenate([-np.sin(ang), np.sin(ang)], 0)
    tri, ones = np.triu(np.ones((P, P))), np.ones((P, P))
    con[:, C_TRI:C_TRI + 3 * P] = np.concatenate([tri, ones, tri], 1)
    con[:, C_ID:C_ID + P] = np.eye(P)
    con[R::32, C_ONECOL] = 1.0
    con[:, C_HALF:C_HALF + 8] = -0.5
    return con


def kernel(x, ctx_2048, mask_BxS2_bk0, L0_attn_Wq, L0_attn_Wk, L0_attn_Wv, L0_attn_Wg, L0_attn_Wo, L0_attn_Ws1,
           L0_attn_Ws2, L0_attn_bs2, L0_attn_g_norm_weight, L0_ffn_router_weight, L0_ffn_router_bias, L0_ffn_w1,
           L0_ffn_b1, L0_ffn_w2, L0_ffn_b2):
    import concourse.bacc as bacc
    from concourse.bass_utils import run_bass_kernel_spmd

    f32 = np.float32
    x, c = np.asarray(x), np.asarray(ctx_2048)

    def by_partition(a, tiles):
        return a.reshape(tiles, P, -1).transpose(1, 0, 2)

    w = [np.asarray(a).reshape(PAIRS, 2 * DK, KT, P).transpose(0, 3, 2, 1) for a in (L0_attn_Wq, L0_attn_Wk, L0_attn_Wv, L0_attn_Wg)]
    w = np.concatenate(w, 3).reshape(PAIRS, P, KT * 1024)
    stack = np.zeros((PAIRS, 4, 32, 2 * M), f32)
    stack[:, :, 0:R] = np.asarray(L0_attn_Ws2).reshape(PAIRS, 1, 2 * M, R).transpose(0, 1, 3, 2)
    stack[:, :, R] = np.asarray(L0_attn_bs2).reshape(PAIRS, 1, 2 * M)
    w_pairs = np.concatenate([w, stack.reshape(PAIRS, P, 2 * M)], 2)
    wo_pairs = np.asarray(L0_attn_Wo).T.reshape(PAIRS, 2, DK, D).transpose(0, 2, 1, 3)
    ws1 = np.zeros((P, KT, 4, 32), f32)
    ws1[:, :, :, 0:R] = np.asarray(L0_attn_Ws1).T.reshape(KT, P, 1, R).transpose(1, 0, 2, 3)
    vectors = np.zeros((P, V_END), f32)
    vectors[:, V_GN] = np.asarray(L0_attn_g_norm_weight)
    vectors[:, V_B1:V_B1 + FT] = np.asarray(L0_ffn_b1).reshape(FT, P).T
    vectors[:, V_RW:V_RW + D] = np.asarray(L0_ffn_router_weight)[None, :]
    vectors[:, V_RB] = np.asarray(L0_ffn_router_bias)[0]
    vectors[:, V_B2:V_B2 + D] = np.asarray(L0_ffn_b2)[None, :]
    arrays = {
        "x_tok": by_partition(x.reshape(B * T, D), B * TT),
        "x_feat": by_partition(x.reshape(B * T, D).T, KT),
        "w_pairs": w_pairs,
        "wo_pairs": wo_pairs,
        "ws1": ws1.reshape(P, KT, P),
        "consts": _constants(),
        "vectors": vectors,
        "ctx_feat": c.transpose(2, 0, 1).reshape(KT, P, B, S2).transpose(1, 2, 0, 3),
        "ctx_tok": c.reshape(B, MT, P, D).transpose(2, 0, 1, 3),
        "mask": np.ascontiguousarray(mask_BxS2_bk0).view(np.int32).reshape(1, B, S2 // 4),
        "w1": by_partition(np.asarray(L0_ffn_w1), KT),
        "w2": by_partition(np.asarray(L0_ffn_w2), FT),
    }
    arrays = {n: np.ascontiguousarray(a) for n, a in arrays.items()}
    nc = bacc.Bacc("TRN2", target_bir_lowering=False, num_devices=1)
    aps = [nc.dram_tensor(n, a.shape, mybir.dt.from_np(a.dtype), kind="ExternalInput").ap() for n, a in arrays.items()]
    out = nc.dram_tensor("out", (P, B, TT, D), F32, kind="ExternalOutput").ap()
    decoder_layer(nc, *aps, out)
    r = run_bass_kernel_spmd(nc, [arrays], core_ids=[0])
    return r.results[0]["out"].reshape(P, B * TT, D).transpose(1, 0, 2).reshape(B, T, D)
```
